# Optimizing a Trainium2 kernel written in Bass

```python
import numpy as np
import jax
import jax.numpy as jnp

def _softmax(x, axis=-1):
    return jax.nn.softmax(x, axis=axis)

def _gelu(x):
    return jax.nn.gelu(x, approximate=True)

def _silu(x):
    return jax.nn.silu(x)

def _sigmoid(x):
    return jax.nn.sigmoid(x)

def _layernorm(x, axis=-1, eps=1e-05):
    m = jnp.mean(x, axis=axis, keepdims=True)
    v = jnp.var(x, axis=axis, keepdims=True)
    return (x - m) / jnp.sqrt(v + eps)

def _scatter_add(tgt, idx, src, axis=0):
    return tgt.at[idx].add(src)

def _segment_sum(src, seg, n):
    return jax.ops.segment_sum(src, seg, n)
kernel_name = 'mk_gnn_resnorm_d4_gnn_r8_bee034'

def setup_inputs(seed: int=0):
    np.random.seed(seed)
    _w = jnp.asarray

    def _rec_inputs():
        import jax
        import jax.numpy as jnp
        _gk = jax.random.key(seed)
        x = -0.0003713 + 1 * jax.random.normal(jax.random.fold_in(_gk, 1), (6250, 256), jnp.float32)
        _s = jax.random.randint(jax.random.fold_in(_gk, 2), (50000,), 0, 6250, jnp.int32)
        _d = jax.random.randint(jax.random.fold_in(_gk, 3), (50000,), 0, 6250, jnp.int32)
        _loop = jnp.arange(6250, dtype=jnp.int32)
        src = jnp.concatenate([_s, _d, _loop])
        dst = jnp.concatenate([_d, _s, _loop])
        _o = jnp.argsort(dst, stable=True)
        src = src[_o]
        dst = dst[_o]
        edge_attr_64 = -9.77346e-05 + 0.999888 * jax.random.normal(jax.random.fold_in(_gk, 12), (106250, 64), jnp.float32)
        return (x, src, dst, edge_attr_64)
    x, src, dst, edge_attr_64 = _rec_inputs()

    def _L0_gnn_setup():
        import jax, jax.numpy as jnp
        import numpy as np
        ALPHA = 0.2
        key = jax.random.key(seed)
        ks = jax.random.split(key, 6)
        N, E, F_IN, F_OUT, E_DIM = (6250, 100000, 256, 256, 64)
        h = jax.random.normal(ks[0], (N, F_IN), dtype=jnp.float32)
        e_feat = jax.random.normal(ks[1], (E, E_DIM), dtype=jnp.float32)
        W = jax.random.normal(ks[2], (F_OUT, F_IN), dtype=jnp.float32) * (1.0 / np.sqrt(F_IN))
        A = jax.random.normal(ks[3], (1, 2 * F_OUT + E_DIM), dtype=jnp.float32) * 0.05
        src = jax.random.randint(ks[4], (E,), 0, N, dtype=jnp.int32)
        dst = jax.random.randint(ks[5], (E,), 0, N, dtype=jnp.int32)
        return {'h': h, 'e_feat': e_feat, 'W': W, 'A': A, 'src': src, 'dst': dst}
    _L0_gnn_all = _L0_gnn_setup()
    _L0_gnn_in = {k: v for k, v in _L0_gnn_all.items() if k in ('W', 'A')}
    del _L0_gnn_all

    def _L1_gnn_setup():
        import jax, jax.numpy as jnp
        import numpy as np
        N_NODES = 6250
        N_EDGES = 100000
        IN_CH = 256
        HID_CH = 256
        OUT_CH = 256
        N_LAYERS = 3
        key = jax.random.key(seed)
        ks = jax.random.split(key, 8)
        s_in = 1.0 / np.sqrt(IN_CH)
        s_h = 1.0 / np.sqrt(HID_CH)
        return {'x': jax.random.normal(ks[0], (N_NODES, IN_CH), dtype=jnp.float32), 'W_in': jax.random.normal(ks[1], (IN_CH, HID_CH), dtype=jnp.float32) * s_in, 'b_in': jnp.zeros((HID_CH,), dtype=jnp.float32), 'W_agg': jax.random.normal(ks[2], (N_LAYERS, HID_CH, HID_CH), dtype=jnp.float32) * s_h, 'W_self': jax.random.normal(ks[3], (N_LAYERS, HID_CH, HID_CH), dtype=jnp.float32) * s_h, 'b_hid': jnp.zeros((N_LAYERS, HID_CH), dtype=jnp.float32), 'W_out': jax.random.normal(ks[4], (HID_CH, OUT_CH), dtype=jnp.float32) * s_h, 'b_out': jnp.zeros((OUT_CH,), dtype=jnp.float32), 'edge_index': jax.random.randint(ks[5], (2, N_EDGES), 0, N_NODES, dtype=jnp.int64)}
    _L1_gnn_all = _L1_gnn_setup()
    _L1_gnn_in = {k: v for k, v in _L1_gnn_all.items() if k in ('W_in', 'b_in', 'W_agg', 'W_self', 'b_hid', 'W_out', 'b_out')}
    del _L1_gnn_all

    def _L2_gnn_setup():
        import jax, jax.numpy as jnp
        import numpy as np

        def _inv_sqrt(deg):
            return jnp.where(deg > 0, jax.lax.rsqrt(deg), 0.0)
        key = jax.random.key(seed)
        k1, k2, k3, k4 = jax.random.split(key, 4)
        n_nodes, n_edges, d_in, d_half = (12500, 200000, 256, 128)
        x = jax.random.normal(k1, (n_nodes, d_in), dtype=jnp.float32)
        edge_index = jax.random.randint(k2, (2, n_edges), 0, n_nodes, dtype=jnp.int64)
        W_f = jax.random.normal(k3, (d_half, d_in), dtype=jnp.float32) * (1.0 / np.sqrt(d_in))
        W_b = jax.random.normal(k4, (d_half, d_in), dtype=jnp.float32) * (1.0 / np.sqrt(d_in))
        bias_param = jnp.zeros((2 * d_half,), dtype=jnp.float32)
        return {'x': x, 'edge_index': edge_index, 'W_f': W_f, 'W_b': W_b, 'bias_param': bias_param}
    _L2_gnn_all = _L2_gnn_setup()
    _L2_gnn_in = {k: v for k, v in _L2_gnn_all.items() if k in ('W_f', 'W_b', 'bias_param')}
    del _L2_gnn_all

    def _L3_gnn_setup():
        import jax, jax.numpy as jnp
        import numpy as np
        N_NODES = 6250
        key = jax.random.key(seed)
        k1, k2, k3 = jax.random.split(key, 3)
        x = jax.random.normal(k1, (N_NODES, 256), dtype=jnp.float32)
        W = jax.random.normal(k2, (256, 256), dtype=jnp.float32) * (1.0 / np.sqrt(256))
        edge_index = jax.random.randint(k3, (2, 200000), 0, N_NODES, dtype=jnp.int64)
        return {'x': x, 'W': W, 'edge_index': edge_index}
    _L3_gnn_all = _L3_gnn_setup()
    _L3_gnn_in = {k: v for k, v in _L3_gnn_all.items() if k in ('W',)}
    del _L3_gnn_all
    return {'x': x, 'src': src, 'dst': dst, 'edge_attr_64': edge_attr_64, 'L0_gnn_W': _L0_gnn_in['W'], 'L0_gnn_A': _L0_gnn_in['A'], 'L1_gnn_W_in': _L1_gnn_in['W_in'], 'L1_gnn_b_in': _L1_gnn_in['b_in'], 'L1_gnn_W_agg': _L1_gnn_in['W_agg'], 'L1_gnn_W_self': _L1_gnn_in['W_self'], 'L1_gnn_b_hid': _L1_gnn_in['b_hid'], 'L1_gnn_W_out': _L1_gnn_in['W_out'], 'L1_gnn_b_out': _L1_gnn_in['b_out'], 'L2_gnn_W_f': _L2_gnn_in['W_f'], 'L2_gnn_W_b': _L2_gnn_in['W_b'], 'L2_gnn_bias_param': _L2_gnn_in['bias_param'], 'L3_gnn_W': _L3_gnn_in['W']}

def reference(x, src, dst, edge_attr_64, L0_gnn_W, L0_gnn_A, L1_gnn_W_in, L1_gnn_b_in, L1_gnn_W_agg, L1_gnn_W_self, L1_gnn_b_hid, L1_gnn_W_out, L1_gnn_b_out, L2_gnn_W_f, L2_gnn_W_b, L2_gnn_bias_param, L3_gnn_W):
    import jax
    import jax.numpy as jnp

    def _L0_gnn_ref(h, e_feat, W, A, src, dst):
        import jax, jax.numpy as jnp
        import numpy as np
        ALPHA = 0.2
        N = h.shape[0]
        F_OUT = W.shape[0]
        z = h @ W.T
        z_src = z[src]
        z_dst = z[dst]
        a_src, a_dst, a_e = (A[0, :F_OUT], A[0, F_OUT:2 * F_OUT], A[0, 2 * F_OUT:])
        logits = z_src @ a_src + z_dst @ a_dst + e_feat @ a_e
        e = jax.nn.leaky_relu(logits, ALPHA)
        m = jax.ops.segment_max(e, dst, num_segments=N)
        ex = jnp.exp(e - m[dst])
        denom = jax.ops.segment_sum(ex, dst, num_segments=N)
        alpha = ex / denom[dst]
        h_out = jax.ops.segment_sum(alpha[:, None] * z_src, dst, num_segments=N)
        return h_out

    def _L1_gnn_ref(x, W_in, b_in, W_agg, W_self, b_hid, W_out, b_out, edge_index):
        import jax, jax.numpy as jnp
        import numpy as np
        N_NODES = 6250
        N_EDGES = 100000
        IN_CH = 256
        HID_CH = 256
        OUT_CH = 256
        N_LAYERS = 3
        n = x.shape[0]
        dst = edge_index[0]
        src = edge_index[1]
        n_layers = W_agg.shape[0]
        h = x @ W_in + b_in
        deg = jax.ops.segment_sum(jnp.ones_like(dst, dtype=h.dtype), dst, num_segments=n)
        deg = jnp.maximum(deg, 1.0)[:, None]
        for l in range(n_layers):
            agg = jax.ops.segment_sum(h[src], dst, num_segments=n) / deg
            h = jax.nn.relu(agg @ W_agg[l] + h @ W_self[l] + b_hid[l])
        return h @ W_out + b_out

    def _L2_gnn_ref(x, edge_index, W_f, W_b, bias_param):
        import jax, jax.numpy as jnp
        import numpy as np

        def _inv_sqrt(deg):
            return jnp.where(deg > 0, jax.lax.rsqrt(deg), 0.0)
        n_nodes = x.shape[0]
        loops = jnp.arange(n_nodes, dtype=edge_index.dtype)
        ei = jnp.concatenate([edge_index, jnp.stack([loops, loops])], axis=1)
        n_e = ei.shape[1]
        w = jnp.ones((n_e,), dtype=x.dtype)
        col, row = (ei[0], ei[1])
        in_deg = jax.ops.segment_sum(w, col, num_segments=n_nodes)
        out_deg = jax.ops.segment_sum(w, row, num_segments=n_nodes)
        ew = _inv_sqrt(out_deg)[row] * w * _inv_sqrt(in_deg)[col]
        mf = (x @ W_f.T)[row] * ew[:, None]
        y_forward = jax.ops.segment_sum(mf, col, num_segments=n_nodes)
        mb = (x @ W_b.T)[col] * ew[:, None]
        y_backward = jax.ops.segment_sum(mb, row, num_segments=n_nodes)
        y = jnp.concatenate([y_forward, y_backward], axis=-1) + bias_param
        return y

    def _L3_gnn_ref(x, W, edge_index):
        import jax, jax.numpy as jnp
        import numpy as np
        N_NODES = 6250
        N = x.shape[0]
        src, dst = (edge_index[0], edge_index[1])
        h = x @ W
        deg = jax.ops.segment_sum(jnp.ones_like(dst, dtype=h.dtype), dst, num_segments=N)
        deg_inv_sqrt = jnp.where(deg > 0, jax.lax.rsqrt(jnp.maximum(deg, 1)), 0.0)
        norm = deg_inv_sqrt[src] * deg_inv_sqrt[dst]
        msgs = h[src] * norm[:, None]
        out = jax.ops.segment_sum(msgs, dst, num_segments=N)
        return out
    edge_index = jnp.stack([src, dst])
    x = _layernorm(x + _L0_gnn_ref(x, edge_attr_64, L0_gnn_W, L0_gnn_A, src, dst), axis=-1)
    x = _layernorm(x + _L1_gnn_ref(x, L1_gnn_W_in, L1_gnn_b_in, L1_gnn_W_agg, L1_gnn_W_self, L1_gnn_b_hid, L1_gnn_W_out, L1_gnn_b_out, edge_index), axis=-1)
    x = _layernorm(x + _L2_gnn_ref(x, edge_index, L2_gnn_W_f, L2_gnn_W_b, L2_gnn_bias_param), axis=-1)
    x = _layernorm(x + _L3_gnn_ref(x, L3_gnn_W, edge_index), axis=-1)
    return x

_drawn_inputs = setup_inputs


def setup_inputs(seed=0):
    import zlib

    import numpy as np

    out = dict(_drawn_inputs(seed))
    spreads = {'L1_gnn_b_in': (0.0, 0.1),
     'L1_gnn_b_hid': (0.0, 0.1),
     'L1_gnn_b_out': (0.0, 0.1),
     'L2_gnn_bias_param': (0.0, 0.1)}
    factors = {}
    for name, (base, spread) in spreads.items():
        noise = np.random.default_rng([zlib.crc32(name.encode()), seed]).standard_normal(out[name].shape)
        drawn = base * np.exp(spread * noise) if base else spread * noise
        out[name] = jnp.asarray(drawn.astype(out[name].dtype))
    for name, factor in factors.items():
        out[name] = (out[name] * factor).astype(out[name].dtype)
    return out
```

```python
import concourse.bass as bass
from concourse import mybir
from contextlib import ExitStack

FP32 = mybir.dt.float32
I32 = mybir.dt.int32
BF16 = mybir.dt.bfloat16
ALU = mybir.AluOpType
ACT = mybir.ActivationFunctionType
AX = mybir.AxisListType

P = 128
N_NODES = 6250
N_EDGES = 106250
F = 256
E_DIM = 64
NT = -(-N_NODES // P)
NPAD = NT * P
LAST = N_NODES - (NT - 1) * P
J = 8
GE = P * J
NG = -(-N_EDGES // GE)
S = NG * J
EPAD = NG * GE
TAIL = N_EDGES - (NG - 1) * GE
PAD_NODE = NPAD - 1
BIG = 2.0 ** 126
H = F // 2
W0 = F + 4
C_ONE, C_SRC = F, F + 1
EPS = 1e-5
ALPHA = 0.2


def copy(eng, out, in_):
    return eng.tensor_scalar(out, in_, 1.0, None, ALU.mult)


def row_on_all(row):
    return row.rearrange("(a n) -> a n", a=1).to_broadcast([P, row.shape[0]])


def is_int(t, least):
    return isinstance(t, int) and t >= least


class Chain:

    def __init__(self, eng, sem, base=0):
        self.eng, self.sem, self.base, self.n = eng, sem, base, 0

    def __call__(self, ins):
        self.n += 1
        ins.then_inc(self.sem, 1)
        self.eng.wait_ge(self.sem, self.base + self.n)


class Kernel:
    def __init__(self, nc, ctx, ins, out):
        self.nc, self.ctx, self.ins, self.out = nc, ctx, ins, out
        self.scopes = {}
        sb, dram = self.sb, self.dram
        self.rec_by_dst = dram("rec_by_dst", [EPAD, 2], I32)
        self.rec_by_src = dram("rec_by_src", [EPAD, 2], I32)
        self.key_row = dram("key_row", [EPAD], I32)
        self.tab_z = dram("tab_z", [NPAD, W0], FP32)
        self.tab_h = [dram(f"tab_h{k}", [NPAD, 3 * F], BF16) for k in range(3)]
        self.tab_fb = [dram(f"tab_{k}", [NPAD, 3 * H], BF16) for k in ("f", "b")]
        self.tab_g = dram("tab_g", [NPAD, 3 * F], BF16)
        self.bounds = sb("bounds", [1, 2, 2, NG], I32)
        self.ident = sb("ident", [P, P], FP32)
        self.ones = sb("ones", [P, P], FP32)
        self.before = sb("before", [P, P], FP32)
        self.col = sb("col", [P, P], FP32)
        self.node_id = sb("node_id", [P, NT], FP32)
        self.tile_no = sb("tile_no", [P, NT], FP32)
        self.neg_base = sb("neg_base", [P, NT], FP32)

    def sb(self, name, shape, dt):
        return self.ctx.enter_context(self.nc.sbuf_tensor(name, shape, dt))

    def ps(self, name, shape, dt):
        return self.ctx.enter_context(self.nc.psum_tensor(name, shape, dt))

    def sem(self, scope, name):
        if scope not in self.scopes:
            self.scopes[scope] = handles = []
            scope.callback(self.nc.all_engine_barrier)
            scope.callback(self.nc.clear_and_free_semaphores, handles)
        self.scopes[scope].append(self.nc.alloc_semaphore(name))
        return self.scopes[scope][-1]

    def dram(self, name, shape, dt):
        return self.nc.dram_tensor(name, shape, dt, kind="Internal").ap()

    def constants(self):
        nc = self.nc
        with ExitStack() as c:
            filled = self.sem(c, "filled")
            made = self.sem(c, "made")
            ids_made = self.sem(c, "ids_made")
            cast = self.sem(c, "cast")
            iot = c.enter_context(nc.sbuf_tensor("iot", [P, P], I32))
            iob = c.enter_context(nc.sbuf_tensor("iob", [P, NT], I32))
            ion = c.enter_context(nc.sbuf_tensor("ion", [P, NT], I32))
            block = c.enter_context(nc.Block())

            @block.gpsimd
            def _(pool):
                pool.memset(self.ident[:, :], 0.0).then_inc(filled, 1)
                pool.memset(self.ones[:, :], 1.0).then_inc(filled, 1)
                pool.memset(self.before[:, :], 1.0).then_inc(filled, 1)
                pool.iota(iot[:, :], pattern=[[1, P]], base=0, channel_multiplier=0).then_inc(ids_made, 1)
                pool.iota(iob[:, :], pattern=[[-P, NT]], base=0, channel_multiplier=0).then_inc(ids_made, 1)
                pool.iota(ion[:, :], pattern=[[P, NT]], base=0, channel_multiplier=1).then_inc(ids_made, 1)
                pool.wait_ge(filled, 3)
                pool.affine_select(out=self.ident[:, :], in_=self.ident[:, :], compare_op=ALU.not_equal, fill=1.0,
                                   base=0, pattern=[[-1, P]], channel_multiplier=1).then_inc(made, 1)
                pool.affine_select(out=self.before[:, :], in_=self.before[:, :], compare_op=ALU.is_gt, fill=0.0,
                                   base=0, pattern=[[1, P]], channel_multiplier=-1).then_inc(made, 1)
                pool.wait_ge(made, 2)

            @block.vector
            def _(dve):
                dve.wait_ge(ids_made, 3)
                dve.tensor_copy(self.col[:, :], iot[:, :]).then_inc(cast, 1)
                dve.tensor_copy(self.neg_base[:, :], iob[:, :]).then_inc(cast, 1)
                dve.tensor_copy(self.node_id[:, :], ion[:, :]).then_inc(cast, 1)
                dve.tensor_copy(self.tile_no[:, :], iot[:, 0:NT]).then_inc(cast, 1)
                dve.wait_ge(cast, 4)

    def edges(self):
        nc = self.nc
        src, dst = self.ins["src"], self.ins["dst"]
        attr = self.ins["edge_attr_64"]
        attr_full = attr[0:(NG - 1) * GE, :].rearrange("(g p j) d -> g p (j d)", p=P, j=J)
        first = (NG - 1) * GE
        whole, rest = TAIL // J, TAIL % J
        rec, place, logit_e = self.rec, self.place, self.logit_e
        with ExitStack() as c:
            def sb(name, shape, dt):
                return c.enter_context(nc.sbuf_tensor(name, shape, dt))

            def sem(name):
                return self.sem(c, name)

            ids = sb("ids", [P, 2, NG, J], I32)
            tile_i = sb("tile_i", [P, S], I32)
            tile_f = sb("tile_f", [P, S], FP32)
            is_b = sb("is_b", [P, S], FP32)
            run = sb("run", [P, S], FP32)
            here = sb("here", [P, S], FP32)
            place_f = sb("place_f", [P, S], FP32)
            ones_s = sb("ones_s", [P, S], FP32)
            counts = sb("counts", [P, NT], FP32)
            total = sb("total", [P, NT], FP32)
            upto = sb("upto", [P, NT], FP32)
            start = sb("start", [P, NT], FP32)
            a_e = sb("a_e", [P, E_DIM], FP32)
            at = sb("at", [P, 2, J, E_DIM], FP32)
            prod = sb("prod", [P, J, E_DIM], FP32)
            pc = c.enter_context(nc.psum_tensor("pc", [P, 2, 256], FP32))
            padded, packed, stored = sem("padded"), sem("packed"), sem("stored")
            loaded, consts, summed = sem("loaded"), sem("consts"), sem("summed")
            attr_in = [sem(f"attr_in{q}") for q in range(2)]
            attr_free, steps, tile_steps, attr_steps = sem("attr_free"), sem("steps"), sem("tile_steps"), sem("attr_steps")
            block = c.enter_context(nc.Block())
            n_loads = 2 * (3 if rest else 2)

            @block.sync
            def _(sp):
                sp.wait_ge(padded, 1)
                for w, a in enumerate((src, dst)):
                    sp.dma_start(ids[:, w, 0:NG - 1, :],
                                 a[0:first].rearrange("(g p j) -> p g j", p=P, j=J)).then_inc(loaded, 16)
                    sp.dma_start(ids[0:whole, w, NG - 1, :],
                                 a[first:first + whole * J].rearrange("(p j) -> p j", j=J)).then_inc(loaded, 16)
                    if rest:
                        sp.dma_start(ids[whole:whole + 1, w, NG - 1, 0:rest],
                                     a[first + whole * J:N_EDGES].rearrange("(p j) -> p j", p=1)).then_inc(loaded, 16)
                sp.dma_start(a_e[:, :], row_on_all(self.ins["L0_gnn_A"][0, 2 * F:2 * F + E_DIM])).then_inc(consts, 16)
                sp.wait_ge(packed, 2)
                sp.dma_start(self.rec_by_dst.rearrange("(g p j) c -> p g (j c)", p=P, j=J),
                             rec[:, :, :, :].rearrange("p g j c -> p g (j c)")).then_inc(stored, 16)
                sp.wait_ge(loaded, 16 * n_loads)
                sp.dma_start(self.key_row.rearrange("(g p j) -> p g j", p=P, j=J), ids[:, 1, :, :]).then_inc(stored, 16)
                with sp.Fori(0, (NG - 2) // 2) as i:
                    for q in range(2):
                        sp.wait_ge(attr_free, i * 2 + (q + 1))
                        sp.dma_start(at[:, q, :, :].rearrange("p j d -> p (j d)"),
                                     attr_full[bass.ds(i * 2 + q, 1), :, :].rearrange("g p x -> (g p) x")
                                     ).then_inc(attr_in[q], 16)
                sp.wait_ge(attr_free, NG - 1)
                sp.dma_start(at[:, 0, :, :].rearrange("p j d -> p (j d)"), attr_full[NG - 2, :, :]).then_inc(attr_in[0], 16)
                sp.wait_ge(attr_free, NG)
                sp.wait_ge(padded, 2)
                sp.dma_start(at[0:whole, 1, :, :],
                             attr[first:first + whole * J, :].rearrange("(p j) d -> p j d", j=J)).then_inc(attr_in[1], 16)
                if rest:
                    sp.dma_start(at[whole:whole + 1, 1, 0:rest, :],
                                 attr[first + whole * J:N_EDGES, :].rearrange("(p j) d -> p j d", p=1)
                                 ).then_inc(attr_in[1], 16)
                sp.wait_ge(stored, 32)

            @block.vector
            def _(dve):
                dve.memset(ids[:, :, NG - 1, :], PAD_NODE).then_inc(padded, 1)
                dve.sem_inc(attr_free, 2)
                dve.wait_ge(loaded, 16 * n_loads)
                for w in range(2):
                    dve.tensor_copy(rec[:, :, :, w], ids[:, w, :, :]).then_inc(packed, 1)
                step = Chain(dve, steps)
                step(dve.tensor_scalar(tile_i[:, :], ids[:, 0, :, :].rearrange("p g j -> p (g j)"),
                                       P.bit_length() - 1, None, ALU.logical_shift_right))
                step(dve.tensor_copy(tile_f[:, :], tile_i[:, :]))
                step(dve.memset(ones_s[:, :], 1.0))
                step(dve.memset(place_f[:, :], 0.0))
                with dve.Fori(0, NT) as b:
                    dve.tensor_scalar(is_b[:, :], tile_f[:, :], self.tile_no[:, bass.ds(b, 1)], 0.0,
                                      ALU.is_equal, ALU.add, accum_out=counts[:, bass.ds(b, 1)]).then_inc(tile_steps, 1)
                    dve.wait_ge(tile_steps, b + 1)
                dve.wait_ge(summed, 1)
                step(dve.tensor_copy(total[:, :], pc[:, 1, 0:NT]))
                step(dve.tensor_tensor_scan(upto[:, :], ones_s[:, 0:NT], total[:, :], 0.0, ALU.mult, ALU.add))
                step(dve.tensor_tensor(start[:, :], upto[:, :], total[:, :], ALU.subtract))
                step(dve.tensor_tensor(start[:, :], start[:, :], pc[:, 0, 0:NT], ALU.add))
                step(dve.tensor_scalar(start[:, :], start[:, :], 1.0, None, ALU.subtract))
                with dve.Fori(0, NT) as b:
                    tstep = Chain(dve, tile_steps, b * 4 + NT)
                    tile_no = self.tile_no[:, bass.ds(b, 1)]
                    tstep(dve.tensor_scalar(is_b[:, :], tile_f[:, :], tile_no, None, ALU.is_equal))
                    tstep(dve.tensor_tensor_scan(run[:, :], ones_s[:, :], is_b[:, :], start[:, bass.ds(b, 1)],
                                                 ALU.mult, ALU.add))
                    tstep(dve.tensor_tensor(here[:, :], is_b[:, :], run[:, :], ALU.mult))
                    tstep(dve.tensor_tensor(place_f[:, :], place_f[:, :], here[:, :], ALU.add))
                step(dve.tensor_copy(place[:, :], place_f[:, :]))
                dve.wait_ge(consts, 16)

                def logits(g, q, wait, base):
                    dve.wait_ge(attr_in[q], wait)
                    astep = Chain(dve, attr_steps, base)
                    astep(dve.tensor_tensor(prod[:, :, :], at[:, q, :, :],
                                            a_e[:, None, :].to_broadcast([P, J, E_DIM]), ALU.mult))
                    dve.sem_inc(attr_free, 1)
                    astep(dve.tensor_reduce(logit_e[:, bass.ds(g, 1), :].rearrange("p g j -> p (g j)"),
                                            prod[:, :, :], AX.X, ALU.add))

                with dve.Fori(0, (NG - 2) // 2) as i:
                    for q in range(2):
                        logits(i * 2 + q, q, i * 16 + 16, (i * 2 + q) * 2)
                logits(NG - 2, 0, 16 * (NG // 2), 2 * (NG - 2))
                dve.memset(at[:, 1, :, :], 0.0).then_inc(padded, 1)
                logits(NG - 1, 1, 16 * ((NG - 2) // 2 + (2 if rest else 1)), 2 * (NG - 1))

            @block.tensor
            def _(pe):
                pe.wait_ge(tile_steps, NT)
                nc.tensor.matmul(pc[:, 0, 0:NT], self.before[:, :], counts[:, :], start=True, stop=True)
                nc.tensor.matmul(pc[:, 1, 0:NT], self.ones[:, :], counts[:, :], start=True, stop=True).then_inc(summed, 1)

    def ranges(self, order):
        nc = self.nc
        rec_dram = (self.rec_by_dst, self.rec_by_src)[order]
        with ExitStack() as c:
            def sb(name, shape, dt):
                return c.enter_context(nc.sbuf_tensor(f"{name}{order}", shape, dt))

            def sem(name):
                return self.sem(c, f"{name}{order}")

            rec = sb("rg_rec", [P, NG, J, 2], I32)
            key = sb("rg_key", [P, NG, J], FP32)
            ext = sb("rg_ext", [P, 2, NG], FP32)
            ext_i = sb("rg_exti", [1, 2, NG], I32)
            ext_t = sb("rg_extt", [NG, 2], FP32)
            pT = c.enter_context(nc.psum_tensor(f"rg_pT{order}", [P, 2, P], FP32))
            pR = c.enter_context(nc.psum_tensor(f"rg_pR{order}", [1, 2, P], FP32))
            got, steps, turned, found = sem("rg_got"), sem("rg_steps"), sem("rg_turned"), sem("rg_found")
            block = c.enter_context(nc.Block())

            @block.sync
            def _(sp):
                sp.dma_start(rec[:, :, :, :].rearrange("p g j c -> p g (j c)"),
                             rec_dram.rearrange("(g p j) c -> p g (j c)", p=P, j=J)).then_inc(got, 16)

            @block.vector
            def _(dve):
                step = Chain(dve, steps)
                dve.wait_ge(got, 16)
                step(dve.tensor_copy(key[:, :, :], rec[:, :, :, 1 - order]))
                step(dve.tensor_reduce(ext[:, 0, :], key[:, :, :], AX.X, ALU.min))
                step(dve.tensor_reduce(ext[:, 1, :], key[:, :, :], AX.X, ALU.max))
                dve.wait_ge(turned, 1)
                step(dve.tensor_reduce(ext_t[:, 0:1], pT[0:NG, 0, :], AX.X, ALU.min))
                step(dve.tensor_reduce(ext_t[:, 1:2], pT[0:NG, 1, :], AX.X, ALU.max))
                step(dve.tensor_scalar(ext_t[:, 1:2], ext_t[:, 1:2], float(P), None, ALU.add))
                dve.wait_ge(turned, 2)
                step(dve.tensor_copy(ext_i[:, :, :], pR[:, :, 0:NG]))
                shift = P.bit_length() - 1
                dve.tensor_scalar(self.bounds[0:1, order, :, :], ext_i[:, :, :], shift, None,
                                  ALU.logical_shift_right).then_inc(found, 1)
                dve.wait_ge(found, 1)

            @block.tensor
            def _(pe):
                pe.wait_ge(steps, 3)
                nc.tensor.transpose(pT[0:NG, 0, :], ext[:, 0, :], self.ident[:, :])
                nc.tensor.transpose(pT[0:NG, 1, :], ext[:, 1, :], self.ident[:, :]).then_inc(turned, 1)
                pe.wait_ge(steps, 6)
                nc.tensor.transpose(pR[:, 0, 0:NG], ext_t[:, 0:1], self.ident[0:NG, 0:NG])
                nc.tensor.transpose(pR[:, 1, 0:NG], ext_t[:, 1:2], self.ident[0:NG, 0:NG]).then_inc(turned, 1)

    def aggregate(self, name, order, table, width, acc, at, zero, count=None):
        nc = self.nc
        rec_dram = (self.rec_by_dst, self.rec_by_src)[order]
        recs = rec_dram.rearrange("(g p j) c -> g p (j c)", p=P, j=J)
        R, GS = 4, 2
        tw = table.shape[1]
        with ExitStack() as c:
            def sb(nm, shape, dt):
                return c.enter_context(nc.sbuf_tensor(f"{name}_{nm}", shape, dt))

            def sem(nm):
                return self.sem(c, f"{name}_{nm}")

            rec = sb("rec", [P, R, J, 2], I32)
            rows = sb("rows", [P, GS, J, tw], BF16)
            krel = sb("krel", [P, J], FP32)
            hot = sb("hot", [P, 2 * J, P], BF16)
            one = sb("one", [P, 1], BF16)
            sums = c.enter_context(nc.psum_tensor(f"{name}_sums", [P, 2 * 512], FP32))
            members = c.enter_context(nc.psum_tensor(f"{name}_members", [P, 2 * 512], FP32))
            rec_in = [sem(f"rec_in{s}") for s in range(R)]
            rows_in = [sem(f"rows_in{s}") for s in range(GS)]
            rows_free = sem("rows_free")
            rec_free, rec_used = sem("rec_free"), sem("rec_used")
            pool_turns, pe_turns = sem("pool_turns"), sem("pe_turns")
            hot_ready, sums_ready, steps, zeroed, added = sem("hot_ready"), sem("sums_ready"), sem("steps"), sem("zeroed"), sem("added")
            block = c.enter_context(nc.Block())

            @block.sync
            def _(sp):
                with sp.Fori(0, NG // R) as i:
                    for s in range(R):
                        sp.wait_ge(rec_free, i * R + (s + 1))
                        sp.wait_ge(rec_used, i * R + (s + 1))
                        sp.dma_start(rec[:, s, :, :].rearrange("p j c -> p (j c)"),
                                     recs[bass.ds(i * R + s, 1), :, :].rearrange("g p x -> (g p) x")).then_inc(rec_in[s], 16)

            @block.gpsimd
            def _(pool):
                with pool.Fori(0, NG // R) as i:
                    for s in range(R):
                        q = s % GS
                        pool.wait_ge(rec_in[s], i * 16 + 16)
                        pool.wait_ge(rows_free, i * R + (s + 1))
                        pool.sem_inc(pool_turns, 1)
                        for j in range(J):
                            pool.indirect_dma_start(
                                out=rows[:, q, j, :], out_offset=None, in_=table,
                                in_offset=bass.IndirectOffsetOnAxis(ap=rec[:, s, j, order:order + 1], axis=0),
                            ).then_inc(rows_in[q], 16)

            @block.vector
            def _(dve):
                dve.memset(one[:, :], 1.0).then_inc(zeroed, 1)
                dve.memset(sums[:, 512:1024], 0.0).then_inc(zeroed, 1)
                dve.memset(members[:, 512:1024], 0.0).then_inc(zeroed, 1)
                if zero:
                    dve.memset(acc[:, :, at:at + width], 0.0).then_inc(zeroed, 1)
                if count is not None:
                    dve.memset(count[:, :], 0.0).then_inc(zeroed, 1)
                dve.wait_ge(zeroed, 3 + (1 if zero else 0) + (1 if count is not None else 0))
                dve.sem_inc(rec_free, R)
                dve.sem_inc(added, 1)
                dve.sem_inc(hot_ready, 1)
                npair = dve.alloc_register(f"{name}_dve_pairs")
                slot = dve.alloc_register(f"{name}_dve_slot")
                last_b = dve.alloc_register(f"{name}_dve_tile")
                dve.reg_mov(npair, 0)
                dve.reg_mov(slot, 0)
                dve.reg_mov(last_b, 0)

                def add_last(n, sl, b):
                    cell = acc[:, bass.ds(b, 1), at:at + width].rearrange("p a w -> p (a w)")
                    dve.wait_ge(added, n + 1)
                    if count is not None:
                        many = count[:, bass.ds(b, 1)]
                        dve.tensor_tensor(many, many, members[:, bass.ds((1 - sl) * 512, 1)], ALU.add).then_inc(steps, 1)
                    dve.tensor_tensor(cell, cell, sums[:, bass.ds((1 - sl) * 512, width)], ALU.add).then_inc(added, 1)

                K = 2 if count is not None else 1
                with dve.Fori(0, NG // R) as i:
                    for s in range(R):
                        dve.wait_ge(rec_in[s], i * 16 + 16)
                        g = i * R + s
                        lo = dve.value_load(self.bounds[0:1, order, 0, bass.ds(g, 1)], min_val=0, max_val=NT - 1)
                        hi = dve.value_load(self.bounds[0:1, order, 1, bass.ds(g, 1)], min_val=1, max_val=NT)
                        with dve.Fori(lo, hi) as b:
                            n = dve.snap(npair)
                            sl = dve.snap(slot, min_val=0, max_val=1)
                            b_last = dve.snap(last_b, min_val=0, max_val=NT - 1)
                            dve.wait_ge(hot_ready, n + 1)
                            dve.tensor_scalar(krel[:, :], rec[:, s, :, 1 - order], self.neg_base[:, bass.ds(b, 1)],
                                              None, ALU.add).then_inc(steps, 1)
                            dve.wait_ge(steps, n * K + 1)
                            dve.tensor_tensor(hot[:, bass.ds(sl * J, J), :], self.col[:, None, :].to_broadcast([P, J, P]),
                                              krel[:, :, None].to_broadcast([P, J, P]), ALU.is_equal).then_inc(hot_ready, 1)
                            dve.wait_ge(sums_ready, n + 1)
                            add_last(n, sl, b_last)
                            dve.reg_mov(last_b, b)
                            dve.reg_add(npair, npair, 1)
                            dve.reg_sub(slot, 1, slot)
                        dve.sem_inc(rec_free, 1)
                n = dve.snap(npair)
                sl = dve.snap(slot, min_val=0, max_val=1)
                b_last = dve.snap(last_b, min_val=0, max_val=NT - 1)
                dve.wait_ge(sums_ready, n + 1)
                if count is not None:
                    dve.sem_inc(steps, 1)
                add_last(n, sl, b_last)
                dve.wait_ge(added, n + 2)
                if count is not None:
                    dve.wait_ge(steps, n * K + 2)
                dve.sem_inc(rec_free, 1)

            @block.tensor
            def _(pe):
                pe.wait_ge(zeroed, 3)
                pe.sem_inc(rows_free, GS)
                pe.sem_inc(rec_used, R)
                pe.sem_inc(sums_ready, 1)
                npair = pe.alloc_register(f"{name}_pe_pairs")
                slot = pe.alloc_register(f"{name}_pe_slot")
                pe.reg_mov(npair, 0)
                pe.reg_mov(slot, 0)
                with pe.Fori(0, NG // R) as i:
                    for s in range(R):
                        q = s % GS
                        g = i * R + s
                        lo = pe.value_load(self.bounds[0:1, order, 0, bass.ds(g, 1)], min_val=0, max_val=NT - 1)
                        hi = pe.value_load(self.bounds[0:1, order, 1, bass.ds(g, 1)], min_val=1, max_val=NT)
                        pe.wait_ge(rows_in[q], (i * (R // GS) + (s // GS + 1)) * (16 * J))
                        pe.sem_inc(pe_turns, 1)
                        with pe.Fori(lo, hi) as b:
                            n = pe.snap(npair)
                            sl = pe.snap(slot, min_val=0, max_val=1)
                            pe.wait_ge(added, n + 1)
                            pe.wait_ge(hot_ready, n + 2)
                            out = sums[:, bass.ds(sl * 512, width)]
                            for j in range(J):
                                hot_j = hot[:, bass.ds(sl * J + j, 1), :].rearrange("p a n -> p (a n)")
                                for part in range(3):
                                    last = nc.tensor.matmul(out, hot_j, rows[:, q, j, part * width:(part + 1) * width],
                                                            start=(j == 0 and part == 0), stop=(j == J - 1 and part == 2))
                                if count is not None:
                                    last = nc.tensor.matmul(members[:, bass.ds(sl * 512, 1)], hot_j, one[:, :],
                                                            start=(j == 0), stop=(j == J - 1))
                            last.then_inc(sums_ready, 1)
                            pe.reg_add(npair, npair, 1)
                            pe.reg_sub(slot, 1, slot)
                        pe.wait_ge(sums_ready, pe.snap(npair) + 1)
                        pe.sem_inc(rows_free, 1)
                        pe.sem_inc(rec_used, 1)

    def attention(self, acc, a_dst, degree):
        nc = self.nc
        table, rec_all, place, logit_e = self.tab_z, self.rec, self.place, self.logit_e
        recs = self.rec_by_dst.rearrange("(g p j) c -> g p (j c)", p=P, j=J)
        R, GS = 4, 2
        with ExitStack() as c:
            def sb(nm, shape, dt):
                return c.enter_context(nc.sbuf_tensor(f"at_{nm}", shape, dt))

            def ps(nm, shape):
                return c.enter_context(nc.psum_tensor(f"at_{nm}", shape, FP32))

            def sem(nm):
                return self.sem(c, f"at_{nm}")

            rec = sb("rec", [P, R, J, 2], I32)
            keys = sb("keys", [P, GS, GE], I32)
            rows = sb("rows", [P, GS, J, W0], FP32)
            moved = sb("moved", [P, GS, J, 2], I32)
            target = sb("target", [P, GS, J], I32)
            u = sb("u", [P, J], FP32)
            pen = sb("pen", [P, J, P], FP32)
            enters = sb("enters", [P, J, P], FP32)
            junk = sb("junk", [P, J, P], FP32)
            hot_w = sb("hot_w", [P, J, P], FP32)
            umax = sb("umax", [P, NT], FP32)
            mrun = sb("mrun", [P, NT], FP32)
            tmax = sb("tmax", [P, 1], FP32)
            lin = sb("lin", [P, 1], FP32)
            adm = sb("adm", [P, 2], FP32)
            fell = sb("fell", [P, 1], FP32)
            keep = sb("keep", [P, 1], FP32)
            joined = sb("joined", [P, 1], FP32)
            lg = sb("lg", [P, J], FP32)
            lr = sb("lr", [P, J], FP32)
            w = sb("w", [P, J], FP32)
            krel = sb("krel", [P, J], FP32)
            u_on_nodes = ps("u_on_nodes", [P, J, P])
            looked = ps("looked", [P, J, 64])
            sums = ps("sums", [P, 512])
            rec_in = [sem(f"rec_in{s}") for s in range(R)]
            rows_in = [sem(f"rows_in{s}") for s in range(GS)]
            keys_in = [sem(f"keys_in{s}") for s in range(GS)]
            sent = [sem(f"sent{s}") for s in range(GS)]
            rec_free, rows_free, keys_free = sem("rec_free"), sem("rows_free"), sem("keys_free")
            copied, zeroed, steps, u_ready, ub_ready = sem("copied"), sem("zeroed"), sem("steps"), sem("u_ready"), sem("ub_ready")
            pen_ready, enters_ready, adm_ready, looked_up = sem("pen_ready"), sem("enters_ready"), sem("adm_ready"), sem("looked_up")
            fell_ready, keep_ready, arg_ready, w_ready = sem("fell_ready"), sem("keep_ready"), sem("arg_ready"), sem("w_ready")
            hot_ready, sums_ready = sem("hot_ready"), sem("sums_ready")
            pool_turns, pe_turns, act_turns = sem("pool_turns"), sem("pe_turns"), sem("act_turns")
            block = c.enter_context(nc.Block())
            K = 15

            def limits(eng, g):
                return (eng.value_load(self.bounds[0:1, 0, 0, bass.ds(g, 1)], min_val=0, max_val=NT - 1),
                        eng.value_load(self.bounds[0:1, 0, 1, bass.ds(g, 1)], min_val=1, max_val=NT))

            @block.sync
            def _(sp):
                with sp.Fori(0, NG // R) as i:
                    for s in range(R):
                        q = s % GS
                        sp.wait_ge(rec_free, i * R + (s + 1))
                        sp.dma_start(rec[:, s, :, :].rearrange("p j c -> p (j c)"),
                                     recs[bass.ds(i * R + s, 1), :, :].rearrange("g p x -> (g p) x")).then_inc(rec_in[s], 16)
                        sp.wait_ge(keys_free, i * R + (s + 1))
                        sp.dma_start(keys[:, q, :],
                                     self.key_row.rearrange("(g e) -> g e", e=GE)[bass.ds(i * R + s, 1), :]
                                     .to_broadcast([P, GE])).then_inc(keys_in[q], 16)

            @block.gpsimd
            def _(pool):
                def scatter(g, q, reused):
                    if reused is not None:
                        pool.wait_ge(sent[q], reused)
                    pool.tensor_copy(moved[:, q, :, :], rec_all[:, bass.ds(g, 1), :, :].rearrange("p g j c -> p (g j) c")
                                     ).then_inc(copied, 1)
                    pool.tensor_copy(target[:, q, :], place[:, bass.ds(g * J, J)]).then_inc(copied, 1)
                    pool.wait_ge(copied, g * 2 + 2)
                    pool.sem_inc(pool_turns, 1)
                    for j in range(J):
                        pool.indirect_dma_start(
                            out=self.rec_by_src, in_=moved[:, q, j, :], in_offset=None,
                            out_offset=bass.IndirectOffsetOnAxis(ap=target[:, q, j:j + 1], axis=0),
                        ).then_inc(sent[q], 16)

                def gather(g, s, q, rec_at):
                    pool.wait_ge(rec_in[s], rec_at)
                    pool.wait_ge(rows_free, g + 1)
                    pool.sem_inc(pool_turns, 1)
                    for j in range(J):
                        pool.indirect_dma_start(
                            out=rows[:, q, j, :], out_offset=None, in_=table,
                            in_offset=bass.IndirectOffsetOnAxis(ap=rec[:, s, j, 0:1], axis=0),
                        ).then_inc(rows_in[q], 16)

                for s in range(R):
                    gather(s, s, s % GS, 16)
                    scatter(s, s % GS, None if s < GS else 16 * J * (s // GS))
                with pool.Fori(1, NG // R) as i:
                    for s in range(R):
                        gather(i * R + s, s, s % GS, i * 16 + 16)
                        scatter(i * R + s, s % GS, (i * (R // GS) + s // GS) * (16 * J))
                for q in range(GS):
                    pool.wait_ge(sent[q], 16 * J * (NG // GS))

            @block.vector
            def _(dve):
                dve.memset(acc[:, :, :], 0.0).then_inc(zeroed, 1)
                dve.memset(umax[:, :], -BIG).then_inc(zeroed, 1)
                dve.memset(mrun[:, :], -BIG).then_inc(zeroed, 1)
                dve.memset(degree[:, :], 0.0).then_inc(zeroed, 1)
                dve.wait_ge(zeroed, 4)
                dve.sem_inc(rec_free, R)
                dve.sem_inc(keys_free, GS)
                npair = dve.alloc_register("at_dve_pairs")
                dve.reg_mov(npair, 0)
                with dve.Fori(0, NG // R) as i:
                    for s in range(R):
                        q = s % GS
                        g = i * R + s
                        dve.wait_ge(rec_in[s], i * 16 + 16)
                        dve.wait_ge(rows_in[q], (i * (R // GS) + (s // GS + 1)) * (16 * J))
                        dve.tensor_tensor(u[:, :], rows[:, q, :, C_SRC],
                                          logit_e[:, bass.ds(g, 1), :].rearrange("p g j -> p (g j)"), ALU.add).then_inc(u_ready, 1)
                        dve.wait_ge(u_ready, g + 1)
                        dve.wait_ge(keys_in[q], (i * (R // GS) + (s // GS + 1)) * 16)
                        dve.wait_ge(ub_ready, g + 1)
                        lo, hi = limits(dve, g)
                        with dve.Fori(lo, hi) as b:
                            n = dve.snap(npair)
                            step = Chain(dve, steps, n * K)
                            at_b = bass.ds(b, 1)
                            dve.tensor_scalar(pen[:, :, :], keys[:, q, :].rearrange("p (e j) -> p j e", j=J),
                                              self.node_id[:, at_b], -BIG, ALU.not_equal, ALU.mult).then_inc(pen_ready, 1)
                            dve.wait_ge(pen_ready, n + 1)
                            step(dve.tensor_tensor(junk[:, :, :], u_on_nodes[:, :, :], pen[:, :, :], ALU.add))
                            step(dve.tensor_reduce(tmax[:, :], junk[:, :, :], AX.XY, ALU.max))
                            step(dve.tensor_tensor(umax[:, at_b], umax[:, at_b], tmax[:, :], ALU.max))
                            step(copy(dve, adm[:, 0:1], a_dst[:, at_b]))
                            step(dve.tensor_tensor(lin[:, :], umax[:, at_b], a_dst[:, at_b], ALU.add))
                            step(dve.scalar_tensor_tensor(adm[:, 1:2], lin[:, :], ALPHA, lin[:, :], ALU.mult, ALU.max))
                            step(dve.tensor_tensor(fell[:, :], mrun[:, at_b], adm[:, 1:2], ALU.subtract))
                            step(copy(dve, mrun[:, at_b], adm[:, 1:2]))
                            step(dve.tensor_scalar(krel[:, :], rec[:, s, :, 1], self.neg_base[:, at_b], None, ALU.add))
                            dve.wait_ge(looked_up, n + 1)
                            step(dve.tensor_tensor(lg[:, :], u[:, :], looked[:, :, 0], ALU.add))
                            step(dve.scalar_tensor_tensor(lr[:, :], lg[:, :], ALPHA, lg[:, :], ALU.mult, ALU.max))
                            step(dve.tensor_tensor(lr[:, :], lr[:, :], looked[:, :, 1], ALU.subtract))
                            step(dve.tensor_scalar(lr[:, :], lr[:, :], 0.0, None, ALU.min))
                            dve.wait_ge(w_ready, n + 1)
                            for j in range(J):
                                last = dve.tensor_scalar(hot_w[:, j, :], self.col[:, :], krel[:, j:j + 1], w[:, j:j + 1],
                                                         ALU.is_equal, ALU.mult)
                            last.then_inc(hot_ready, 1)
                            dve.wait_ge(enters_ready, n + 1)
                            step(dve.tensor_tensor(degree[:, at_b], degree[:, at_b], joined[:, :], ALU.add))
                            dve.wait_ge(keep_ready, n + 1)
                            dve.wait_ge(sums_ready, n + 1)
                            cell = acc[:, at_b, :].rearrange("p a w -> p (a w)")
                            step(dve.scalar_tensor_tensor(cell, cell, keep[:, :], sums[:, 0:F + 1], ALU.mult, ALU.add))
                            assert step.n == K
                            dve.reg_add(npair, npair, 1)
                        dve.sem_inc(rec_free, 1)
                        dve.sem_inc(keys_free, 1)

            @block.scalar
            def _(act):
                npair = act.alloc_register("at_act_pairs")
                act.reg_mov(npair, 0)
                with act.Fori(0, NG) as g:
                    lo, hi = limits(act, g)
                    with act.Fori(lo, hi) as b:
                        n = act.snap(npair)
                        act.wait_ge(pen_ready, n + 1)
                        act.activation(enters[:, :, :], pen[:, :, :], ACT.Identity, bias=1.0, scale=1.0 / BIG,
                                       accum_out=joined[:, :]).then_inc(enters_ready, 1)
                        act.wait_ge(steps, n * K + 7)
                        act.activation(keep[:, :], fell[:, :], ACT.Exp).then_inc(keep_ready, 1)
                        act.wait_ge(steps, n * K + 13)
                        act.activation(w[:, :], lr[:, :], ACT.Exp).then_inc(w_ready, 1)
                        act.reg_add(npair, npair, 1)

            @block.tensor
            def _(pe):
                pe.sem_inc(rows_free, GS)
                npair = pe.alloc_register("at_pe_pairs")
                pe.reg_mov(npair, 0)
                with pe.Fori(0, NG // R) as i:
                    for s in range(R):
                        q = s % GS
                        g = i * R + s
                        lo, hi = limits(pe, g)
                        pe.wait_ge(rows_in[q], (i * (R // GS) + (s // GS + 1)) * (16 * J))
                        pe.wait_ge(u_ready, g + 1)
                        for j in range(J):
                            last = nc.tensor.matmul(u_on_nodes[:, j, :], u[:, j:j + 1].to_broadcast([P, P]),
                                                    self.ident[:, :], start=True, stop=True)
                        last.then_inc(ub_ready, 1)
                        with pe.Fori(lo, hi) as b:
                            n = pe.snap(npair)
                            pe.wait_ge(enters_ready, n + 1)
                            pe.wait_ge(steps, n * K + 6)
                            for j in range(J):
                                last = nc.tensor.matmul(looked[:, j, 0:2], enters[:, j, :], adm[:, :], start=True, stop=True)
                            last.then_inc(looked_up, 1)
                            pe.wait_ge(hot_ready, n + 1)
                            for j in range(J):
                                last = nc.tensor.matmul(sums[:, 0:F + 1], hot_w[:, j, :], rows[:, q, j, 0:F + 1],
                                                        start=(j == 0), stop=(j == J - 1))
                            last.then_inc(sums_ready, 1)
                            pe.reg_add(npair, npair, 1)
                        pe.wait_ge(sums_ready, pe.snap(npair))
                        pe.sem_inc(rows_free, 1)

    def product(self, name, terms, vectors, finish, finish_steps, prepare=None, prepare_steps=0, bufs=(), stores=()):
        nc = self.nc
        nk = len(terms)
        with ExitStack() as c:
            def sb(nm, shape, dt):
                return c.enter_context(nc.sbuf_tensor(f"{name}_{nm}", shape, dt))

            def sem(nm):
                return self.sem(c, f"{name}_{nm}")

            xin = sb("xin", [P, 2, nk, F], FP32)
            xT = sb("xT", [P, 2, 2 * nk, P], FP32)
            weights, vecs, loads = [], [], []
            for k, (_, w) in enumerate(terms):
                if w.shape[0] == F:
                    weights.append(sb(f"w{k}", [P, 2, F], FP32))
                    loads.append((weights[k][:, :, :], w.rearrange("(c k) n -> k c n", k=P)))
                else:
                    weights.append(w)
            for k, v in enumerate(vectors):
                vecs.append(sb(f"v{k}", [P, v.shape[0]], FP32))
                loads.append((vecs[k][:, :], row_on_all(v)))
            buf = {nm: sb(nm, [P, 2] + shape, dt) for nm, shape, dt in bufs}
            pT = c.enter_context(nc.psum_tensor(f"{name}_pT", [P, 2, 4, P], FP32))
            pY = c.enter_context(nc.psum_tensor(f"{name}_pY", [P, 2, 512], FP32))
            loaded, prepared, fetched, turned, xT_ready = sem("loaded"), sem("prepared"), sem("fetched"), sem("turned"), sem("xT_ready")
            y_ready, finished, psteps, fsteps = sem("y_ready"), sem("finished"), sem("psteps"), sem("fsteps")
            stored = [sem(f"stored{s}") for s in range(2)]
            block = c.enter_context(nc.Block())

            def over_tiles(eng, body):
                body(0, 0, None)
                body(1, 1, None)
                with eng.Fori(1, NT // 2 - 1) as i:
                    for s in range(2):
                        body(i * 2 + s, s, i)
                for t in range((NT // 2 - 1) * 2, NT):
                    body(t, t % 2, t // 2)

            @block.sync
            def _(sp):
                for dst, src in loads:
                    sp.dma_start(dst, src).then_inc(loaded, 16)

                def body(t, s, used):
                    sp.wait_ge(finished, t + 1)
                    for rows, part in stores:
                        sp.dma_start(rows.rearrange("(b p) f -> b p f", p=P)[bass.ds(t, 1), :, :]
                                     .rearrange("b p f -> (b p) f"), part(buf, s)).then_inc(stored[s], 16)
                if stores:
                    over_tiles(sp, body)
                    for s in range(2):
                        sp.wait_ge(stored[s], 16 * len(stores) * ((NT + 1 - s) // 2))

            @block.vector
            def _(dve):
                def prep(t):
                    step = Chain(dve, psteps, t * prepare_steps)
                    prepare(dve, step, t)
                    assert step.n == prepare_steps
                    dve.sem_inc(prepared, 1)

                def body(t, s, used):
                    if prepare and not is_int(t, NT - 2):
                        prep(t + 2)
                    dve.wait_ge(y_ready, t + 1)
                    if stores and used is not None:
                        dve.wait_ge(stored[s], used * (16 * len(stores)))
                    step = Chain(dve, fsteps, t * finish_steps)
                    finish(dve, step, t, pY[:, s, 0:F], {nm: b[:, s] for nm, b in buf.items()}, vecs)
                    assert step.n == finish_steps
                    dve.sem_inc(finished, 1)

                dve.wait_ge(loaded, 16 * len(loads))
                if prepare:
                    prep(0)
                    prep(1)
                over_tiles(dve, body)

            @block.scalar
            def _(act):
                def fetch(t, s):
                    if prepare:
                        act.wait_ge(prepared, t + 1)
                    for k, (a, _) in enumerate(terms):
                        act.activation(xin[:, s, k, :], tile(a, t)[:, 0:F], ACT.Copy).then_inc(fetched, 1)

                fetch(0, 0)
                fetch(1, 1)

                def body(t, s, used):
                    act.wait_ge(turned, t + 1)
                    act.activation(xT[:, s, :, :], pT[:, s, 0:2 * nk, :], ACT.Copy).then_inc(xT_ready, 1)
                    if not is_int(t, NT - 2):
                        fetch(t + 2, s)
                over_tiles(act, body)

            @block.tensor
            def _(pe):
                def turn(t, s):
                    pe.wait_ge(fetched, (t + 1) * nk)
                    for k in range(nk):
                        for h in range(2):
                            last = nc.tensor.transpose(pT[:, s, 2 * k + h, :], xin[:, s, k, h * P:(h + 1) * P],
                                                       self.ident[:, :])
                    last.then_inc(turned, 1)

                def body(t, s, used):
                    if not is_int(t, NT - 1):
                        turn(t + 1, 1 - s)
                    pe.wait_ge(xT_ready, t + 1)
                    if used is not None:
                        pe.wait_ge(finished, t - 1)
                    for k in range(nk):
                        for h in range(2):
                            last = nc.tensor.matmul(pY[:, s, 0:F], xT[:, s, 2 * k + h, :], weights[k][:, h, :],
                                                    start=(k == 0 and h == 0), stop=(k == nk - 1 and h == 1))
                    last.then_inc(y_ready, 1)

                if loads:
                    pe.wait_ge(loaded, 16 * len(loads))
                turn(0, 0)
                over_tiles(pe, body)

    def statistics(self, name, combine, steps_of_tile, setup=None, setup_steps=0, vectors=()):
        nc = self.nc
        with ExitStack() as c:
            def sem(nm):
                return self.sem(c, f"{name}_{nm}")

            vecs = [c.enter_context(nc.sbuf_tensor(f"{name}_v{k}", [P, v.shape[0]], FP32)) for k, v in enumerate(vectors)]
            ssteps, tsteps, loaded = sem("ssteps"), sem("tsteps"), sem("loaded")
            block = c.enter_context(nc.Block())

            @block.sync
            def _(sp):
                for dst, v in zip(vecs, vectors):
                    sp.dma_start(dst[:, :], row_on_all(v)).then_inc(loaded, 16)

            @block.vector
            def _(dve):
                if vectors:
                    dve.wait_ge(loaded, 16 * len(vectors))
                step = Chain(dve, ssteps)
                if setup:
                    setup(dve, step)
                with dve.Fori(0, NT) as t:
                    step = Chain(dve, tsteps, t * (steps_of_tile + 4))
                    combine(dve, step, t, vecs)
                    self.moments(dve, step, t)
                    assert step.n == steps_of_tile + 4
        self.inverse_deviation(name)

    def moments(self, dve, step, t):
        step(copy(dve, self.xt[:, :], tile(self.x, t)))
        step(dve.bn_stats(self.bn[:, 0:6], self.xt[:, :]))
        dve.sem_inc(self.dve_turns, 1)
        step(dve.bn_aggr(self.bn[:, 6:8], self.bn[:, 0:6]))
        step(copy(dve, tile(self.moment, t), self.bn[:, 6:8]))

    def inverse_deviation(self, name):
        nc = self.nc
        with ExitStack() as c:
            added, rooted, inverted = (self.sem(c, f"{name}_{nm}") for nm in ("added", "rooted", "inverted"))
            block = c.enter_context(nc.Block())
            var = self.moment[:, :, 1]

            @block.vector
            def _(dve):
                dve.tensor_scalar(var, var, EPS, None, ALU.add).then_inc(added, 1)
                dve.wait_ge(rooted, 1)
                dve.reciprocal(var, var).then_inc(inverted, 1)
                dve.wait_ge(inverted, 1)

            @block.scalar
            def _(act):
                act.wait_ge(added, 1)
                act.activation(var, var, ACT.Sqrt).then_inc(rooted, 1)

    def normalize(self, dve, step, t):
        x = tile(self.x, t)
        step(dve.tensor_scalar(x, x, self.moment[:, bass.ds(t, 1), 0], self.moment[:, bass.ds(t, 1), 1],
                               ALU.subtract, ALU.mult))

    def split(self, dve, step, parts, v, width):
        r = self.rest[:, 0:width]
        step(copy(dve, parts[0], v))
        step(dve.tensor_tensor(r, v, parts[0], ALU.subtract))
        step(dve.tensor_copy(parts[1], r))
        step(dve.tensor_tensor(parts[2], r, parts[1], ALU.subtract))

    def load_nodes(self):
        nc = self.nc
        x, w_z, w_f, w_b = (self.ins[n] for n in ("x", "L0_gnn_W", "L2_gnn_W_f", "L2_gnn_W_b"))
        with ExitStack() as c:
            wr = c.enter_context(nc.sbuf_tensor("ln_w", [P, 4, F], FP32))
            pw = c.enter_context(nc.psum_tensor("ln_pw", [P, 4, 2, P], FP32))
            cleared, nodes_in, w_in, turned, kept = (self.sem(c, f"ln_{n}")
                                                     for n in ("cleared", "nodes_in", "w_in", "turned", "kept"))
            block = c.enter_context(nc.Block())

            @block.sync
            def _(sp):
                sp.dma_start(wr[:, 0:2, :], w_z.rearrange("(c m) k -> m c k", m=P)).then_inc(w_in, 16)
                sp.dma_start(wr[:, 2, :], w_f).then_inc(w_in, 16)
                sp.dma_start(wr[:, 3, :], w_b).then_inc(w_in, 16)
                sp.wait_ge(cleared, 1)
                sp.dma_start(self.x[:, 0:NT - 1, :], x[0:(NT - 1) * P, :].rearrange("(b p) f -> p b f", p=P)).then_inc(nodes_in, 16)
                sp.dma_start(self.x[0:LAST, NT - 1, :], x[(NT - 1) * P:N_NODES, :]).then_inc(nodes_in, 16)
                sp.wait_ge(nodes_in, 32)

            @block.vector
            def _(dve):
                dve.memset(self.x[:, NT - 1, :], 0.0).then_inc(cleared, 1)
                dve.wait_ge(turned, 1)
                for m in range(4):
                    dst = (self.w_z, self.w_fb)[m // 2]
                    dve.tensor_copy(dst[:, :, (m % 2) * P:(m % 2 + 1) * P], pw[:, m, :, :]).then_inc(kept, 1)
                dve.wait_ge(kept, 4)

            @block.tensor
            def _(pe):
                pe.wait_ge(w_in, 48)
                for m in range(4):
                    for h in range(2):
                        last = nc.tensor.transpose(pw[:, m, h, :], wr[:, m, h * P:(h + 1) * P], self.ident[:, :])
                last.then_inc(turned, 1)

    def degree_factors(self):
        nc = self.nc
        with ExitStack() as c:
            steps, rooted = (self.sem(c, f"df_{n}") for n in ("steps", "rooted"))
            safe = c.enter_context(nc.sbuf_tensor("df_safe", [P, NT], FP32))
            some = c.enter_context(nc.sbuf_tensor("df_some", [P, NT], FP32))
            block = c.enter_context(nc.Block())

            @block.vector
            def _(dve):
                step = Chain(dve, steps)
                step(dve.tensor_scalar(self.r_in[:, :], self.deg_src[:, :], 1.0, None, ALU.add))
                step(dve.tensor_scalar(self.r_out[:, :], self.deg_dst[:, :], 1.0, None, ALU.add))
                step(dve.tensor_scalar(safe[:, :], self.deg_dst[:, :], 1.0, None, ALU.max))
                step(dve.tensor_scalar(some[:, :], self.deg_dst[:, :], 0.0, None, ALU.is_gt))
                dve.wait_ge(rooted, 3)
                step(dve.reciprocal(self.r_in[:, :], self.r_in[:, :]))
                step(dve.reciprocal(self.r_out[:, :], self.r_out[:, :]))
                step(dve.reciprocal(safe[:, :], safe[:, :]))
                step(dve.tensor_tensor(self.r_dst[:, :], safe[:, :], some[:, :], ALU.mult))
                step(dve.tensor_scalar(safe[:, :], self.deg_src[:, :], 1.0, None, ALU.max))
                step(dve.reciprocal(self.mean_src[:, :], safe[:, :]))

            @block.scalar
            def _(act):
                act.wait_ge(steps, 4)
                for a in (self.r_in, self.r_out, safe):
                    act.activation(a[:, :], a[:, :], ACT.Sqrt).then_inc(rooted, 1)

    def finish_nodes(self):
        nc = self.nc
        CH = 7
        with ExitStack() as c:
            steps, stored = (self.sem(c, f"fn_{n}") for n in ("steps", "stored"))
            block = c.enter_context(nc.Block())

            @block.vector
            def _(dve):
                with dve.Fori(0, NT) as t:
                    step = Chain(dve, steps, t)
                    self.normalize(dve, step, t)

            @block.sync
            def _(sp):
                for b in range(0, NT - CH, CH):
                    sp.wait_ge(steps, b + CH)
                    sp.dma_start(self.out[b * P:(b + CH) * P, :].rearrange("(b p) f -> p b f", p=P),
                                 self.x[:, b:b + CH, :]).then_inc(stored, 16)
                b = NT - CH
                sp.wait_ge(steps, NT)
                sp.dma_start(self.out[b * P:(NT - 1) * P, :].rearrange("(b p) f -> p b f", p=P),
                             self.x[:, b:NT - 1, :]).then_inc(stored, 16)
                sp.dma_start(self.out[(NT - 1) * P:N_NODES, :], self.x[0:LAST, NT - 1, :]).then_inc(stored, 16)
                sp.wait_ge(stored, 16 * (NT // CH + 1))


def tile(a, t):
    return a[:, bass.ds(t, 1), :].rearrange("p b f -> p (b f)")


def build(nc, ins, out):
    with ExitStack() as ctx:
        k = Kernel(nc, ctx, ins, out)
        sb = k.sb
        k.x = sb("x", [P, NT, F], FP32)
        k.acc = acc = sb("acc", [P, NT, F + 1], FP32)
        k.moment = sb("moment", [P, NT, 2], FP32)
        k.bn = sb("bn", [P, 8], FP32)
        k.dve_turns = ctx.enter_context(nc.semaphore("dve_turns"))
        k.xt = sb("xt", [P, F], FP32)
        k.rest = sb("rest", [P, F], FP32)
        k.tmp = sb("tmp", [P, F], FP32)
        k.w_z = sb("w_z", [P, 2, F], FP32)
        k.w_fb = sb("w_fb", [P, 2, F], FP32)
        k.deg_src = sb("deg_src", [P, NT], FP32)
        k.deg_dst = sb("deg_dst", [P, NT], FP32)
        k.r_in = sb("r_in", [P, NT], FP32)
        k.r_out = sb("r_out", [P, NT], FP32)
        k.r_dst = sb("r_dst", [P, NT], FP32)
        k.mean_src = sb("mean_src", [P, NT], FP32)
        k.constants()
        k.load_nodes()

        with ExitStack() as c:
            def scoped(name, shape, dt):
                return c.enter_context(nc.sbuf_tensor(name, shape, dt))

            k.rec = scoped("rec_all", [P, NG, J, 2], I32)
            k.place = scoped("place", [P, S], I32)
            k.logit_e = scoped("logit_e", [P, NG, J], FP32)
            a_dst = scoped("a_dst", [P, NT], FP32)
            k.edges()
            k.ranges(0)

            def finish_z(dve, step, t, y, buf, vec):
                z = buf["row"][:, 0:F]
                step(dve.memset(buf["row"][:, F:W0], 1.0))
                step(dve.tensor_copy(z, y))
                step(dve.tensor_tensor(k.tmp[:, :], z, vec[0][:, :], ALU.mult))
                step(dve.tensor_reduce(buf["row"][:, C_SRC:C_SRC + 1], k.tmp[:, :], AX.X, ALU.add))
                step(dve.tensor_tensor(k.tmp[:, :], z, vec[1][:, :], ALU.mult))
                step(dve.tensor_reduce(a_dst[:, bass.ds(t, 1)], k.tmp[:, :], AX.X, ALU.add))

            k.product("z", [(k.x, k.w_z)], [ins["L0_gnn_A"][0, 0:F], ins["L0_gnn_A"][0, F:2 * F]], finish_z, 6,
                      bufs=[("row", [W0], FP32)], stores=[(k.tab_z, lambda b, s: b["row"][:, s, :])])
            k.attention(acc, a_dst, k.deg_dst)
        k.ranges(1)

        def softmax_setup(dve, step):
            step(dve.tensor_scalar(acc[:, :, F], acc[:, :, F], 2.0 ** -100, None, ALU.max))
            step(dve.reciprocal(acc[:, :, F], acc[:, :, F]))

        def add_attention(dve, step, t, vec):
            x = tile(k.x, t)
            step(dve.scalar_tensor_tensor(x, tile(acc, t)[:, 0:F], acc[:, bass.ds(t, 1), F], x, ALU.mult, ALU.add))

        k.statistics("s0", add_attention, 1, softmax_setup)

        with ExitStack() as c:
            h = c.enter_context(nc.sbuf_tensor("h", [P, NT, F], FP32))
            parts = [("parts", [3, F], BF16)]

            def three(buf, width=F):
                return [buf[:, p, :] for p in range(3)]

            def row_of(b, s):
                return b["parts"][:, s, :, :].rearrange("p c f -> p (c f)")

            def finish_in(dve, step, t, y, buf, vec):
                step(dve.tensor_tensor(tile(h, t), y, vec[0][:, :], ALU.add))
                k.split(dve, step, three(buf["parts"]), tile(h, t), F)

            k.product("in", [(k.x, ins["L1_gnn_W_in"])], [ins["L1_gnn_b_in"]], finish_in, 5,
                      prepare=k.normalize, prepare_steps=1, bufs=parts, stores=[(k.tab_h[0], row_of)])

            def mean(dve, step, t):
                a = tile(acc, t)[:, 0:F]
                step(dve.tensor_scalar(a, a, k.mean_src[:, bass.ds(t, 1)], None, ALU.mult))

            def finish_layer(dve, step, t, y, buf, vec):
                step(dve.tensor_tensor(k.tmp[:, :], y, vec[0][:, :], ALU.add))
                step(dve.tensor_scalar(tile(h, t), k.tmp[:, :], 0.0, None, ALU.max))
                k.split(dve, step, three(buf["parts"]), tile(h, t), F)

            for layer in range(3):
                k.aggregate(f"h{layer}", 1, k.tab_h[layer], F, acc, 0, True, count=k.deg_src if layer == 0 else None)
                if layer == 0:
                    k.degree_factors()
                k.product(f"l{layer}", [(acc, ins["L1_gnn_W_agg"][layer]), (h, ins["L1_gnn_W_self"][layer])],
                          [ins["L1_gnn_b_hid"][layer]], finish_layer, 6, prepare=mean, prepare_steps=1,
                          bufs=parts if layer < 2 else [("parts", [3, F], BF16)],
                          stores=[(k.tab_h[layer + 1], row_of)] if layer < 2 else [])

            def finish_out(dve, step, t, y, buf, vec):
                x = tile(k.x, t)
                step(dve.tensor_tensor(k.tmp[:, :], y, vec[0][:, :], ALU.add))
                step(dve.tensor_tensor(x, x, k.tmp[:, :], ALU.add))
                k.moments(dve, step, t)

            k.product("out", [(h, ins["L1_gnn_W_out"])], [ins["L1_gnn_b_out"]], finish_out, 6)
        k.inverse_deviation("out")

        def finish_fb(dve, step, t, y, buf, vec):
            for w, r in enumerate((k.r_out, k.r_in)):
                a = tile(acc, t)[:, w * H:(w + 1) * H]
                step(dve.tensor_scalar(a, y[:, w * H:(w + 1) * H], r[:, bass.ds(t, 1)], None, ALU.mult))
                k.split(dve, step, [buf[f"parts{w}"][:, p, :] for p in range(3)], a, H)

        k.product("fb", [(k.x, k.w_fb)], [], finish_fb, 10, prepare=k.normalize, prepare_steps=1,
                  bufs=[(f"parts{w}", [3, H], BF16) for w in range(2)],
                  stores=[(k.tab_fb[w], lambda b, s, w=w: b[f"parts{w}"][:, s, :, :].rearrange("p c f -> p (c f)"))
                          for w in range(2)])
        k.aggregate("f", 1, k.tab_fb[0], H, acc, 0, False)
        k.aggregate("b", 0, k.tab_fb[1], H, acc, H, False)

        def add_fb(dve, step, t, vec):
            x = tile(k.x, t)
            for w, r in enumerate((k.r_in, k.r_out)):
                cols = slice(w * H, (w + 1) * H)
                step(dve.scalar_tensor_tensor(k.tmp[:, cols], tile(acc, t)[:, cols], r[:, bass.ds(t, 1)], vec[0][:, cols],
                                              ALU.mult, ALU.add))
            step(dve.tensor_tensor(x, x, k.tmp[:, :], ALU.add))

        k.statistics("s2", add_fb, 3, vectors=[ins["L2_gnn_bias_param"]])

        def finish_g(dve, step, t, y, buf, vec):
            step(dve.tensor_scalar(k.tmp[:, :], y, k.r_dst[:, bass.ds(t, 1)], None, ALU.mult))
            k.split(dve, step, [buf["parts"][:, p, :] for p in range(3)], k.tmp[:, :], F)

        k.product("g", [(k.x, ins["L3_gnn_W"])], [], finish_g, 5, prepare=k.normalize, prepare_steps=1,
                  bufs=[("parts", [3, F], BF16)],
                  stores=[(k.tab_g, lambda b, s: b["parts"][:, s, :, :].rearrange("p c f -> p (c f)"))])
        k.aggregate("gg", 0, k.tab_g, F, acc, 0, True)

        def add_g(dve, step, t, vec):
            x = tile(k.x, t)
            step(dve.scalar_tensor_tensor(x, tile(acc, t)[:, 0:F], k.r_dst[:, bass.ds(t, 1)], x, ALU.mult, ALU.add))

        k.statistics("s3", add_g, 1)
        k.finish_nodes()


_INS = ['x', 'src', 'dst', 'edge_attr_64', 'L0_gnn_W', 'L0_gnn_A', 'L1_gnn_W_in', 'L1_gnn_b_in', 'L1_gnn_W_agg',
        'L1_gnn_W_self', 'L1_gnn_b_hid', 'L1_gnn_W_out', 'L1_gnn_b_out', 'L2_gnn_W_f', 'L2_gnn_W_b',
        'L2_gnn_bias_param', 'L3_gnn_W']


def kernel(**inputs):
    import numpy as _np
    import concourse.bacc as _bacc
    from concourse import mybir as _mybir
    from concourse.bass_utils import run_bass_kernel_spmd as _run

    nc = _bacc.Bacc("TRN2", target_bir_lowering=False, num_devices=1)
    arrays, args = {}, {}
    for name in _INS:
        a = _np.ascontiguousarray(inputs[name])
        arrays[f"in_{name}_dram"] = a
        args[name] = nc.dram_tensor(f"in_{name}_dram", a.shape, _mybir.dt.from_np(a.dtype), kind="ExternalInput").ap()
    out = nc.dram_tensor("out_0_dram", (6250, 256), _mybir.dt.float32, kind="ExternalOutput").ap()
    build(nc, args, out)
    r = _run(nc, [arrays], core_ids=[0])
    return r.results[0]["out_0_dram"]
```

```python
import concourse.bass as bass
from concourse import mybir
from contextlib import ExitStack

FP32 = mybir.dt.float32
I32 = mybir.dt.int32
BF16 = mybir.dt.bfloat16
ALU = mybir.AluOpType
ACT = mybir.ActivationFunctionType
AX = mybir.AxisListType

P = 128
N_NODES = 6250
N_EDGES = 106250
F = 256
E_DIM = 64
NT = -(-N_NODES // P)
NPAD = NT * P
LAST = N_NODES - (NT - 1) * P
J = 8
GE = P * J
NG = -(-N_EDGES // GE)
S = NG * J
EPAD = NG * GE
TAIL = N_EDGES - (NG - 1) * GE
PAD_NODE = NPAD - 1
BIG = 2.0 ** 126
H = F // 2
W0 = F + 4
C_ONE, C_SRC = F, F + 1
EPS = 1e-5
ALPHA = 0.2


def copy(eng, out, in_):
    return eng.tensor_scalar(out, in_, 1.0, None, ALU.mult)


def row_on_all(row):
    return row.rearrange("(a n) -> a n", a=1).to_broadcast([P, row.shape[0]])


def is_int(t, least):
    return isinstance(t, int) and t >= least


class Chain:

    def __init__(self, eng, sem, base=0):
        self.eng, self.sem, self.base, self.n = eng, sem, base, 0

    def __call__(self, ins):
        self.n += 1
        ins.then_inc(self.sem, 1)
        self.eng.wait_ge(self.sem, self.base + self.n)


class Kernel:
    def __init__(self, nc, ctx, ins, out):
        self.nc, self.ctx, self.ins, self.out = nc, ctx, ins, out
        self.scopes = {}
        sb, dram = self.sb, self.dram
        self.rec_by_dst = dram("rec_by_dst", [EPAD, 2], I32)
        self.rec_by_src = dram("rec_by_src", [EPAD, 2], I32)
        self.key_row = dram("key_row", [EPAD], I32)
        self.tab_z = dram("tab_z", [NPAD, W0], FP32)
        self.tab_h = [dram(f"tab_h{k}", [NPAD, 3 * F], BF16) for k in range(3)]
        self.tab_fb = [dram(f"tab_{k}", [NPAD, 3 * H], BF16) for k in ("f", "b")]
        self.tab_g = dram("tab_g", [NPAD, 3 * F], BF16)
        self.bounds = sb("bounds", [1, 2, 2, NG], I32)
        self.ident = sb("ident", [P, P], FP32)
        self.ones = sb("ones", [P, P], FP32)
        self.before = sb("before", [P, P], FP32)
        self.col = sb("col", [P, P], FP32)
        self.node_id = sb("node_id", [P, NT], FP32)
        self.tile_no = sb("tile_no", [P, NT], FP32)
        self.neg_base = sb("neg_base", [P, NT], FP32)

    def sb(self, name, shape, dt):
        return self.ctx.enter_context(self.nc.sbuf_tensor(name, shape, dt))

    def ps(self, name, shape, dt):
        return self.ctx.enter_context(self.nc.psum_tensor(name, shape, dt))

    def sem(self, scope, name):
        if scope not in self.scopes:
            self.scopes[scope] = handles = []
            scope.callback(self.nc.all_engine_barrier)
            scope.callback(self.nc.clear_and_free_semaphores, handles)
        self.scopes[scope].append(self.nc.alloc_semaphore(name))
        return self.scopes[scope][-1]

    def dram(self, name, shape, dt):
        return self.nc.dram_tensor(name, shape, dt, kind="Internal").ap()

    def constants(self):
        nc = self.nc
        with ExitStack() as c:
            filled = self.sem(c, "filled")
            made = self.sem(c, "made")
            ids_made = self.sem(c, "ids_made")
            cast = self.sem(c, "cast")
            iot = c.enter_context(nc.sbuf_tensor("iot", [P, P], I32))
            iob = c.enter_context(nc.sbuf_tensor("iob", [P, NT], I32))
            ion = c.enter_context(nc.sbuf_tensor("ion", [P, NT], I32))
            block = c.enter_context(nc.Block())

            @block.gpsimd
            def _(pool):
                pool.memset(self.ident[:, :], 0.0).then_inc(filled, 1)
                pool.memset(self.ones[:, :], 1.0).then_inc(filled, 1)
                pool.memset(self.before[:, :], 1.0).then_inc(filled, 1)
                pool.iota(iot[:, :], pattern=[[1, P]], base=0, channel_multiplier=0).then_inc(ids_made, 1)
                pool.iota(iob[:, :], pattern=[[-P, NT]], base=0, channel_multiplier=0).then_inc(ids_made, 1)
                pool.iota(ion[:, :], pattern=[[P, NT]], base=0, channel_multiplier=1).then_inc(ids_made, 1)
                pool.wait_ge(filled, 3)
                pool.affine_select(out=self.ident[:, :], in_=self.ident[:, :], compare_op=ALU.not_equal, fill=1.0,
                                   base=0, pattern=[[-1, P]], channel_multiplier=1).then_inc(made, 1)
                pool.affine_select(out=self.before[:, :], in_=self.before[:, :], compare_op=ALU.is_gt, fill=0.0,
                                   base=0, pattern=[[1, P]], channel_multiplier=-1).then_inc(made, 1)
                pool.wait_ge(made, 2)

            @block.vector
            def _(dve):
                dve.wait_ge(ids_made, 3)
                dve.tensor_copy(self.col[:, :], iot[:, :]).then_inc(cast, 1)
                dve.tensor_copy(self.neg_base[:, :], iob[:, :]).then_inc(cast, 1)
                dve.tensor_copy(self.node_id[:, :], ion[:, :]).then_inc(cast, 1)
                dve.tensor_copy(self.tile_no[:, :], iot[:, 0:NT]).then_inc(cast, 1)
                dve.wait_ge(cast, 4)

    def edges(self):
        nc = self.nc
        src, dst = self.ins["src"], self.ins["dst"]
        attr = self.ins["edge_attr_64"]
        attr_full = attr[0:(NG - 1) * GE, :].rearrange("(g p j) d -> g p (j d)", p=P, j=J)
        first = (NG - 1) * GE
        whole, rest = TAIL // J, TAIL % J
        rec, place, logit_e = self.rec, self.place, self.logit_e
        with ExitStack() as c:
            def sb(name, shape, dt):
                return c.enter_context(nc.sbuf_tensor(name, shape, dt))

            def sem(name):
                return self.sem(c, name)

            ids = sb("ids", [P, 2, NG, J], I32)
            tile_i = sb("tile_i", [P, S], I32)
            tile_f = sb("tile_f", [P, S], FP32)
            is_b = sb("is_b", [P, S], FP32)
            run = sb("run", [P, S], FP32)
            here = sb("here", [P, S], FP32)
            place_f = sb("place_f", [P, S], FP32)
            ones_s = sb("ones_s", [P, S], FP32)
            counts = sb("counts", [P, NT], FP32)
            total = sb("total", [P, NT], FP32)
            upto = sb("upto", [P, NT], FP32)
            start = sb("start", [P, NT], FP32)
            a_e = sb("a_e", [P, E_DIM], FP32)
            at = sb("at", [P, 2, J, E_DIM], FP32)
            prod = sb("prod", [P, J, E_DIM], FP32)
            pc = c.enter_context(nc.psum_tensor("pc", [P, 2, 256], FP32))
            padded, packed, stored = sem("padded"), sem("packed"), sem("stored")
            loaded, consts, summed = sem("loaded"), sem("consts"), sem("summed")
            attr_in = [sem(f"attr_in{q}") for q in range(2)]
            attr_free, steps, tile_steps, attr_steps = sem("attr_free"), sem("steps"), sem("tile_steps"), sem("attr_steps")
            block = c.enter_context(nc.Block())
            n_loads = 2 * (3 if rest else 2)

            @block.sync
            def _(sp):
                sp.wait_ge(padded, 1)
                for w, a in enumerate((src, dst)):
                    sp.dma_start(ids[:, w, 0:NG - 1, :],
                                 a[0:first].rearrange("(g p j) -> p g j", p=P, j=J)).then_inc(loaded, 16)
                    sp.dma_start(ids[0:whole, w, NG - 1, :],
                                 a[first:first + whole * J].rearrange("(p j) -> p j", j=J)).then_inc(loaded, 16)
                    if rest:
                        sp.dma_start(ids[whole:whole + 1, w, NG - 1, 0:rest],
                                     a[first + whole * J:N_EDGES].rearrange("(p j) -> p j", p=1)).then_inc(loaded, 16)
                sp.dma_start(a_e[:, :], row_on_all(self.ins["L0_gnn_A"][0, 2 * F:2 * F + E_DIM])).then_inc(consts, 16)
                sp.wait_ge(packed, 2)
                sp.dma_start(self.rec_by_dst.rearrange("(g p j) c -> p g (j c)", p=P, j=J),
                             rec[:, :, :, :].rearrange("p g j c -> p g (j c)")).then_inc(stored, 16)
                sp.wait_ge(loaded, 16 * n_loads)
                sp.dma_start(self.key_row.rearrange("(g p j) -> p g j", p=P, j=J), ids[:, 1, :, :]).then_inc(stored, 16)
                with sp.Fori(0, (NG - 2) // 2) as i:
                    for q in range(2):
                        sp.wait_ge(attr_free, i * 2 + (q + 1))
                        sp.dma_start(at[:, q, :, :].rearrange("p j d -> p (j d)"),
                                     attr_full[bass.ds(i * 2 + q, 1), :, :].rearrange("g p x -> (g p) x")
                                     ).then_inc(attr_in[q], 16)
                sp.wait_ge(attr_free, NG - 1)
                sp.dma_start(at[:, 0, :, :].rearrange("p j d -> p (j d)"), attr_full[NG - 2, :, :]).then_inc(attr_in[0], 16)
                sp.wait_ge(attr_free, NG)
                sp.wait_ge(padded, 2)
                sp.dma_start(at[0:whole, 1, :, :],
                             attr[first:first + whole * J, :].rearrange("(p j) d -> p j d", j=J)).then_inc(attr_in[1], 16)
                if rest:
                    sp.dma_start(at[whole:whole + 1, 1, 0:rest, :],
                                 attr[first + whole * J:N_EDGES, :].rearrange("(p j) d -> p j d", p=1)
                                 ).then_inc(attr_in[1], 16)
                sp.wait_ge(stored, 32)

            @block.vector
            def _(dve):
                dve.memset(ids[:, :, NG - 1, :], PAD_NODE).then_inc(padded, 1)
                dve.sem_inc(attr_free, 2)
                dve.wait_ge(loaded, 16 * n_loads)
                for w in range(2):
                    dve.tensor_copy(rec[:, :, :, w], ids[:, w, :, :]).then_inc(packed, 1)
                step = Chain(dve, steps)
                step(dve.tensor_scalar(tile_i[:, :], ids[:, 0, :, :].rearrange("p g j -> p (g j)"),
                                       P.bit_length() - 1, None, ALU.logical_shift_right))
                step(dve.tensor_copy(tile_f[:, :], tile_i[:, :]))
                step(dve.memset(ones_s[:, :], 1.0))
                step(dve.memset(place_f[:, :], 0.0))
                with dve.Fori(0, NT) as b:
                    dve.tensor_scalar(is_b[:, :], tile_f[:, :], self.tile_no[:, bass.ds(b, 1)], 0.0,
                                      ALU.is_equal, ALU.add, accum_out=counts[:, bass.ds(b, 1)]).then_inc(tile_steps, 1)
                    dve.wait_ge(tile_steps, b + 1)
                dve.wait_ge(summed, 1)
                step(dve.tensor_copy(total[:, :], pc[:, 1, 0:NT]))
                step(dve.tensor_tensor_scan(upto[:, :], ones_s[:, 0:NT], total[:, :], 0.0, ALU.mult, ALU.add))
                step(dve.tensor_tensor(start[:, :], upto[:, :], total[:, :], ALU.subtract))
                step(dve.tensor_tensor(start[:, :], start[:, :], pc[:, 0, 0:NT], ALU.add))
                step(dve.tensor_scalar(start[:, :], start[:, :], 1.0, None, ALU.subtract))
                with dve.Fori(0, NT) as b:
                    tstep = Chain(dve, tile_steps, b * 4 + NT)
                    tile_no = self.tile_no[:, bass.ds(b, 1)]
                    tstep(dve.tensor_scalar(is_b[:, :], tile_f[:, :], tile_no, None, ALU.is_equal))
                    tstep(dve.tensor_tensor_scan(run[:, :], ones_s[:, :], is_b[:, :], start[:, bass.ds(b, 1)],
                                                 ALU.mult, ALU.add))
                    tstep(dve.tensor_tensor(here[:, :], is_b[:, :], run[:, :], ALU.mult))
                    tstep(dve.tensor_tensor(place_f[:, :], place_f[:, :], here[:, :], ALU.add))
                step(dve.tensor_copy(place[:, :], place_f[:, :]))
                dve.wait_ge(consts, 16)

                def logits(g, q, wait, base):
                    dve.wait_ge(attr_in[q], wait)
                    astep = Chain(dve, attr_steps, base)
                    astep(dve.tensor_tensor(prod[:, :, :], at[:, q, :, :],
                                            a_e[:, None, :].to_broadcast([P, J, E_DIM]), ALU.mult))
                    dve.sem_inc(attr_free, 1)
                    astep(dve.tensor_reduce(logit_e[:, bass.ds(g, 1), :].rearrange("p g j -> p (g j)"),
                                            prod[:, :, :], AX.X, ALU.add))

                with dve.Fori(0, (NG - 2) // 2) as i:
                    for q in range(2):
                        logits(i * 2 + q, q, i * 16 + 16, (i * 2 + q) * 2)
                logits(NG - 2, 0, 16 * (NG // 2), 2 * (NG - 2))
                dve.memset(at[:, 1, :, :], 0.0).then_inc(padded, 1)
                logits(NG - 1, 1, 16 * ((NG - 2) // 2 + (2 if rest else 1)), 2 * (NG - 1))

            @block.tensor
            def _(pe):
                pe.wait_ge(tile_steps, NT)
                nc.tensor.matmul(pc[:, 0, 0:NT], self.before[:, :], counts[:, :], start=True, stop=True)
                nc.tensor.matmul(pc[:, 1, 0:NT], self.ones[:, :], counts[:, :], start=True, stop=True).then_inc(summed, 1)

    def ranges(self, order):
        nc = self.nc
        rec_dram = (self.rec_by_dst, self.rec_by_src)[order]
        with ExitStack() as c:
            def sb(name, shape, dt):
                return c.enter_context(nc.sbuf_tensor(f"{name}{order}", shape, dt))

            def sem(name):
                return self.sem(c, f"{name}{order}")

            rec = sb("rg_rec", [P, NG, J, 2], I32)
            key = sb("rg_key", [P, NG, J], FP32)
            ext = sb("rg_ext", [P, 2, NG], FP32)
            ext_i = sb("rg_exti", [1, 2, NG], I32)
            ext_t = sb("rg_extt", [NG, 2], FP32)
            pT = c.enter_context(nc.psum_tensor(f"rg_pT{order}", [P, 2, P], FP32))
            pR = c.enter_context(nc.psum_tensor(f"rg_pR{order}", [1, 2, P], FP32))
            got, steps, turned, found = sem("rg_got"), sem("rg_steps"), sem("rg_turned"), sem("rg_found")
            block = c.enter_context(nc.Block())

            @block.sync
            def _(sp):
                sp.dma_start(rec[:, :, :, :].rearrange("p g j c -> p g (j c)"),
                             rec_dram.rearrange("(g p j) c -> p g (j c)", p=P, j=J)).then_inc(got, 16)

            @block.vector
            def _(dve):
                step = Chain(dve, steps)
                dve.wait_ge(got, 16)
                step(dve.tensor_copy(key[:, :, :], rec[:, :, :, 1 - order]))
                step(dve.tensor_reduce(ext[:, 0, :], key[:, :, :], AX.X, ALU.min))
                step(dve.tensor_reduce(ext[:, 1, :], key[:, :, :], AX.X, ALU.max))
                dve.wait_ge(turned, 1)
                step(dve.tensor_reduce(ext_t[:, 0:1], pT[0:NG, 0, :], AX.X, ALU.min))
                step(dve.tensor_reduce(ext_t[:, 1:2], pT[0:NG, 1, :], AX.X, ALU.max))
                step(dve.tensor_scalar(ext_t[:, 1:2], ext_t[:, 1:2], float(P), None, ALU.add))
                dve.wait_ge(turned, 2)
                step(dve.tensor_copy(ext_i[:, :, :], pR[:, :, 0:NG]))
                shift = P.bit_length() - 1
                dve.tensor_scalar(self.bounds[0:1, order, :, :], ext_i[:, :, :], shift, None,
                                  ALU.logical_shift_right).then_inc(found, 1)
                dve.wait_ge(found, 1)

            @block.tensor
            def _(pe):
                pe.wait_ge(steps, 3)
                nc.tensor.transpose(pT[0:NG, 0, :], ext[:, 0, :], self.ident[:, :])
                nc.tensor.transpose(pT[0:NG, 1, :], ext[:, 1, :], self.ident[:, :]).then_inc(turned, 1)
                pe.wait_ge(steps, 6)
                nc.tensor.transpose(pR[:, 0, 0:NG], ext_t[:, 0:1], self.ident[0:NG, 0:NG])
                nc.tensor.transpose(pR[:, 1, 0:NG], ext_t[:, 1:2], self.ident[0:NG, 0:NG]).then_inc(turned, 1)

    def tiles_of_group(self, eng, order, g):
        return (eng.value_load(self.bounds[0:1, order, 0, bass.ds(g, 1)], min_val=0, max_val=NT - 1),
                eng.value_load(self.bounds[0:1, order, 1, bass.ds(g, 1)], min_val=1, max_val=NT))

    def aggregate(self, name, order, table, width, acc, at, zero, count=None):
        nc = self.nc
        rec_dram = (self.rec_by_dst, self.rec_by_src)[order]
        recs = rec_dram.rearrange("(g p j) c -> g p (j c)", p=P, j=J)
        R, GS = 4, 2
        SL, LAG = 4, 2
        tw = table.shape[1]
        with ExitStack() as c:
            def sb(nm, shape, dt):
                return c.enter_context(nc.sbuf_tensor(f"{name}_{nm}", shape, dt))

            def sem(nm):
                return self.sem(c, f"{name}_{nm}")

            rec = sb("rec", [P, R, J, 2], I32)
            rows = sb("rows", [P, GS, J, tw], BF16)
            krel = sb("krel", [P, J], FP32)
            hot = sb("hot", [P, SL * J, P], BF16)
            one = sb("one", [P, 1], BF16)
            sums = c.enter_context(nc.psum_tensor(f"{name}_sums", [P, SL * 512], FP32))
            if count is not None:
                members = c.enter_context(nc.psum_tensor(f"{name}_members", [P, SL * 512], FP32))
            rec_in = [sem(f"rec_in{s}") for s in range(R)]
            rows_in = [[sem(f"rows_in{s}_{j}") for j in range(J)] for s in range(GS)]
            rows_free = sem("rows_free")
            rec_free, rec_used = sem("rec_free"), sem("rec_used")
            pool_turns = sem("pool_turns")
            hot_ready, sums_ready, steps, zeroed, added = sem("hot_ready"), sem("sums_ready"), sem("steps"), sem("zeroed"), sem("added")
            block = c.enter_context(nc.Block())
            n_zeroed = 2 + (1 if zero else 0) + (2 if count is not None else 0)

            @block.sync
            def _(sp):
                with sp.Fori(0, NG // R) as i:
                    for s in range(R):
                        sp.wait_ge(rec_free, i * R + (s + 1))
                        sp.wait_ge(rec_used, i * R + (s + 1))
                        sp.dma_start(rec[:, s, :, :].rearrange("p j c -> p (j c)"),
                                     recs[bass.ds(i * R + s, 1), :, :].rearrange("g p x -> (g p) x")).then_inc(rec_in[s], 16)

            @block.gpsimd
            def _(pool):
                with pool.Fori(0, NG // R) as i:
                    for s in range(R):
                        q = s % GS
                        pool.wait_ge(rec_in[s], i * 16 + 16)
                        pool.wait_ge(rows_free, i * R + (s + 1))
                        pool.sem_inc(pool_turns, 1)
                        for j in range(J):
                            pool.indirect_dma_start(
                                out=rows[:, q, j, :], out_offset=None, in_=table,
                                in_offset=bass.IndirectOffsetOnAxis(ap=rec[:, s, j, order:order + 1], axis=0),
                            ).then_inc(rows_in[q][j], 16)

            @block.vector
            def _(dve):
                dve.memset(one[:, :], 1.0).then_inc(zeroed, 1)
                dve.memset(sums[:, (SL - LAG) * 512:SL * 512], 0.0).then_inc(zeroed, 1)
                if zero:
                    dve.memset(acc[:, :, at:at + width], 0.0).then_inc(zeroed, 1)
                if count is not None:
                    dve.memset(members[:, (SL - LAG) * 512:SL * 512], 0.0).then_inc(zeroed, 1)
                    dve.memset(count[:, :], 0.0).then_inc(zeroed, 1)
                dve.wait_ge(zeroed, n_zeroed)
                dve.sem_inc(rec_free, R)
                dve.sem_inc(added, LAG)
                dve.sem_inc(hot_ready, 1)
                npair = dve.alloc_register(f"{name}_dve_pairs")
                slot = dve.alloc_register(f"{name}_dve_slot")
                old_slot = dve.alloc_register(f"{name}_dve_old_slot")
                tiles = [dve.alloc_register(f"{name}_dve_tile{k}") for k in range(LAG)]
                dve.reg_mov(npair, 0)
                dve.reg_mov(slot, 0)
                dve.reg_mov(old_slot, SL - LAG)
                for r in tiles:
                    dve.reg_mov(r, 0)

                def add_old(n, sl, b):
                    cell = acc[:, bass.ds(b, 1), at:at + width].rearrange("p a w -> p (a w)")
                    dve.wait_ge(added, n + LAG)
                    if count is not None:
                        many = count[:, bass.ds(b, 1)]
                        dve.tensor_tensor(many, many, members[:, bass.ds(sl * 512, 1)], ALU.add).then_inc(steps, 1)
                    dve.tensor_tensor(cell, cell, sums[:, bass.ds(sl * 512, width)], ALU.add).then_inc(added, 1)

                K = 2 if count is not None else 1
                with dve.Fori(0, NG // R) as i:
                    for s in range(R):
                        dve.wait_ge(rec_in[s], i * 16 + 16)
                        lo, hi = self.tiles_of_group(dve, order, i * R + s)
                        with dve.Fori(lo, hi) as b:
                            n = dve.snap(npair)
                            sl = dve.snap(slot, min_val=0, max_val=SL - 1)
                            old = dve.snap(old_slot, min_val=0, max_val=SL - 1)
                            b_old = dve.snap(tiles[0], min_val=0, max_val=NT - 1)
                            dve.wait_ge(hot_ready, n + 1)
                            dve.tensor_scalar(krel[:, :], rec[:, s, :, 1 - order], self.neg_base[:, bass.ds(b, 1)],
                                              None, ALU.add).then_inc(steps, 1)
                            dve.wait_ge(steps, n * K + 1)
                            dve.tensor_tensor(hot[:, bass.ds(sl * J, J), :], self.col[:, None, :].to_broadcast([P, J, P]),
                                              krel[:, :, None].to_broadcast([P, J, P]), ALU.is_equal).then_inc(hot_ready, 1)
                            dve.wait_ge(sums_ready, n + 1)
                            add_old(n, old, b_old)
                            for r, newer in zip(tiles, tiles[1:]):
                                dve.reg_mov(r, newer)
                            dve.reg_mov(tiles[-1], b)
                            dve.reg_add(npair, npair, 1)
                            dve.reg_alu(slot, npair, SL - 1, ALU.bitwise_and)
                            dve.reg_add(old_slot, npair, SL - LAG)
                            dve.reg_alu(old_slot, old_slot, SL - 1, ALU.bitwise_and)
                        dve.sem_inc(rec_free, 1)
                for r in tiles:
                    n = dve.snap(npair)
                    old = dve.snap(old_slot, min_val=0, max_val=SL - 1)
                    b_old = dve.snap(r, min_val=0, max_val=NT - 1)
                    dve.wait_ge(sums_ready, n + 1)
                    if count is not None:
                        dve.sem_inc(steps, 1)
                    add_old(n, old, b_old)
                    dve.reg_add(npair, npair, 1)
                    dve.reg_add(old_slot, npair, SL - LAG)
                    dve.reg_alu(old_slot, old_slot, SL - 1, ALU.bitwise_and)
                n = dve.snap(npair)
                dve.wait_ge(added, n + LAG)
                if count is not None:
                    dve.wait_ge(steps, n * K)
                dve.sem_inc(rec_free, 1)

            @block.tensor
            def _(pe):
                pe.wait_ge(zeroed, n_zeroed)
                pe.sem_inc(rows_free, GS)
                pe.sem_inc(rec_used, R)
                pe.sem_inc(sums_ready, LAG)
                npair = pe.alloc_register(f"{name}_pe_pairs")
                slot = pe.alloc_register(f"{name}_pe_slot")
                pe.reg_mov(npair, 0)
                pe.reg_mov(slot, 0)
                with pe.Fori(0, NG // R) as i:
                    for s in range(R):
                        q = s % GS
                        lo, hi = self.tiles_of_group(pe, order, i * R + s)
                        with pe.Fori(lo, hi) as b:
                            n = pe.snap(npair)
                            sl = pe.snap(slot, min_val=0, max_val=SL - 1)
                            pe.wait_ge(added, n + 1)
                            pe.wait_ge(hot_ready, n + 2)
                            out = sums[:, bass.ds(sl * 512, width)]
                            for j in range(J):
                                pe.wait_ge(rows_in[q][j], (i * (R // GS) + (s // GS + 1)) * 16)
                                hot_j = hot[:, bass.ds(sl * J + j, 1), :].rearrange("p a n -> p (a n)")
                                for part in range(3):
                                    last = nc.tensor.matmul(out, hot_j, rows[:, q, j, part * width:(part + 1) * width],
                                                            start=(j == 0 and part == 0), stop=(j == J - 1 and part == 2))
                                if count is not None:
                                    last = nc.tensor.matmul(members[:, bass.ds(sl * 512, 1)], hot_j, one[:, :],
                                                            start=(j == 0), stop=(j == J - 1))
                            last.then_inc(sums_ready, 1)
                            pe.reg_add(npair, npair, 1)
                            pe.reg_alu(slot, npair, SL - 1, ALU.bitwise_and)
                        pe.wait_ge(sums_ready, pe.snap(npair) + LAG)
                        pe.sem_inc(rows_free, 1)
                        pe.sem_inc(rec_used, 1)

    def attention(self, acc, a_dst, degree):
        nc = self.nc
        table, rec_all, place, logit_e = self.tab_z, self.rec, self.place, self.logit_e
        recs = self.rec_by_dst.rearrange("(g p j) c -> g p (j c)", p=P, j=J)
        R, GS = 4, 2
        with ExitStack() as c:
            def sb(nm, shape, dt):
                return c.enter_context(nc.sbuf_tensor(f"at_{nm}", shape, dt))

            def ps(nm, shape):
                return c.enter_context(nc.psum_tensor(f"at_{nm}", shape, FP32))

            def sem(nm):
                return self.sem(c, f"at_{nm}")

            rec = sb("rec", [P, R, J, 2], I32)
            keys = sb("keys", [P, GS, GE], I32)
            rows = sb("rows", [P, GS, J, W0], FP32)
            moved = sb("moved", [P, GS, J, 2], I32)
            target = sb("target", [P, GS, J], I32)
            u = sb("u", [P, J], FP32)
            pen = sb("pen", [P, J, P], FP32)
            logit = sb("logit", [P, J, P], FP32)
            shifted = sb("shifted", [P, J, P], FP32)
            leaky = sb("leaky", [P, J, P], FP32)
            w = sb("w", [P, J, P], FP32)
            w_e = sb("w_e", [P, J, P], FP32)
            enters = sb("enters", [P, J, P], BF16)
            umax = sb("umax", [P, NT], FP32)
            mrun = sb("mrun", [P, NT], FP32)
            tmax = sb("tmax", [P, 1], FP32)
            lin = sb("lin", [P, 1], FP32)
            mnew = sb("mnew", [P, 1], FP32)
            mneg = sb("mneg", [P, 1], FP32)
            fell = sb("fell", [P, 1], FP32)
            keep = sb("keep", [P, 1], FP32)
            keep_old = sb("keep_old", [P, 1], FP32)
            wsum = sb("wsum", [P, 1], FP32)
            joined = sb("joined", [P, 1], FP32)
            u_on_nodes = ps("u_on_nodes", [P, J, P])
            w_turned = ps("w_turned", [P, J, P])
            sums = ps("sums", [P, 2 * 512])
            rec_in = [sem(f"rec_in{s}") for s in range(R)]
            rows_in = [sem(f"rows_in{s}") for s in range(GS)]
            keys_in = [sem(f"keys_in{s}") for s in range(GS)]
            sent = [sem(f"sent{s}") for s in range(GS)]
            rec_free, rows_free, keys_free = sem("rec_free"), sem("rows_free"), sem("keys_free")
            copied, zeroed, steps, u_ready, ub_ready = sem("copied"), sem("zeroed"), sem("steps"), sem("u_ready"), sem("ub_ready")
            pen_ready, logit_ready, m_ready, fell_ready = sem("pen_ready"), sem("logit_ready"), sem("m_ready"), sem("fell_ready")
            shifted_ready, leaky_ready, w_ready, keep_ready, counted = sem("shifted_ready"), sem("leaky_ready"), sem("w_ready"), sem("keep_ready"), sem("counted")
            turned, w_e_ready, sums_ready, added = sem("turned"), sem("w_e_ready"), sem("sums_ready"), sem("added")
            pool_turns, dve_turns = sem("pool_turns"), sem("dve_turns")
            block = c.enter_context(nc.Block())
            K = 7

            def limits(eng, g):
                return self.tiles_of_group(eng, 0, g)

            @block.sync
            def _(sp):
                with sp.Fori(0, NG // R) as i:
                    for s in range(R):
                        q = s % GS
                        sp.wait_ge(rec_free, i * R + (s + 1))
                        sp.dma_start(rec[:, s, :, :].rearrange("p j c -> p (j c)"),
                                     recs[bass.ds(i * R + s, 1), :, :].rearrange("g p x -> (g p) x")).then_inc(rec_in[s], 16)
                        sp.wait_ge(keys_free, i * R + (s + 1))
                        sp.dma_start(keys[:, q, :],
                                     self.key_row.rearrange("(g e) -> g e", e=GE)[bass.ds(i * R + s, 1), :]
                                     .to_broadcast([P, GE])).then_inc(keys_in[q], 16)

            @block.gpsimd
            def _(pool):
                def scatter(g, q, reused):
                    if reused is not None:
                        pool.wait_ge(sent[q], reused)
                    pool.tensor_copy(moved[:, q, :, :], rec_all[:, bass.ds(g, 1), :, :].rearrange("p g j c -> p (g j) c")
                                     ).then_inc(copied, 1)
                    pool.tensor_copy(target[:, q, :], place[:, bass.ds(g * J, J)]).then_inc(copied, 1)
                    pool.wait_ge(copied, g * 2 + 2)
                    pool.sem_inc(pool_turns, 1)
                    for j in range(J):
                        pool.indirect_dma_start(
                            out=self.rec_by_src, in_=moved[:, q, j, :], in_offset=None,
                            out_offset=bass.IndirectOffsetOnAxis(ap=target[:, q, j:j + 1], axis=0),
                        ).then_inc(sent[q], 16)

                def gather(g, s, q, rec_at):
                    pool.wait_ge(rec_in[s], rec_at)
                    pool.wait_ge(rows_free, g + 1)
                    pool.sem_inc(pool_turns, 1)
                    for j in range(J):
                        pool.indirect_dma_start(
                            out=rows[:, q, j, :], out_offset=None, in_=table,
                            in_offset=bass.IndirectOffsetOnAxis(ap=rec[:, s, j, 0:1], axis=0),
                        ).then_inc(rows_in[q], 16)

                for s in range(R):
                    gather(s, s, s % GS, 16)
                    scatter(s, s % GS, None if s < GS else 16 * J * (s // GS))
                with pool.Fori(1, NG // R) as i:
                    for s in range(R):
                        gather(i * R + s, s, s % GS, i * 16 + 16)
                        scatter(i * R + s, s % GS, (i * (R // GS) + s // GS) * (16 * J))
                for q in range(GS):
                    pool.wait_ge(sent[q], 16 * J * (NG // GS))

            @block.vector
            def _(dve):
                dve.memset(acc[:, :, :], 0.0).then_inc(zeroed, 1)
                dve.memset(umax[:, :], -BIG).then_inc(zeroed, 1)
                dve.memset(mrun[:, :], -BIG).then_inc(zeroed, 1)
                dve.memset(degree[:, :], 0.0).then_inc(zeroed, 1)
                dve.memset(sums[:, 512:1024], 0.0).then_inc(zeroed, 1)
                dve.memset(keep_old[:, :], 1.0).then_inc(zeroed, 1)
                dve.wait_ge(zeroed, 6)
                dve.sem_inc(rec_free, R)
                dve.sem_inc(keys_free, GS)
                dve.sem_inc(logit_ready, 1)
                dve.sem_inc(leaky_ready, 1)
                dve.sem_inc(added, 1)
                npair = dve.alloc_register("at_dve_pairs")
                slot = dve.alloc_register("at_dve_slot")
                last_b = dve.alloc_register("at_dve_tile")
                dve.reg_mov(npair, 0)
                dve.reg_mov(slot, 0)
                dve.reg_mov(last_b, 0)

                def add_last(sl, b):
                    cell = acc[:, bass.ds(b, 1), 0:F].rearrange("p a w -> p (a w)")
                    return dve.scalar_tensor_tensor(cell, cell, keep_old[:, :], sums[:, bass.ds((1 - sl) * 512, F)],
                                                    ALU.mult, ALU.add)

                with dve.Fori(0, NG // R) as i:
                    for s in range(R):
                        q = s % GS
                        g = i * R + s
                        dve.wait_ge(rec_in[s], i * 16 + 16)
                        dve.wait_ge(rows_in[q], (i * (R // GS) + (s // GS + 1)) * (16 * J))
                        dve.tensor_tensor(u[:, :], rows[:, q, :, C_SRC],
                                          logit_e[:, bass.ds(g, 1), :].rearrange("p g j -> p (g j)"), ALU.add).then_inc(u_ready, 1)
                        dve.wait_ge(u_ready, g + 1)
                        dve.wait_ge(keys_in[q], (i * (R // GS) + (s // GS + 1)) * 16)
                        lo, hi = limits(dve, g)
                        with dve.Fori(lo, hi) as b:
                            n = dve.snap(npair)
                            sl = dve.snap(slot, min_val=0, max_val=1)
                            b_last = dve.snap(last_b, min_val=0, max_val=NT - 1)
                            step = Chain(dve, steps, n * K)
                            at_b = bass.ds(b, 1)
                            dve.wait_ge(counted, n + 1)
                            dve.wait_ge(logit_ready, n + 1)
                            dve.tensor_scalar(pen[:, :, :], keys[:, q, :].rearrange("p (e j) -> p j e", j=J),
                                              self.node_id[:, at_b], -BIG, ALU.not_equal, ALU.mult).then_inc(pen_ready, 1)
                            dve.wait_ge(pen_ready, n + 1)
                            dve.wait_ge(ub_ready, g + 1)
                            dve.wait_ge(shifted_ready, n + 1)
                            dve.sem_inc(dve_turns, 1)
                            dve.tensor_tensor_reduce(out=logit[:, :, :], in0=u_on_nodes[:, :, :], in1=pen[:, :, :], scale=1.0,
                                                     scalar=-BIG, op0=ALU.add, op1=ALU.max,
                                                     accum_out=tmax[:, :]).then_inc(logit_ready, 1)
                            dve.wait_ge(logit_ready, n + 2)
                            step(dve.tensor_tensor(umax[:, at_b], umax[:, at_b], tmax[:, :], ALU.max))
                            step(dve.tensor_tensor(lin[:, :], umax[:, at_b], a_dst[:, at_b], ALU.add))
                            step(dve.scalar_tensor_tensor(mnew[:, :], lin[:, :], ALPHA, lin[:, :], ALU.mult, ALU.max))
                            dve.tensor_scalar(mneg[:, :], mnew[:, :], -1.0, None, ALU.mult).then_inc(m_ready, 1)
                            dve.tensor_tensor(fell[:, :], mrun[:, at_b], mnew[:, :], ALU.subtract).then_inc(fell_ready, 1)
                            dve.wait_ge(fell_ready, n + 1)
                            step(copy(dve, mrun[:, at_b], mnew[:, :]))
                            dve.wait_ge(w_ready, n + 1)
                            dve.wait_ge(shifted_ready, n + 2)
                            dve.scalar_tensor_tensor(leaky[:, :, :], shifted[:, :, :], ALPHA, shifted[:, :, :],
                                                     ALU.mult, ALU.max).then_inc(leaky_ready, 1)
                            dve.wait_ge(sums_ready, n + 1)
                            add_last(sl, b_last).then_inc(added, 1)
                            for half in range(2):
                                dve.wait_ge(turned, n * 2 + half + 1)
                                js = slice(half * J // 2, (half + 1) * J // 2)
                                dve.tensor_copy(w_e[:, js, :], w_turned[:, js, :]).then_inc(w_e_ready, 1)
                            dve.wait_ge(keep_ready, n + 1)
                            den = acc[:, at_b, F:F + 1].rearrange("p a w -> p (a w)")
                            step(dve.scalar_tensor_tensor(den, den, keep[:, :], wsum[:, :], ALU.mult, ALU.add))
                            dve.wait_ge(added, n + 2)
                            step(dve.tensor_scalar(keep_old[:, :], keep[:, :], 1.0, None, ALU.mult))
                            dve.wait_ge(counted, n + 2)
                            step(dve.tensor_tensor(degree[:, at_b], degree[:, at_b], joined[:, :], ALU.add))
                            assert step.n == K
                            dve.reg_mov(last_b, b)
                            dve.reg_add(npair, npair, 1)
                            dve.reg_sub(slot, 1, slot)
                        dve.sem_inc(rec_free, 1)
                        dve.sem_inc(keys_free, 1)
                n = dve.snap(npair)
                sl = dve.snap(slot, min_val=0, max_val=1)
                b_last = dve.snap(last_b, min_val=0, max_val=NT - 1)
                dve.wait_ge(sums_ready, n + 1)
                add_last(sl, b_last).then_inc(added, 1)
                dve.wait_ge(added, n + 2)
                dve.sem_inc(dve_turns, 1)

            @block.scalar
            def _(act):
                act.sem_inc(shifted_ready, 1)
                act.sem_inc(w_ready, 1)
                act.sem_inc(counted, 1)
                npair = act.alloc_register("at_act_pairs")
                act.reg_mov(npair, 0)
                with act.Fori(0, NG) as g:
                    lo, hi = limits(act, g)
                    with act.Fori(lo, hi) as b:
                        n = act.snap(npair)
                        act.wait_ge(logit_ready, n + 2)
                        act.wait_ge(leaky_ready, n + 1)
                        act.activation(shifted[:, :, :], logit[:, :, :], ACT.Identity, bias=a_dst[:, bass.ds(b, 1)],
                                       scale=1.0).then_inc(shifted_ready, 1)
                        act.wait_ge(leaky_ready, n + 2)
                        act.wait_ge(m_ready, n + 1)
                        act.activation(w[:, :, :], leaky[:, :, :], ACT.Exp, bias=mneg[:, :], scale=1.0,
                                       accum_out=wsum[:, :]).then_inc(w_ready, 1)
                        act.wait_ge(fell_ready, n + 1)
                        act.activation(keep[:, :], fell[:, :], ACT.Exp).then_inc(keep_ready, 1)
                        act.wait_ge(pen_ready, n + 1)
                        act.activation(enters[:, :, :], pen[:, :, :], ACT.Identity, bias=1.0, scale=1.0 / BIG,
                                       accum_out=joined[:, :]).then_inc(counted, 1)
                        act.reg_add(npair, npair, 1)

            @block.tensor
            def _(pe):
                pe.wait_ge(zeroed, 6)
                pe.sem_inc(rows_free, GS)
                pe.sem_inc(sums_ready, 1)
                npair = pe.alloc_register("at_pe_pairs")
                slot = pe.alloc_register("at_pe_slot")
                pe.reg_mov(npair, 0)
                pe.reg_mov(slot, 0)
                with pe.Fori(0, NG // R) as i:
                    for s in range(R):
                        q = s % GS
                        g = i * R + s
                        lo, hi = limits(pe, g)
                        pe.wait_ge(rows_in[q], (i * (R // GS) + (s // GS + 1)) * (16 * J))
                        pe.wait_ge(u_ready, g + 1)
                        for j in range(J):
                            last = nc.tensor.transpose(u_on_nodes[:, j, :], u[:, j:j + 1].to_broadcast([P, P]), self.ident[:, :])
                        last.then_inc(ub_ready, 1)
                        with pe.Fori(lo, hi) as b:
                            n = pe.snap(npair)
                            sl = pe.snap(slot, min_val=0, max_val=1)
                            pe.wait_ge(w_ready, n + 2)
                            for j in range(J):
                                last = nc.tensor.transpose(w_turned[:, j, :], w[:, j, :], self.ident[:, :])
                                if j % (J // 2) == J // 2 - 1:
                                    last.then_inc(turned, 1)
                            pe.wait_ge(added, n + 1)
                            for j in range(J):
                                if j % (J // 2) == 0:
                                    pe.wait_ge(w_e_ready, n * 2 + (j // (J // 2) + 1))
                                last = nc.tensor.matmul(sums[:, bass.ds(sl * 512, F)], w_e[:, j, :], rows[:, q, j, 0:F],
                                                        start=(j == 0), stop=(j == J - 1))
                            last.then_inc(sums_ready, 1)
                            pe.reg_add(npair, npair, 1)
                            pe.reg_sub(slot, 1, slot)
                        pe.wait_ge(sums_ready, pe.snap(npair) + 1)
                        pe.sem_inc(rows_free, 1)

    def product(self, name, terms, vectors, finish, finish_steps, prepare=None, prepare_steps=0, bufs=(), stores=()):
        nc = self.nc
        nk = len(terms)
        with ExitStack() as c:
            def sb(nm, shape, dt):
                return c.enter_context(nc.sbuf_tensor(f"{name}_{nm}", shape, dt))

            def sem(nm):
                return self.sem(c, f"{name}_{nm}")

            xin = sb("xin", [P, 2, nk, F], FP32)
            xT = sb("xT", [P, 2, 2 * nk, P], FP32)
            weights, vecs, loads = [], [], []
            for k, (_, w) in enumerate(terms):
                if w.shape[0] == F:
                    weights.append(sb(f"w{k}", [P, 2, F], FP32))
                    loads.append((weights[k][:, :, :], w.rearrange("(c k) n -> k c n", k=P)))
                else:
                    weights.append(w)
            for k, v in enumerate(vectors):
                vecs.append(sb(f"v{k}", [P, v.shape[0]], FP32))
                loads.append((vecs[k][:, :], row_on_all(v)))
            buf = {nm: sb(nm, [P, 2] + shape, dt) for nm, shape, dt in bufs}
            pT = c.enter_context(nc.psum_tensor(f"{name}_pT", [P, 2, 4, P], FP32))
            pY = c.enter_context(nc.psum_tensor(f"{name}_pY", [P, 2, 512], FP32))
            loaded, prepared, fetched, turned, xT_ready = sem("loaded"), sem("prepared"), sem("fetched"), sem("turned"), sem("xT_ready")
            y_ready, finished, psteps, fsteps = sem("y_ready"), sem("finished"), sem("psteps"), sem("fsteps")
            stored = [sem(f"stored{s}") for s in range(2)]
            block = c.enter_context(nc.Block())

            def over_tiles(eng, body):
                body(0, 0, None)
                body(1, 1, None)
                with eng.Fori(1, NT // 2 - 1) as i:
                    for s in range(2):
                        body(i * 2 + s, s, i)
                for t in range((NT // 2 - 1) * 2, NT):
                    body(t, t % 2, t // 2)

            @block.sync
            def _(sp):
                for dst, src in loads:
                    sp.dma_start(dst, src).then_inc(loaded, 16)

                def body(t, s, used):
                    sp.wait_ge(finished, t + 1)
                    for rows, part in stores:
                        sp.dma_start(rows.rearrange("(b p) f -> b p f", p=P)[bass.ds(t, 1), :, :]
                                     .rearrange("b p f -> (b p) f"), part(buf, s)).then_inc(stored[s], 16)
                if stores:
                    over_tiles(sp, body)
                    for s in range(2):
                        sp.wait_ge(stored[s], 16 * len(stores) * ((NT + 1 - s) // 2))

            @block.vector
            def _(dve):
                def prep(t):
                    step = Chain(dve, psteps, t * prepare_steps)
                    prepare(dve, step, t)
                    assert step.n == prepare_steps
                    dve.sem_inc(prepared, 1)

                def body(t, s, used):
                    if prepare and not is_int(t, NT - 2):
                        prep(t + 2)
                    dve.wait_ge(y_ready, t + 1)
                    if stores and used is not None:
                        dve.wait_ge(stored[s], used * (16 * len(stores)))
                    step = Chain(dve, fsteps, t * finish_steps)
                    finish(dve, step, t, pY[:, s, 0:F], {nm: b[:, s] for nm, b in buf.items()}, vecs)
                    assert step.n == finish_steps
                    dve.sem_inc(finished, 1)

                dve.wait_ge(loaded, 16 * len(loads))
                if prepare:
                    prep(0)
                    prep(1)
                over_tiles(dve, body)

            @block.scalar
            def _(act):
                def fetch(t, s):
                    if prepare:
                        act.wait_ge(prepared, t + 1)
                    for k, (a, _) in enumerate(terms):
                        act.activation(xin[:, s, k, :], tile(a, t)[:, 0:F], ACT.Copy).then_inc(fetched, 1)

                fetch(0, 0)
                fetch(1, 1)

                def body(t, s, used):
                    act.wait_ge(turned, t + 1)
                    act.activation(xT[:, s, :, :], pT[:, s, 0:2 * nk, :], ACT.Copy).then_inc(xT_ready, 1)
                    if not is_int(t, NT - 2):
                        fetch(t + 2, s)
                over_tiles(act, body)

            @block.tensor
            def _(pe):
                def turn(t, s):
                    pe.wait_ge(fetched, (t + 1) * nk)
                    for k in range(nk):
                        for h in range(2):
                            last = nc.tensor.transpose(pT[:, s, 2 * k + h, :], xin[:, s, k, h * P:(h + 1) * P],
                                                       self.ident[:, :])
                    last.then_inc(turned, 1)

                def body(t, s, used):
                    if not is_int(t, NT - 1):
                        turn(t + 1, 1 - s)
                    pe.wait_ge(xT_ready, t + 1)
                    if used is not None:
                        pe.wait_ge(finished, t - 1)
                    for k in range(nk):
                        for h in range(2):
                            last = nc.tensor.matmul(pY[:, s, 0:F], xT[:, s, 2 * k + h, :], weights[k][:, h, :],
                                                    start=(k == 0 and h == 0), stop=(k == nk - 1 and h == 1))
                    last.then_inc(y_ready, 1)

                if loads:
                    pe.wait_ge(loaded, 16 * len(loads))
                turn(0, 0)
                over_tiles(pe, body)

    def statistics(self, name, combine, steps_of_tile, setup=None, setup_steps=0, vectors=()):
        nc = self.nc
        with ExitStack() as c:
            def sem(nm):
                return self.sem(c, f"{name}_{nm}")

            vecs = [c.enter_context(nc.sbuf_tensor(f"{name}_v{k}", [P, v.shape[0]], FP32)) for k, v in enumerate(vectors)]
            ssteps, tsteps, loaded = sem("ssteps"), sem("tsteps"), sem("loaded")
            block = c.enter_context(nc.Block())

            @block.sync
            def _(sp):
                for dst, v in zip(vecs, vectors):
                    sp.dma_start(dst[:, :], row_on_all(v)).then_inc(loaded, 16)

            @block.vector
            def _(dve):
                if vectors:
                    dve.wait_ge(loaded, 16 * len(vectors))
                step = Chain(dve, ssteps)
                if setup:
                    setup(dve, step)
                with dve.Fori(0, NT) as t:
                    step = Chain(dve, tsteps, t * (steps_of_tile + 4))
                    combine(dve, step, t, vecs)
                    self.moments(dve, step, t)
                    assert step.n == steps_of_tile + 4
        self.inverse_deviation(name)

    def moments(self, dve, step, t):
        step(copy(dve, self.xt[:, :], tile(self.x, t)))
        step(dve.bn_stats(self.bn[:, 0:6], self.xt[:, :]))
        dve.sem_inc(self.dve_turns, 1)
        step(dve.bn_aggr(self.bn[:, 6:8], self.bn[:, 0:6]))
        step(copy(dve, tile(self.moment, t), self.bn[:, 6:8]))

    def inverse_deviation(self, name):
        nc = self.nc
        with ExitStack() as c:
            added, rooted, inverted = (self.sem(c, f"{name}_{nm}") for nm in ("added", "rooted", "inverted"))
            block = c.enter_context(nc.Block())
            var = self.moment[:, :, 1]

            @block.vector
            def _(dve):
                dve.tensor_scalar(var, var, EPS, None, ALU.add).then_inc(added, 1)
                dve.wait_ge(rooted, 1)
                dve.reciprocal(var, var).then_inc(inverted, 1)
                dve.wait_ge(inverted, 1)

            @block.scalar
            def _(act):
                act.wait_ge(added, 1)
                act.activation(var, var, ACT.Sqrt).then_inc(rooted, 1)

    def normalize(self, dve, step, t):
        x = tile(self.x, t)
        step(dve.tensor_scalar(x, x, self.moment[:, bass.ds(t, 1), 0], self.moment[:, bass.ds(t, 1), 1],
                               ALU.subtract, ALU.mult))

    def split(self, dve, step, parts, v, width):
        r = self.rest[:, 0:width]
        step(copy(dve, parts[0], v))
        step(dve.tensor_tensor(r, v, parts[0], ALU.subtract))
        step(dve.tensor_copy(parts[1], r))
        step(dve.tensor_tensor(parts[2], r, parts[1], ALU.subtract))

    def load_nodes(self):
        nc = self.nc
        x, w_z, w_f, w_b = (self.ins[n] for n in ("x", "L0_gnn_W", "L2_gnn_W_f", "L2_gnn_W_b"))
        with ExitStack() as c:
            wr = c.enter_context(nc.sbuf_tensor("ln_w", [P, 4, F], FP32))
            pw = c.enter_context(nc.psum_tensor("ln_pw", [P, 4, 2, P], FP32))
            cleared, nodes_in, w_in, turned, kept = (self.sem(c, f"ln_{n}")
                                                     for n in ("cleared", "nodes_in", "w_in", "turned", "kept"))
            block = c.enter_context(nc.Block())

            @block.sync
            def _(sp):
                sp.dma_start(wr[:, 0:2, :], w_z.rearrange("(c m) k -> m c k", m=P)).then_inc(w_in, 16)
                sp.dma_start(wr[:, 2, :], w_f).then_inc(w_in, 16)
                sp.dma_start(wr[:, 3, :], w_b).then_inc(w_in, 16)
                sp.wait_ge(cleared, 1)
                sp.dma_start(self.x[:, 0:NT - 1, :], x[0:(NT - 1) * P, :].rearrange("(b p) f -> p b f", p=P)).then_inc(nodes_in, 16)
                sp.dma_start(self.x[0:LAST, NT - 1, :], x[(NT - 1) * P:N_NODES, :]).then_inc(nodes_in, 16)
                sp.wait_ge(nodes_in, 32)

            @block.vector
            def _(dve):
                dve.memset(self.x[:, NT - 1, :], 0.0).then_inc(cleared, 1)
                dve.wait_ge(turned, 1)
                for m in range(4):
                    dst = (self.w_z, self.w_fb)[m // 2]
                    dve.tensor_copy(dst[:, :, (m % 2) * P:(m % 2 + 1) * P], pw[:, m, :, :]).then_inc(kept, 1)
                dve.wait_ge(kept, 4)

            @block.tensor
            def _(pe):
                pe.wait_ge(w_in, 48)
                for m in range(4):
                    for h in range(2):
                        last = nc.tensor.transpose(pw[:, m, h, :], wr[:, m, h * P:(h + 1) * P], self.ident[:, :])
                last.then_inc(turned, 1)

    def degree_factors(self):
        nc = self.nc
        with ExitStack() as c:
            steps, rooted = (self.sem(c, f"df_{n}") for n in ("steps", "rooted"))
            safe = c.enter_context(nc.sbuf_tensor("df_safe", [P, NT], FP32))
            some = c.enter_context(nc.sbuf_tensor("df_some", [P, NT], FP32))
            block = c.enter_context(nc.Block())

            @block.vector
            def _(dve):
                step = Chain(dve, steps)
                step(dve.tensor_scalar(self.r_in[:, :], self.deg_src[:, :], 1.0, None, ALU.add))
                step(dve.tensor_scalar(self.r_out[:, :], self.deg_dst[:, :], 1.0, None, ALU.add))
                step(dve.tensor_scalar(safe[:, :], self.deg_dst[:, :], 1.0, None, ALU.max))
                step(dve.tensor_scalar(some[:, :], self.deg_dst[:, :], 0.0, None, ALU.is_gt))
                dve.wait_ge(rooted, 3)
                step(dve.reciprocal(self.r_in[:, :], self.r_in[:, :]))
                step(dve.reciprocal(self.r_out[:, :], self.r_out[:, :]))
                step(dve.reciprocal(safe[:, :], safe[:, :]))
                step(dve.tensor_tensor(self.r_dst[:, :], safe[:, :], some[:, :], ALU.mult))
                step(dve.tensor_scalar(safe[:, :], self.deg_src[:, :], 1.0, None, ALU.max))
                step(dve.reciprocal(self.mean_src[:, :], safe[:, :]))

            @block.scalar
            def _(act):
                act.wait_ge(steps, 4)
                for a in (self.r_in, self.r_out, safe):
                    act.activation(a[:, :], a[:, :], ACT.Sqrt).then_inc(rooted, 1)

    def finish_nodes(self):
        nc = self.nc
        CH = 7
        with ExitStack() as c:
            steps, stored = (self.sem(c, f"fn_{n}") for n in ("steps", "stored"))
            block = c.enter_context(nc.Block())

            @block.vector
            def _(dve):
                with dve.Fori(0, NT) as t:
                    step = Chain(dve, steps, t)
                    self.normalize(dve, step, t)

            @block.sync
            def _(sp):
                for b in range(0, NT - CH, CH):
                    sp.wait_ge(steps, b + CH)
                    sp.dma_start(self.out[b * P:(b + CH) * P, :].rearrange("(b p) f -> p b f", p=P),
                                 self.x[:, b:b + CH, :]).then_inc(stored, 16)
                b = NT - CH
                sp.wait_ge(steps, NT)
                sp.dma_start(self.out[b * P:(NT - 1) * P, :].rearrange("(b p) f -> p b f", p=P),
                             self.x[:, b:NT - 1, :]).then_inc(stored, 16)
                sp.dma_start(self.out[(NT - 1) * P:N_NODES, :], self.x[0:LAST, NT - 1, :]).then_inc(stored, 16)
                sp.wait_ge(stored, 16 * (NT // CH + 1))


def tile(a, t):
    return a[:, bass.ds(t, 1), :].rearrange("p b f -> p (b f)")


def build(nc, ins, out):
    with ExitStack() as ctx:
        k = Kernel(nc, ctx, ins, out)
        sb = k.sb
        k.x = sb("x", [P, NT, F], FP32)
        k.acc = acc = sb("acc", [P, NT, F + 1], FP32)
        k.moment = sb("moment", [P, NT, 2], FP32)
        k.bn = sb("bn", [P, 8], FP32)
        k.dve_turns = ctx.enter_context(nc.semaphore("dve_turns"))
        k.xt = sb("xt", [P, F], FP32)
        k.rest = sb("rest", [P, F], FP32)
        k.tmp = sb("tmp", [P, F], FP32)
        k.w_z = sb("w_z", [P, 2, F], FP32)
        k.w_fb = sb("w_fb", [P, 2, F], FP32)
        k.deg_src = sb("deg_src", [P, NT], FP32)
        k.deg_dst = sb("deg_dst", [P, NT], FP32)
        k.r_in = sb("r_in", [P, NT], FP32)
        k.r_out = sb("r_out", [P, NT], FP32)
        k.r_dst = sb("r_dst", [P, NT], FP32)
        k.mean_src = sb("mean_src", [P, NT], FP32)
        k.constants()
        k.load_nodes()

        with ExitStack() as c:
            def scoped(name, shape, dt):
                return c.enter_context(nc.sbuf_tensor(name, shape, dt))

            k.rec = scoped("rec_all", [P, NG, J, 2], I32)
            k.place = scoped("place", [P, S], I32)
            k.logit_e = scoped("logit_e", [P, NG, J], FP32)
            a_dst = scoped("a_dst", [P, NT], FP32)
            k.edges()
            k.ranges(0)

            def finish_z(dve, step, t, y, buf, vec):
                z = buf["row"][:, 0:F]
                step(dve.memset(buf["row"][:, F:W0], 1.0))
                step(dve.tensor_copy(z, y))
                step(dve.tensor_tensor(k.tmp[:, :], z, vec[0][:, :], ALU.mult))
                step(dve.tensor_reduce(buf["row"][:, C_SRC:C_SRC + 1], k.tmp[:, :], AX.X, ALU.add))
                step(dve.tensor_tensor(k.tmp[:, :], z, vec[1][:, :], ALU.mult))
                step(dve.tensor_reduce(a_dst[:, bass.ds(t, 1)], k.tmp[:, :], AX.X, ALU.add))

            k.product("z", [(k.x, k.w_z)], [ins["L0_gnn_A"][0, 0:F], ins["L0_gnn_A"][0, F:2 * F]], finish_z, 6,
                      bufs=[("row", [W0], FP32)], stores=[(k.tab_z, lambda b, s: b["row"][:, s, :])])
            k.attention(acc, a_dst, k.deg_dst)
        k.ranges(1)

        def softmax_setup(dve, step):
            step(dve.tensor_scalar(acc[:, :, F], acc[:, :, F], 2.0 ** -100, None, ALU.max))
            step(dve.reciprocal(acc[:, :, F], acc[:, :, F]))

        def add_attention(dve, step, t, vec):
            x = tile(k.x, t)
            step(dve.scalar_tensor_tensor(x, tile(acc, t)[:, 0:F], acc[:, bass.ds(t, 1), F], x, ALU.mult, ALU.add))

        k.statistics("s0", add_attention, 1, softmax_setup)

        with ExitStack() as c:
            h = c.enter_context(nc.sbuf_tensor("h", [P, NT, F], FP32))
            parts = [("parts", [3, F], BF16)]

            def three(buf, width=F):
                return [buf[:, p, :] for p in range(3)]

            def row_of(b, s):
                return b["parts"][:, s, :, :].rearrange("p c f -> p (c f)")

            def finish_in(dve, step, t, y, buf, vec):
                step(dve.tensor_tensor(tile(h, t), y, vec[0][:, :], ALU.add))
                k.split(dve, step, three(buf["parts"]), tile(h, t), F)

            k.product("in", [(k.x, ins["L1_gnn_W_in"])], [ins["L1_gnn_b_in"]], finish_in, 5,
                      prepare=k.normalize, prepare_steps=1, bufs=parts, stores=[(k.tab_h[0], row_of)])

            def mean(dve, step, t):
                a = tile(acc, t)[:, 0:F]
                step(dve.tensor_scalar(a, a, k.mean_src[:, bass.ds(t, 1)], None, ALU.mult))

            def finish_layer(dve, step, t, y, buf, vec):
                step(dve.tensor_tensor(k.tmp[:, :], y, vec[0][:, :], ALU.add))
                step(dve.tensor_scalar(tile(h, t), k.tmp[:, :], 0.0, None, ALU.max))
                k.split(dve, step, three(buf["parts"]), tile(h, t), F)

            for layer in range(3):
                k.aggregate(f"h{layer}", 1, k.tab_h[layer], F, acc, 0, True, count=k.deg_src if layer == 0 else None)
                if layer == 0:
                    k.degree_factors()
                k.product(f"l{layer}", [(acc, ins["L1_gnn_W_agg"][layer]), (h, ins["L1_gnn_W_self"][layer])],
                          [ins["L1_gnn_b_hid"][layer]], finish_layer, 6, prepare=mean, prepare_steps=1,
                          bufs=parts if layer < 2 else [("parts", [3, F], BF16)],
                          stores=[(k.tab_h[layer + 1], row_of)] if layer < 2 else [])

            def finish_out(dve, step, t, y, buf, vec):
                x = tile(k.x, t)
                step(dve.tensor_tensor(k.tmp[:, :], y, vec[0][:, :], ALU.add))
                step(dve.tensor_tensor(x, x, k.tmp[:, :], ALU.add))
                k.moments(dve, step, t)

            k.product("out", [(h, ins["L1_gnn_W_out"])], [ins["L1_gnn_b_out"]], finish_out, 6)
        k.inverse_deviation("out")

        def finish_fb(dve, step, t, y, buf, vec):
            for w, r in enumerate((k.r_out, k.r_in)):
                a = tile(acc, t)[:, w * H:(w + 1) * H]
                step(dve.tensor_scalar(a, y[:, w * H:(w + 1) * H], r[:, bass.ds(t, 1)], None, ALU.mult))
                k.split(dve, step, [buf[f"parts{w}"][:, p, :] for p in range(3)], a, H)

        k.product("fb", [(k.x, k.w_fb)], [], finish_fb, 10, prepare=k.normalize, prepare_steps=1,
                  bufs=[(f"parts{w}", [3, H], BF16) for w in range(2)],
                  stores=[(k.tab_fb[w], lambda b, s, w=w: b[f"parts{w}"][:, s, :, :].rearrange("p c f -> p (c f)"))
                          for w in range(2)])
        k.aggregate("f", 1, k.tab_fb[0], H, acc, 0, False)
        k.aggregate("b", 0, k.tab_fb[1], H, acc, H, False)

        def add_fb(dve, step, t, vec):
            x = tile(k.x, t)
            for w, r in enumerate((k.r_in, k.r_out)):
                cols = slice(w * H, (w + 1) * H)
                step(dve.scalar_tensor_tensor(k.tmp[:, cols], tile(acc, t)[:, cols], r[:, bass.ds(t, 1)], vec[0][:, cols],
                                              ALU.mult, ALU.add))
            step(dve.tensor_tensor(x, x, k.tmp[:, :], ALU.add))

        k.statistics("s2", add_fb, 3, vectors=[ins["L2_gnn_bias_param"]])

        def finish_g(dve, step, t, y, buf, vec):
            step(dve.tensor_scalar(k.tmp[:, :], y, k.r_dst[:, bass.ds(t, 1)], None, ALU.mult))
            k.split(dve, step, [buf["parts"][:, p, :] for p in range(3)], k.tmp[:, :], F)

        k.product("g", [(k.x, ins["L3_gnn_W"])], [], finish_g, 5, prepare=k.normalize, prepare_steps=1,
                  bufs=[("parts", [3, F], BF16)],
                  stores=[(k.tab_g, lambda b, s: b["parts"][:, s, :, :].rearrange("p c f -> p (c f)"))])
        k.aggregate("gg", 0, k.tab_g, F, acc, 0, True)

        def add_g(dve, step, t, vec):
            x = tile(k.x, t)
            step(dve.scalar_tensor_tensor(x, tile(acc, t)[:, 0:F], k.r_dst[:, bass.ds(t, 1)], x, ALU.mult, ALU.add))

        k.statistics("s3", add_g, 1)
        k.finish_nodes()


_INS = ['x', 'src', 'dst', 'edge_attr_64', 'L0_gnn_W', 'L0_gnn_A', 'L1_gnn_W_in', 'L1_gnn_b_in', 'L1_gnn_W_agg',
        'L1_gnn_W_self', 'L1_gnn_b_hid', 'L1_gnn_W_out', 'L1_gnn_b_out', 'L2_gnn_W_f', 'L2_gnn_W_b',
        'L2_gnn_bias_param', 'L3_gnn_W']


def kernel(**inputs):
    import numpy as _np
    import concourse.bacc as _bacc
    from concourse import mybir as _mybir
    from concourse.bass_utils import run_bass_kernel_spmd as _run

    nc = _bacc.Bacc("TRN2", target_bir_lowering=False, num_devices=1)
    arrays, args = {}, {}
    for name in _INS:
        a = _np.ascontiguousarray(inputs[name])
        arrays[f"in_{name}_dram"] = a
        args[name] = nc.dram_tensor(f"in_{name}_dram", a.shape, _mybir.dt.from_np(a.dtype), kind="ExternalInput").ap()
    out = nc.dram_tensor("out_0_dram", (6250, 256), _mybir.dt.float32, kind="ExternalOutput").ap()
    build(nc, args, out)
    r = _run(nc, [arrays], core_ids=[0])
    return r.results[0]["out_0_dram"]
```

```python
import concourse.bass as bass
from concourse import mybir
from contextlib import ExitStack

FP32 = mybir.dt.float32
I32 = mybir.dt.int32
U8 = mybir.dt.uint8
BF16 = mybir.dt.bfloat16
ALU = mybir.AluOpType
ACT = mybir.ActivationFunctionType
AX = mybir.AxisListType

P = 128
N_NODES = 6250
N_EDGES = 106250
F = 256
E_DIM = 64
NT = -(-N_NODES // P)
NPAD = NT * P
LAST = N_NODES - (NT - 1) * P
J = 8
GE = P * J
NG = -(-N_EDGES // GE)
S = NG * J
EPAD = NG * GE
TAIL = N_EDGES - (NG - 1) * GE
PAD_NODE = NPAD - 1
BIG = 2.0 ** 126
H = F // 2
W0 = F + 4
C_ONE, C_SRC = F, F + 1
EPS = 1e-5
ALPHA = 0.2


def copy(eng, out, in_):
    return eng.tensor_scalar(out, in_, 1.0, None, ALU.mult)


def row_on_all(row):
    return row.rearrange("(a n) -> a n", a=1).to_broadcast([P, row.shape[0]])


def is_int(t, least):
    return isinstance(t, int) and t >= least


class Chain:

    def __init__(self, eng, sem, base=0):
        self.eng, self.sem, self.base, self.n = eng, sem, base, 0

    def __call__(self, ins):
        self.issue(ins)
        self.wait()

    def wait(self):
        self.eng.wait_ge(self.sem, self.base + self.n)

    def issue(self, ins):
        self.n += 1
        ins.then_inc(self.sem, 1)


class Kernel:
    def __init__(self, nc, ctx, ins, out):
        self.nc, self.ctx, self.ins, self.out = nc, ctx, ins, out
        self.scopes = {}
        sb, dram = self.sb, self.dram
        self.rec_by_dst = dram("rec_by_dst", [EPAD, 2], I32)
        self.rec_by_src = dram("rec_by_src", [EPAD, 2], I32)
        self.key_row = dram("key_row", [EPAD], I32)
        self.tab_z = dram("tab_z", [NPAD, W0], FP32)
        self.tab_h = [dram(f"tab_h{k}", [NPAD, 3 * F], BF16) for k in range(3)]
        self.tab_fb = [dram(f"tab_{k}", [NPAD, 3 * H], BF16) for k in ("f", "b")]
        self.tab_g = dram("tab_g", [NPAD, 3 * F], BF16)
        self.bounds = sb("bounds", [1, 2, 2, NG], I32)
        self.ident = sb("ident", [P, P], FP32)
        self.ones = sb("ones", [P, P], FP32)
        self.before = sb("before", [P, P], FP32)
        self.col = sb("col", [P, P], FP32)
        self.node_id = sb("node_id", [P, NT], FP32)
        self.tile_no = sb("tile_no", [P, NT], FP32)
        self.neg_base = sb("neg_base", [P, NT], FP32)

    def sb(self, name, shape, dt):
        return self.ctx.enter_context(self.nc.sbuf_tensor(name, shape, dt))

    def sem(self, scope, name):
        if scope not in self.scopes:
            self.scopes[scope] = handles = []
            scope.callback(self.nc.all_engine_barrier)
            scope.callback(self.nc.clear_and_free_semaphores, handles)
        self.scopes[scope].append(self.nc.alloc_semaphore(name))
        return self.scopes[scope][-1]

    def dram(self, name, shape, dt):
        return self.nc.dram_tensor(name, shape, dt, kind="Internal").ap()

    def constants(self):
        nc = self.nc
        with ExitStack() as c:
            filled = self.sem(c, "filled")
            made = self.sem(c, "made")
            ids_made = self.sem(c, "ids_made")
            cast = self.sem(c, "cast")
            iot = c.enter_context(nc.sbuf_tensor("iot", [P, P], I32))
            iob = c.enter_context(nc.sbuf_tensor("iob", [P, NT], I32))
            ion = c.enter_context(nc.sbuf_tensor("ion", [P, NT], I32))
            block = c.enter_context(nc.Block())

            @block.gpsimd
            def _(pool):
                pool.memset(self.ident[:, :], 0.0).then_inc(filled, 1)
                pool.memset(self.ones[:, :], 1.0).then_inc(filled, 1)
                pool.memset(self.before[:, :], 1.0).then_inc(filled, 1)
                pool.iota(iot[:, :], pattern=[[1, P]], base=0, channel_multiplier=0).then_inc(ids_made, 1)
                pool.iota(iob[:, :], pattern=[[-P, NT]], base=0, channel_multiplier=0).then_inc(ids_made, 1)
                pool.iota(ion[:, :], pattern=[[P, NT]], base=0, channel_multiplier=1).then_inc(ids_made, 1)
                pool.wait_ge(filled, 3)
                pool.affine_select(out=self.ident[:, :], in_=self.ident[:, :], compare_op=ALU.not_equal, fill=1.0,
                                   base=0, pattern=[[-1, P]], channel_multiplier=1).then_inc(made, 1)
                pool.affine_select(out=self.before[:, :], in_=self.before[:, :], compare_op=ALU.is_gt, fill=0.0,
                                   base=0, pattern=[[1, P]], channel_multiplier=-1).then_inc(made, 1)
                pool.wait_ge(made, 2)

            @block.vector
            def _(dve):
                dve.wait_ge(ids_made, 3)
                dve.tensor_copy(self.col[:, :], iot[:, :]).then_inc(cast, 1)
                dve.tensor_copy(self.neg_base[:, :], iob[:, :]).then_inc(cast, 1)
                dve.tensor_copy(self.node_id[:, :], ion[:, :]).then_inc(cast, 1)
                dve.tensor_copy(self.tile_no[:, :], iot[:, 0:NT]).then_inc(cast, 1)
                dve.wait_ge(cast, 4)

    def edges(self):
        nc = self.nc
        src, dst = self.ins["src"], self.ins["dst"]
        attr = self.ins["edge_attr_64"]
        attr_full = attr[0:(NG - 1) * GE, :].rearrange("(g p j) d -> g p (j d)", p=P, j=J)
        first = (NG - 1) * GE
        whole, rest = TAIL // J, TAIL % J
        rec, place, logit_e = self.rec, self.place, self.logit_e
        ATS = 4
        U = 7
        assert (NG - 4) % ATS == 0 and J * E_DIM == 4 * P
        with ExitStack() as c:
            def sb(name, shape, dt):
                return c.enter_context(nc.sbuf_tensor(name, shape, dt))

            def sem(name):
                return self.sem(c, name)

            ids = sb("ids", [P, 2, NG, J], I32)
            tile_i = place
            tile_f = sb("tile_f", [P, S], FP32)
            is_b = sb("is_b", [P, NT, S], U8)
            run = sb("run", [P, S], FP32)
            here = sb("here", [P, 2, S], FP32)
            place_f = sb("place_f", [P, S], FP32)
            ones_s = sb("ones_s", [P, S], FP32)
            counts = sb("counts", [P, NT], FP32)
            total = sb("total", [P, NT], FP32)
            upto = sb("upto", [P, NT], FP32)
            start = sb("start", [P, NT], FP32)
            a_e = sb("a_e", [P, 2], FP32)
            at = sb("at", [P, ATS, J, E_DIM], FP32)
            at_last = sb("at_last", [P, J, E_DIM], FP32)
            at_T = sb("at_T", [P, 2, J // 2, P], FP32)
            pc = c.enter_context(nc.psum_tensor("pc", [P, 2, 256], FP32))
            p_at = c.enter_context(nc.psum_tensor("p_at", [P, 2, J // 2, P], FP32))
            p_logit = c.enter_context(nc.psum_tensor("p_logit", [P, 2, 512], FP32))
            padded, packed, stored = sem("padded"), sem("packed"), sem("stored")
            loaded, consts, summed, cleared = sem("loaded"), sem("consts"), sem("summed"), sem("cleared")
            attr_in = [sem(f"attr_in{q}") for q in range(ATS)]
            last_in, attr_free, steps, tile_steps = sem("last_in"), sem("attr_free"), sem("steps"), sem("tile_steps")
            at_T_ready, logit_ready, logit_out = sem("at_T_ready"), sem("logit_ready"), sem("logit_out")
            here_ready, placed, scanned = sem("here_ready"), sem("placed"), sem("scanned")
            block = c.enter_context(nc.Block())
            n_loads = 2 * (3 if rest else 2)

            @block.sync
            def _(sp):
                def load(g, q):
                    sp.wait_ge(attr_free, g + 1)
                    sp.dma_start(at[:, q, :, :].rearrange("p j d -> p (j d)"),
                                 attr_full[bass.ds(g, 1), :, :].rearrange("g p x -> (g p) x")).then_inc(attr_in[q], 16)

                sp.wait_ge(cleared, 3)
                for k in range(2):
                    sp.dma_start(a_e[k * E_DIM:(k + 1) * E_DIM, k:k + 1],
                                 self.ins["L0_gnn_A"][0, 2 * F:2 * F + E_DIM].rearrange("(d a) -> d a", a=1)
                                 ).then_inc(consts, 16)
                sp.wait_ge(padded, 1)
                for w, a in enumerate((src, dst)):
                    if w == 1:
                        for q in range(ATS):
                            load(q, q)
                    sp.dma_start(ids[:, w, 0:NG - 1, :],
                                 a[0:first].rearrange("(g p j) -> p g j", p=P, j=J)).then_inc(loaded, 16)
                    sp.dma_start(ids[0:whole, w, NG - 1, :],
                                 a[first:first + whole * J].rearrange("(p j) -> p j", j=J)).then_inc(loaded, 16)
                    if rest:
                        sp.dma_start(ids[whole:whole + 1, w, NG - 1, 0:rest],
                                     a[first + whole * J:N_EDGES].rearrange("(p j) -> p j", p=1)).then_inc(loaded, 16)
                sp.dma_start(at_last[0:whole, :, :],
                             attr[first:first + whole * J, :].rearrange("(p j) d -> p j d", j=J)).then_inc(last_in, 16)
                if rest:
                    sp.dma_start(at_last[whole:whole + 1, 0:rest, :],
                                 attr[first + whole * J:N_EDGES, :].rearrange("(p j) d -> p j d", p=1)
                                 ).then_inc(last_in, 16)
                sp.wait_ge(packed, 2)
                sp.dma_start(self.rec_by_dst.rearrange("(g p j) c -> p g (j c)", p=P, j=J),
                             rec[:, :, :, :].rearrange("p g j c -> p g (j c)")).then_inc(stored, 16)
                sp.wait_ge(loaded, 16 * n_loads)
                sp.dma_start(self.key_row.rearrange("(g p j) -> p g j", p=P, j=J), ids[:, 1, :, :]).then_inc(stored, 16)
                with sp.Fori(1, (NG - 4) // ATS) as i:
                    for q in range(ATS):
                        load(i * ATS + q, q)
                for g in range(NG - 4, NG - 1):
                    load(g, g % ATS)
                sp.wait_ge(stored, 32)

            @block.vector
            def _(dve):
                dve.memset(ids[:, :, NG - 1, :], PAD_NODE).then_inc(padded, 1)
                dve.wait_ge(loaded, 16 * n_loads)
                for w in range(2):
                    dve.tensor_copy(rec[:, :, :, w], ids[:, w, :, :]).then_inc(packed, 1)
                step = Chain(dve, steps)
                step(dve.tensor_scalar(tile_i[:, :], ids[:, 0, :, :].rearrange("p g j -> p (g j)"),
                                       P.bit_length() - 1, None, ALU.logical_shift_right))
                step(dve.tensor_copy(tile_f[:, :], tile_i[:, :]))
                step(dve.memset(ones_s[:, :], 1.0))
                with dve.Fori(0, NT // U) as i:
                    for k in range(U):
                        b = i * U + k
                        dve.tensor_scalar(is_b[:, bass.ds(b, 1), :].rearrange("p b s -> p (b s)"), tile_f[:, :],
                                          self.tile_no[:, bass.ds(b, 1)], 0.0,
                                          ALU.is_equal, ALU.add, accum_out=counts[:, bass.ds(b, 1)]).then_inc(tile_steps, 1)
                dve.wait_ge(tile_steps, NT)
                dve.wait_ge(summed, 1)
                step(dve.tensor_copy(total[:, :], pc[:, 1, 0:NT]))
                step(dve.tensor_tensor_scan(upto[:, :], ones_s[:, 0:NT], total[:, :], 0.0, ALU.mult, ALU.add))
                step(dve.tensor_tensor(start[:, :], upto[:, :], total[:, :], ALU.subtract))
                step(dve.tensor_tensor(start[:, :], start[:, :], pc[:, 0, 0:NT], ALU.add))
                step(dve.tensor_scalar(start[:, :], start[:, :], 1.0, None, ALU.subtract))
                def places(b, s, scans):
                    dve.tensor_tensor_scan(run[:, :], ones_s[:, :],
                                           is_b[:, bass.ds(b, 1), :].rearrange("p b s -> p (b s)"), start[:, bass.ds(b, 1)],
                                           ALU.mult, ALU.add).then_inc(scanned, 1)
                    dve.wait_ge(scanned, scans)
                    dve.wait_ge(placed, b + 1)
                    dve.scalar_tensor_tensor(here[:, s, :], tile_f[:, :], self.tile_no[:, bass.ds(b, 1)], run[:, :],
                                             ALU.is_equal, ALU.mult).then_inc(here_ready, 1)
                    dve.wait_ge(here_ready, scans)

                with dve.Fori(0, NT // (2 * U)) as i:
                    for k in range(2 * U):
                        places(i * 2 * U + k, k % 2, i * 2 * U + (k + 1))
                for b in range(NT // (2 * U) * 2 * U, NT):
                    places(b, b % 2, b + 1)
                dve.wait_ge(placed, NT + 2)
                step(dve.tensor_copy(place[:, :], place_f[:, :]))

            @block.gpsimd
            def _(pool):
                pool.memset(a_e[:, :], 0.0).then_inc(cleared, 1)
                pool.memset(at_last[:, :, :], 0.0).then_inc(cleared, 1)
                pool.memset(place_f[:, :], 0.0).then_inc(cleared, 1)
                pool.sem_inc(placed, 2)
                pool.wait_ge(cleared, 3)

                def add(b, s):
                    pool.wait_ge(here_ready, b + 1)
                    pool.tensor_tensor(place_f[:, :], place_f[:, :], here[:, s, :], ALU.add).then_inc(placed, 1)
                    pool.wait_ge(placed, b + 3)

                with pool.Fori(0, NT // (2 * U)) as i:
                    for k in range(2 * U):
                        add(i * 2 * U + k, k % 2)
                for b in range(NT // (2 * U) * 2 * U, NT):
                    add(b, b % 2)

            @block.scalar
            def _(act):
                act.sem_inc(at_T_ready, 2)
                act.sem_inc(logit_out, 2)

                def fetch(g, q):
                    act.wait_ge(attr_free, g + (ATS + 1))
                    act.wait_ge(logit_ready, g + 1)
                    act.activation(at_T[:, q, :, :], p_at[:, q, :, :], ACT.Copy).then_inc(at_T_ready, 1)

                def keep(g, q):
                    act.wait_ge(logit_ready, g + 3)
                    act.activation(logit_e[:, bass.ds(g, 1), :].rearrange("p g j -> p (g j)"), p_logit[:, q, 0:J],
                                   ACT.Copy).then_inc(logit_out, 1)

                fetch(0, 0)
                with act.Fori(0, (NG - 4) // ATS) as i:
                    for q in range(ATS):
                        fetch(i * ATS + (q + 1), (q + 1) % 2)
                        keep(i * ATS + q, q % 2)
                for g in range(NG - 4, NG):
                    if g < NG - 1:
                        fetch(g + 1, (g + 1) % 2)
                    keep(g, g % 2)

            @block.tensor
            def _(pe):
                pe.sem_inc(attr_free, ATS)
                pe.sem_inc(logit_ready, 2)
                pe.wait_ge(consts, 32)

                def turn(g, q, attributes):
                    pe.wait_ge(at_T_ready, g + 1)
                    for k in range(J // 2):
                        last = nc.tensor.transpose(p_at[:, q, k, :],
                                                   attributes[:, 2 * k:2 * k + 2, :].rearrange("p j d -> p (j d)"),
                                                   self.ident[:, :])
                    last.then_inc(attr_free, 1)

                def dot(g, q):
                    pe.wait_ge(at_T_ready, g + 3)
                    pe.wait_ge(logit_out, g + 1)
                    for k in range(J // 2):
                        last = nc.tensor.matmul(p_logit[:, q, 2 * k:2 * k + 2], at_T[:, q, k, :], a_e[:, :],
                                                start=True, stop=True)
                    last.then_inc(logit_ready, 1)

                pe.wait_ge(attr_in[0], 16)
                turn(0, 0, at[:, 0])
                half = (NG - 4) // ATS // 3
                for lo, hi in ((0, half), (half, (NG - 4) // ATS)):
                    with pe.Fori(lo, hi) as i:
                        for q in range(ATS):
                            r = (q + 1) % ATS
                            pe.wait_ge(attr_in[r], i * 16 + 16 * (1 + (q + 1) // ATS))
                            turn(i * ATS + (q + 1), (q + 1) % 2, at[:, r])
                            dot(i * ATS + q, q % 2)
                    if lo == 0:
                        pe.wait_ge(tile_steps, NT)
                        nc.tensor.matmul(pc[:, 0, 0:NT], self.before[:, :], counts[:, :], start=True, stop=True)
                        nc.tensor.matmul(pc[:, 1, 0:NT], self.ones[:, :], counts[:, :],
                                         start=True, stop=True).then_inc(summed, 1)
                for g in range(NG - 4, NG):
                    if g < NG - 2:
                        pe.wait_ge(attr_in[(g + 1) % ATS], 16 * ((g + 1) // ATS + 1))
                        turn(g + 1, (g + 1) % 2, at[:, (g + 1) % ATS])
                    elif g == NG - 2:
                        pe.wait_ge(last_in, 16 * (2 if rest else 1))
                        turn(g + 1, (g + 1) % 2, at_last)
                    dot(g, g % 2)

    def ranges(self, order):
        nc = self.nc
        rec_dram = (self.rec_by_dst, self.rec_by_src)[order]
        with ExitStack() as c:
            def sb(name, shape, dt):
                return c.enter_context(nc.sbuf_tensor(f"{name}{order}", shape, dt))

            def sem(name):
                return self.sem(c, f"{name}{order}")

            rec = sb("rg_rec", [P, NG, J, 2], I32)
            key = sb("rg_key", [P, NG, J], FP32)
            ext = sb("rg_ext", [P, 2, NG], FP32)
            ext_i = sb("rg_exti", [1, 2, NG], I32)
            ext_t = sb("rg_extt", [NG, 2], FP32)
            pT = c.enter_context(nc.psum_tensor(f"rg_pT{order}", [P, 2, P], FP32))
            pR = c.enter_context(nc.psum_tensor(f"rg_pR{order}", [1, 2, P], FP32))
            got, steps, turned, found = sem("rg_got"), sem("rg_steps"), sem("rg_turned"), sem("rg_found")
            block = c.enter_context(nc.Block())

            @block.sync
            def _(sp):
                sp.dma_start(rec[:, :, :, :].rearrange("p g j c -> p g (j c)"),
                             rec_dram.rearrange("(g p j) c -> p g (j c)", p=P, j=J)).then_inc(got, 16)

            @block.vector
            def _(dve):
                step = Chain(dve, steps)
                dve.wait_ge(got, 16)
                step(dve.tensor_copy(key[:, :, :], rec[:, :, :, 1 - order]))
                step(dve.tensor_reduce(ext[:, 0, :], key[:, :, :], AX.X, ALU.min))
                step(dve.tensor_reduce(ext[:, 1, :], key[:, :, :], AX.X, ALU.max))
                dve.wait_ge(turned, 1)
                step(dve.tensor_reduce(ext_t[:, 0:1], pT[0:NG, 0, :], AX.X, ALU.min))
                step(dve.tensor_reduce(ext_t[:, 1:2], pT[0:NG, 1, :], AX.X, ALU.max))
                step(dve.tensor_scalar(ext_t[:, 1:2], ext_t[:, 1:2], float(P), None, ALU.add))
                dve.wait_ge(turned, 2)
                step(dve.tensor_copy(ext_i[:, :, :], pR[:, :, 0:NG]))
                shift = P.bit_length() - 1
                dve.tensor_scalar(self.bounds[0:1, order, :, :], ext_i[:, :, :], shift, None,
                                  ALU.logical_shift_right).then_inc(found, 1)
                dve.wait_ge(found, 1)

            @block.tensor
            def _(pe):
                pe.wait_ge(steps, 3)
                nc.tensor.transpose(pT[0:NG, 0, :], ext[:, 0, :], self.ident[:, :])
                nc.tensor.transpose(pT[0:NG, 1, :], ext[:, 1, :], self.ident[:, :]).then_inc(turned, 1)
                pe.wait_ge(steps, 6)
                nc.tensor.transpose(pR[:, 0, 0:NG], ext_t[:, 0:1], self.ident[0:NG, 0:NG])
                nc.tensor.transpose(pR[:, 1, 0:NG], ext_t[:, 1:2], self.ident[0:NG, 0:NG]).then_inc(turned, 1)

    def tiles_of_group(self, eng, order, g):
        return (eng.value_load(self.bounds[0:1, order, 0, bass.ds(g, 1)], min_val=0, max_val=NT - 1),
                eng.value_load(self.bounds[0:1, order, 1, bass.ds(g, 1)], min_val=1, max_val=NT))

    def aggregate(self, name, order, table, width, acc, at, zero, count=None, own=None):
        nc = self.nc
        OWN = NG // 2
        assert OWN >= NT
        rec_dram = (self.rec_by_dst, self.rec_by_src)[order]
        recs = rec_dram.rearrange("(g p j) c -> g p (j c)", p=P, j=J)
        R, GS = 4, 2
        SL, LAG = 4, 2
        tw = table.shape[1]
        with ExitStack() as c:
            def sb(nm, shape, dt):
                return c.enter_context(nc.sbuf_tensor(f"{name}_{nm}", shape, dt))

            def sem(nm):
                return self.sem(c, f"{name}_{nm}")

            rec = sb("rec", [P, R, J, 2], I32)
            extra = 2 if count is not None else 0
            rows = sb("rows", [P, GS, J, tw + extra], BF16)
            krel = sb("krel", [P, J], FP32)
            hot = sb("hot", [P, SL * J, P], BF16)
            sums = c.enter_context(nc.psum_tensor(f"{name}_sums", [P, SL * 512], FP32))
            MEMBERS = width
            if own:
                h, w_own, b_own = own
                own_w = sb("own_w", [P, 2, F], FP32)
                own_b = sb("own_b", [1, F], FP32)
                own_in = sb("own_in", [P, F], FP32)
                own_T = sb("own_T", [P, 2, P], FP32)
                p_own_T = c.enter_context(nc.psum_tensor(f"{name}_p_own_T", [P, 2, P], FP32))
                p_own = c.enter_context(nc.psum_tensor(f"{name}_p_own", [P, 512], FP32))
                own_loaded, own_fetched, own_turned, own_T_ready, own_ready, own_kept = (
                    sem(n) for n in ("own_loaded", "own_fetched", "own_turned", "own_T_ready", "own_ready", "own_kept"))
                act_turns = sem("act_turns")
            rec_in = [sem(f"rec_in{s}") for s in range(R)]
            rows_in = [[sem(f"rows_in{s}_{j}") for j in range(J)] for s in range(GS)]
            rows_free = sem("rows_free")
            rec_free, rec_used = sem("rec_free"), sem("rec_used")
            pool_turns = sem("pool_turns")
            hot_ready, sums_ready, steps, zeroed, added = (
                sem(n) for n in ("hot_ready", "sums_ready", "steps", "zeroed", "added"))
            block = c.enter_context(nc.Block())
            n_zeroed = 1 + (1 if zero else 0) + (2 if count is not None else 0) + (1 if own else 0)

            @block.sync
            def _(sp):
                if own:
                    sp.dma_start(own_w[:, :, :], w_own.rearrange("(c k) n -> k c n", k=P)).then_inc(own_loaded, 16)
                    sp.dma_start(own_b[:, :], b_own.rearrange("(a n) -> a n", a=1)).then_inc(own_loaded, 16)
                with sp.Fori(0, NG // R) as i:
                    for s in range(R):
                        sp.wait_ge(rec_free, i * R + (s + 1))
                        sp.wait_ge(rec_used, i * R + (s + 1))
                        sp.dma_start(rec[:, s, :, :].rearrange("p j c -> p (j c)"),
                                     recs[bass.ds(i * R + s, 1), :, :].rearrange("g p x -> (g p) x")).then_inc(rec_in[s], 16)

            @block.gpsimd
            def _(pool):
                with pool.Fori(0, NG // R) as i:
                    for s in range(R):
                        q = s % GS
                        pool.wait_ge(rec_in[s], i * 16 + 16)
                        pool.wait_ge(rows_free, i * R + (s + 1))
                        pool.sem_inc(pool_turns, 1)
                        for j in range(J):
                            pool.indirect_dma_start(
                                out=rows[:, q, j, 0:tw], out_offset=None, in_=table,
                                in_offset=bass.IndirectOffsetOnAxis(ap=rec[:, s, j, order:order + 1], axis=0),
                            ).then_inc(rows_in[q][j], 16)

            @block.vector
            def _(dve):
                dve.sem_inc(rec_free, R)
                dve.memset(sums[:, (SL - LAG) * 512:SL * 512], 0.0).then_inc(zeroed, 1)
                if zero:
                    dve.memset(acc[:, :, at:at + width], 0.0).then_inc(zeroed, 1)
                if count is not None:
                    dve.memset(count[:, :], 0.0).then_inc(zeroed, 1)
                    dve.memset(rows[:, :, :, tw:tw + extra], 1.0).then_inc(zeroed, 1)
                if own:
                    dve.memset(h[:, NT:OWN, :], 0.0).then_inc(zeroed, 1)
                dve.wait_ge(zeroed, n_zeroed)
                dve.sem_inc(added, LAG)
                dve.sem_inc(hot_ready, 1)
                npair = dve.alloc_register(f"{name}_dve_pairs")
                slot = dve.alloc_register(f"{name}_dve_slot")
                old_slot = dve.alloc_register(f"{name}_dve_old_slot")
                tiles = [dve.alloc_register(f"{name}_dve_tile{k}") for k in range(LAG)]
                dve.reg_mov(npair, 0)
                dve.reg_mov(slot, 0)
                dve.reg_mov(old_slot, SL - LAG)
                for r in tiles:
                    dve.reg_mov(r, 0)

                def add_old(n, sl, b):
                    cell = acc[:, bass.ds(b, 1), at:at + width].rearrange("p a w -> p (a w)")
                    dve.wait_ge(added, n + LAG)
                    if count is not None:
                        many = count[:, bass.ds(b, 1)]
                        dve.tensor_tensor(many, many, sums[:, bass.ds(sl * 512 + MEMBERS, 1)], ALU.add).then_inc(steps, 1)
                    dve.tensor_tensor(cell, cell, sums[:, bass.ds(sl * 512, width)], ALU.add).then_inc(added, 1)

                K = 2 if count is not None else 1
                with dve.Fori(0, NG // R) as i:
                    for s in range(R):
                        dve.wait_ge(rec_in[s], i * 16 + 16)
                        lo, hi = self.tiles_of_group(dve, order, i * R + s)
                        with dve.Fori(lo, hi) as b:
                            n = dve.snap(npair)
                            sl = dve.snap(slot, min_val=0, max_val=SL - 1)
                            old = dve.snap(old_slot, min_val=0, max_val=SL - 1)
                            b_old = dve.snap(tiles[0], min_val=0, max_val=NT - 1)
                            dve.wait_ge(hot_ready, n + 1)
                            dve.tensor_scalar(krel[:, :], rec[:, s, :, 1 - order], self.neg_base[:, bass.ds(b, 1)],
                                              None, ALU.add).then_inc(steps, 1)
                            dve.wait_ge(steps, n * K + 1)
                            dve.tensor_tensor(hot[:, bass.ds(sl * J, J), :], self.col[:, None, :].to_broadcast([P, J, P]),
                                              krel[:, :, None].to_broadcast([P, J, P]), ALU.is_equal).then_inc(hot_ready, 1)
                            dve.wait_ge(sums_ready, n + 1)
                            add_old(n, old, b_old)
                            for r, newer in zip(tiles, tiles[1:]):
                                dve.reg_mov(r, newer)
                            dve.reg_mov(tiles[-1], b)
                            dve.reg_add(npair, npair, 1)
                            dve.reg_alu(slot, npair, SL - 1, ALU.bitwise_and)
                            dve.reg_add(old_slot, npair, SL - LAG)
                            dve.reg_alu(old_slot, old_slot, SL - 1, ALU.bitwise_and)
                        dve.sem_inc(rec_free, 1)
                for r in tiles:
                    n = dve.snap(npair)
                    old = dve.snap(old_slot, min_val=0, max_val=SL - 1)
                    b_old = dve.snap(r, min_val=0, max_val=NT - 1)
                    dve.wait_ge(sums_ready, n + 1)
                    if count is not None:
                        dve.sem_inc(steps, 1)
                    add_old(n, old, b_old)
                    dve.reg_add(npair, npair, 1)
                    dve.reg_add(old_slot, npair, SL - LAG)
                    dve.reg_alu(old_slot, old_slot, SL - 1, ALU.bitwise_and)
                n = dve.snap(npair)
                dve.wait_ge(added, n + LAG)
                if count is not None:
                    dve.wait_ge(steps, n * K)
                dve.sem_inc(rec_free, 1)

            if own:
                @block.scalar
                def _(act):
                    act.sem_inc(own_kept, 1)
                    act.wait_ge(zeroed, n_zeroed)
                    with act.Fori(0, OWN) as t:
                        act.wait_ge(own_turned, t + 1)
                        act.sem_inc(act_turns, 1)
                        act.activation(own_in[:, :], tile(h, t), ACT.Copy).then_inc(own_fetched, 1)
                        act.wait_ge(own_turned, t + 2)
                        act.activation(own_T[:, :, :], p_own_T[:, :, :], ACT.Copy).then_inc(own_T_ready, 1)
                        act.wait_ge(own_ready, t + 1)
                        act.sem_inc(act_turns, 1)
                        act.activation(tile(h, t), p_own[:, 0:F], ACT.Copy).then_inc(own_kept, 1)
                    act.wait_ge(own_kept, OWN + 1)
                    act.sem_inc(act_turns, 1)

            @block.tensor
            def _(pe):
                def turn_own(t):
                    pe.wait_ge(own_fetched, t + 1)
                    for k in range(2):
                        last = nc.tensor.transpose(p_own_T[:, k, :], own_in[:, k * P:(k + 1) * P], self.ident[:, :])
                    last.then_inc(own_turned, 1)

                def multiply_own(t):
                    pe.wait_ge(own_T_ready, t + 1)
                    pe.wait_ge(own_kept, t + 1)
                    for k in range(2):
                        nc.tensor.matmul(p_own[:, 0:F], own_T[:, k, :], own_w[:, k, :], start=(k == 0), stop=False)
                    nc.tensor.matmul(p_own[:, 0:F], self.ones[0:1, :], own_b[:, :], start=False, stop=True
                                     ).then_inc(own_ready, 1)

                pe.sem_inc(rows_free, GS)
                pe.sem_inc(rec_used, R)
                if own:
                    pe.wait_ge(own_loaded, 32)
                    pe.sem_inc(own_turned, 1)
                pe.wait_ge(zeroed, n_zeroed)
                pe.sem_inc(sums_ready, LAG)
                npair = pe.alloc_register(f"{name}_pe_pairs")
                slot = pe.alloc_register(f"{name}_pe_slot")
                pe.reg_mov(npair, 0)
                pe.reg_mov(slot, 0)
                with pe.Fori(0, NG // R) as i:
                    for s in range(R):
                        q = s % GS
                        if own:
                            (turn_own, multiply_own)[s % 2](i * 2 + s // 2)
                        lo, hi = self.tiles_of_group(pe, order, i * R + s)
                        with pe.Fori(lo, hi) as b:
                            n = pe.snap(npair)
                            sl = pe.snap(slot, min_val=0, max_val=SL - 1)
                            pe.wait_ge(added, n + 1)
                            pe.wait_ge(hot_ready, n + 2)
                            out = sums[:, bass.ds(sl * 512, width)]
                            for j in range(J):
                                pe.wait_ge(rows_in[q][j], (i * (R // GS) + (s // GS + 1)) * 16)
                                hot_j = hot[:, bass.ds(sl * J + j, 1), :].rearrange("p a n -> p (a n)")
                                nc.tensor.matmul(sums[:, bass.ds(sl * 512, width + extra)], hot_j,
                                                 rows[:, q, j, 2 * width:3 * width + extra], start=(j == 0), stop=False)
                                for part in range(2):
                                    last = nc.tensor.matmul(out, hot_j, rows[:, q, j, part * width:(part + 1) * width],
                                                            start=False, stop=(j == J - 1 and part == 1))
                            last.then_inc(sums_ready, 1)
                            pe.reg_add(npair, npair, 1)
                            pe.reg_alu(slot, npair, SL - 1, ALU.bitwise_and)
                        pe.wait_ge(sums_ready, pe.snap(npair) + LAG)
                        pe.sem_inc(rows_free, 1)
                        pe.sem_inc(rec_used, 1)

    def attention(self, acc, a_dst, degree):
        nc = self.nc
        table, rec_all, place, logit_e = self.tab_z, self.rec, self.place, self.logit_e
        recs = self.rec_by_dst.rearrange("(g p j) c -> g p (j c)", p=P, j=J)
        R, GS = 4, 2
        with ExitStack() as c:
            def sb(nm, shape, dt):
                return c.enter_context(nc.sbuf_tensor(f"at_{nm}", shape, dt))

            def ps(nm, shape):
                return c.enter_context(nc.psum_tensor(f"at_{nm}", shape, FP32))

            def sem(nm):
                return self.sem(c, f"at_{nm}")

            rec = sb("rec", [P, R, J, 2], I32)
            keys = sb("keys", [P, GS, GE], I32)
            rows = sb("rows", [P, R, J, W0], FP32)
            moved = sb("moved", [P, GS, J, 2], I32)
            target = sb("target", [P, GS, J], I32)
            u = sb("u", [P, 2, J], FP32)
            pen = sb("pen", [P, J, P], FP32)
            logit = sb("logit", [P, J, P], FP32)
            shifted = sb("shifted", [P, J, P], FP32)
            leaky = sb("leaky", [P, J, P], FP32)
            w = sb("w", [P, J, P], FP32)
            w_e = sb("w_e", [P, J, P], FP32)
            enters = sb("enters", [P, J, P], BF16)
            umax = sb("umax", [P, NT], FP32)
            mrun = sb("mrun", [P, NT], FP32)
            tmax = sb("tmax", [P, 1], FP32)
            lin = sb("lin", [P, 1], FP32)
            mnew = sb("mnew", [P, 1], FP32)
            mneg = sb("mneg", [P, 1], FP32)
            fell = sb("fell", [P, 1], FP32)
            keep = sb("keep", [P, 1], FP32)
            keep_old = sb("keep_old", [P, 1], FP32)
            wsum = sb("wsum", [P, 1], FP32)
            joined = sb("joined", [P, 1], FP32)
            u_on_nodes = ps("u_on_nodes", [P, 2, J, P])
            w_turned = ps("w_turned", [P, J, P])
            sums = ps("sums", [P, 2 * 512])
            rec_in = [sem(f"rec_in{s}") for s in range(R)]
            rows_in = [sem(f"rows_in{s}") for s in range(R)]
            keys_in = [sem(f"keys_in{s}") for s in range(GS)]
            sent = [sem(f"sent{s}") for s in range(GS)]
            rec_free, rows_free, keys_free = sem("rec_free"), sem("rows_free"), sem("keys_free")
            copied, zeroed, steps, u_ready, ub_ready = (
                sem(n) for n in ("copied", "zeroed", "steps", "u_ready", "ub_ready"))
            pen_ready, logit_ready, m_ready, fell_ready = (
                sem(n) for n in ("pen_ready", "logit_ready", "m_ready", "fell_ready"))
            shifted_ready, leaky_ready, w_ready, keep_ready, counted = (
                sem(n) for n in ("shifted_ready", "leaky_ready", "w_ready", "keep_ready", "counted"))
            turned, w_e_ready, sums_ready, added = sem("turned"), sem("w_e_ready"), sem("sums_ready"), sem("added")
            pool_turns, dve_turns = sem("pool_turns"), sem("dve_turns")
            block = c.enter_context(nc.Block())
            K = 7

            def limits(eng, g):
                return self.tiles_of_group(eng, 0, g)

            @block.sync
            def _(sp):
                def load_records(g, s):
                    sp.wait_ge(rec_free, g + 1)
                    sp.dma_start(rec[:, s, :, :].rearrange("p j c -> p (j c)"),
                                 recs[bass.ds(g, 1), :, :].rearrange("g p x -> (g p) x")).then_inc(rec_in[s], 16)

                def load_keys(g, q):
                    sp.wait_ge(keys_free, g + 1)
                    sp.dma_start(keys[:, q, :], self.key_row.rearrange("(g e) -> g e", e=GE)[bass.ds(g, 1), :]
                                 .to_broadcast([P, GE])).then_inc(keys_in[q], 16)

                for g in range(GS):
                    load_records(g, g)
                with sp.Fori(0, NG // R - 1) as i:
                    for s in range(R):
                        load_records(i * R + (s + GS), (s + GS) % R)
                        load_keys(i * R + s, s % GS)
                for g in range(NG - R, NG):
                    if g + GS < NG:
                        load_records(g + GS, (g + GS) % R)
                    load_keys(g, g % GS)

            @block.gpsimd
            def _(pool):
                def scatter(g, q, reused):
                    if reused is not None:
                        pool.wait_ge(sent[q], reused)
                    pool.tensor_copy(moved[:, q, :, :], rec_all[:, bass.ds(g, 1), :, :].rearrange("p g j c -> p (g j) c")
                                     ).then_inc(copied, 1)
                    pool.tensor_copy(target[:, q, :], place[:, bass.ds(g * J, J)]).then_inc(copied, 1)
                    pool.wait_ge(copied, g * 2 + 2)
                    pool.sem_inc(pool_turns, 1)
                    for j in range(J):
                        pool.indirect_dma_start(
                            out=self.rec_by_src, in_=moved[:, q, j, :], in_offset=None,
                            out_offset=bass.IndirectOffsetOnAxis(ap=target[:, q, j:j + 1], axis=0),
                        ).then_inc(sent[q], 16)

                def gather(g, s, rec_at):
                    pool.wait_ge(rec_in[s], rec_at)
                    pool.wait_ge(rows_free, g + 1)
                    pool.sem_inc(pool_turns, 1)
                    for j in range(J):
                        pool.indirect_dma_start(
                            out=rows[:, s, j, :], out_offset=None, in_=table,
                            in_offset=bass.IndirectOffsetOnAxis(ap=rec[:, s, j, 0:1], axis=0),
                        ).then_inc(rows_in[s], 16)

                for s in range(R):
                    gather(s, s, 16)
                    scatter(s, s % GS, None if s < GS else 16 * J * (s // GS))
                with pool.Fori(1, NG // R) as i:
                    for s in range(R):
                        gather(i * R + s, s, i * 16 + 16)
                        scatter(i * R + s, s % GS, (i * (R // GS) + s // GS) * (16 * J))
                for q in range(GS):
                    pool.wait_ge(sent[q], 16 * J * (NG // GS))

            @block.vector
            def _(dve):
                dve.sem_inc(rec_free, R)
                dve.sem_inc(keys_free, GS)
                dve.memset(acc[:, :, :], 0.0).then_inc(zeroed, 1)
                dve.memset(umax[:, :], -BIG).then_inc(zeroed, 1)
                dve.memset(mrun[:, :], -BIG).then_inc(zeroed, 1)
                dve.memset(degree[:, :], 0.0).then_inc(zeroed, 1)
                dve.memset(sums[:, 512:1024], 0.0).then_inc(zeroed, 1)
                dve.memset(keep_old[:, :], 1.0).then_inc(zeroed, 1)
                dve.wait_ge(zeroed, 6)
                dve.sem_inc(logit_ready, 1)
                dve.sem_inc(leaky_ready, 1)
                dve.sem_inc(added, 1)
                npair = dve.alloc_register("at_dve_pairs")
                slot = dve.alloc_register("at_dve_slot")
                last_b = dve.alloc_register("at_dve_tile")
                dve.reg_mov(npair, 0)
                dve.reg_mov(slot, 0)
                dve.reg_mov(last_b, 0)

                def add_last(sl, b):
                    cell = acc[:, bass.ds(b, 1), 0:F].rearrange("p a w -> p (a w)")
                    return dve.scalar_tensor_tensor(cell, cell, keep_old[:, :], sums[:, bass.ds((1 - sl) * 512, F)],
                                                    ALU.mult, ALU.add)

                def edge_terms(g, s, rounds):
                    dve.wait_ge(rows_in[s], rounds * (16 * J))
                    dve.tensor_tensor(u[:, s % 2, :], rows[:, s, :, C_SRC],
                                      logit_e[:, bass.ds(g, 1), :].rearrange("p g j -> p (g j)"), ALU.add).then_inc(u_ready, 1)

                def groups(i, s, last):
                    q = s % GS
                    g = i * R + s
                    if not last:
                        edge_terms(g + 1, (s + 1) % R, i + (1 + (s + 1) // R))
                    dve.wait_ge(keys_in[q], (i * (R // GS) + (s // GS + 1)) * 16)
                    lo, hi = limits(dve, g)
                    with dve.Fori(lo, hi) as b:
                        n = dve.snap(npair)
                        sl = dve.snap(slot, min_val=0, max_val=1)
                        b_last = dve.snap(last_b, min_val=0, max_val=NT - 1)
                        step = Chain(dve, steps, n * K)
                        at_b = bass.ds(b, 1)
                        dve.wait_ge(counted, n + 1)
                        dve.wait_ge(logit_ready, n + 1)
                        dve.tensor_scalar(pen[:, :, :], keys[:, q, :].rearrange("p (e j) -> p j e", j=J),
                                          self.node_id[:, at_b], -BIG, ALU.not_equal, ALU.mult).then_inc(pen_ready, 1)
                        dve.wait_ge(pen_ready, n + 1)
                        dve.wait_ge(ub_ready, g + 1)
                        dve.wait_ge(shifted_ready, n + 1)
                        dve.sem_inc(dve_turns, 1)
                        dve.tensor_tensor_reduce(out=logit[:, :, :], in0=u_on_nodes[:, s % 2, :, :], in1=pen[:, :, :], scale=1.0,
                                                 scalar=-BIG, op0=ALU.add, op1=ALU.max,
                                                 accum_out=tmax[:, :]).then_inc(logit_ready, 1)
                        dve.wait_ge(logit_ready, n + 2)
                        step(dve.tensor_tensor(umax[:, at_b], umax[:, at_b], tmax[:, :], ALU.max))
                        step(dve.tensor_tensor(lin[:, :], umax[:, at_b], a_dst[:, at_b], ALU.add))
                        step(dve.scalar_tensor_tensor(mnew[:, :], lin[:, :], ALPHA, lin[:, :], ALU.mult, ALU.max))
                        dve.tensor_scalar(mneg[:, :], mnew[:, :], -1.0, None, ALU.mult).then_inc(m_ready, 1)
                        dve.tensor_tensor(fell[:, :], mrun[:, at_b], mnew[:, :], ALU.subtract).then_inc(fell_ready, 1)
                        dve.wait_ge(fell_ready, n + 1)
                        step(copy(dve, mrun[:, at_b], mnew[:, :]))
                        dve.wait_ge(w_ready, n + 1)
                        dve.wait_ge(shifted_ready, n + 2)
                        dve.scalar_tensor_tensor(leaky[:, :, :], shifted[:, :, :], ALPHA, shifted[:, :, :],
                                                 ALU.mult, ALU.max).then_inc(leaky_ready, 1)
                        dve.wait_ge(sums_ready, n + 1)
                        add_last(sl, b_last).then_inc(added, 1)
                        for half in range(2):
                            dve.wait_ge(turned, n * 2 + half + 1)
                            js = slice(half * J // 2, (half + 1) * J // 2)
                            dve.tensor_copy(w_e[:, js, :], w_turned[:, js, :]).then_inc(w_e_ready, 1)
                        dve.wait_ge(keep_ready, n + 1)
                        den = acc[:, at_b, F:F + 1].rearrange("p a w -> p (a w)")
                        step(dve.scalar_tensor_tensor(den, den, keep[:, :], wsum[:, :], ALU.mult, ALU.add))
                        dve.wait_ge(added, n + 2)
                        step(dve.tensor_scalar(keep_old[:, :], keep[:, :], 1.0, None, ALU.mult))
                        dve.wait_ge(counted, n + 2)
                        step(dve.tensor_tensor(degree[:, at_b], degree[:, at_b], joined[:, :], ALU.add))
                        assert step.n == K
                        dve.reg_mov(last_b, b)
                        dve.reg_add(npair, npair, 1)
                        dve.reg_sub(slot, 1, slot)
                    dve.sem_inc(rec_free, 1)
                    dve.sem_inc(keys_free, 1)

                edge_terms(0, 0, 1)
                with dve.Fori(0, NG // R - 1) as i:
                    for s in range(R):
                        groups(i, s, False)
                for s in range(R):
                    groups(NG // R - 1, s, s == R - 1)
                n = dve.snap(npair)
                sl = dve.snap(slot, min_val=0, max_val=1)
                b_last = dve.snap(last_b, min_val=0, max_val=NT - 1)
                dve.wait_ge(sums_ready, n + 1)
                add_last(sl, b_last).then_inc(added, 1)
                dve.wait_ge(added, n + 2)
                dve.sem_inc(dve_turns, 1)

            @block.scalar
            def _(act):
                act.sem_inc(shifted_ready, 1)
                act.sem_inc(w_ready, 1)
                act.sem_inc(counted, 1)
                npair = act.alloc_register("at_act_pairs")
                act.reg_mov(npair, 0)
                with act.Fori(0, NG) as g:
                    lo, hi = limits(act, g)
                    with act.Fori(lo, hi) as b:
                        n = act.snap(npair)
                        act.wait_ge(logit_ready, n + 2)
                        act.wait_ge(leaky_ready, n + 1)
                        act.activation(shifted[:, :, :], logit[:, :, :], ACT.Identity, bias=a_dst[:, bass.ds(b, 1)],
                                       scale=1.0).then_inc(shifted_ready, 1)
                        act.wait_ge(leaky_ready, n + 2)
                        act.wait_ge(m_ready, n + 1)
                        act.activation(w[:, :, :], leaky[:, :, :], ACT.Exp, bias=mneg[:, :], scale=1.0,
                                       accum_out=wsum[:, :]).then_inc(w_ready, 1)
                        act.wait_ge(fell_ready, n + 1)
                        act.activation(keep[:, :], fell[:, :], ACT.Exp).then_inc(keep_ready, 1)
                        act.wait_ge(pen_ready, n + 1)
                        act.activation(enters[:, :, :], pen[:, :, :], ACT.Identity, bias=1.0, scale=1.0 / BIG,
                                       accum_out=joined[:, :]).then_inc(counted, 1)
                        act.reg_add(npair, npair, 1)

            @block.tensor
            def _(pe):
                pe.sem_inc(rows_free, R)
                pe.wait_ge(zeroed, 6)
                pe.sem_inc(sums_ready, 1)
                npair = pe.alloc_register("at_pe_pairs")
                slot = pe.alloc_register("at_pe_slot")
                pe.reg_mov(npair, 0)
                pe.reg_mov(slot, 0)
                def spread(g, s):
                    pe.wait_ge(u_ready, g + 1)
                    for j in range(J):
                        last = nc.tensor.transpose(u_on_nodes[:, s % 2, j, :], u[:, s % 2, j:j + 1].to_broadcast([P, P]),
                                                   self.ident[:, :])
                    last.then_inc(ub_ready, 1)

                def groups(i, s, last_group):
                    g = i * R + s
                    if not last_group:
                        spread(g + 1, s + 1)
                    pe.wait_ge(rows_in[s], (i + 1) * (16 * J))
                    lo, hi = limits(pe, g)
                    with pe.Fori(lo, hi) as b:
                        n = pe.snap(npair)
                        sl = pe.snap(slot, min_val=0, max_val=1)
                        pe.wait_ge(w_ready, n + 2)
                        for j in range(J):
                            last = nc.tensor.transpose(w_turned[:, j, :], w[:, j, :], self.ident[:, :])
                            if j % (J // 2) == J // 2 - 1:
                                last.then_inc(turned, 1)
                        pe.wait_ge(added, n + 1)
                        for j in range(J):
                            if j % (J // 2) == 0:
                                pe.wait_ge(w_e_ready, n * 2 + (j // (J // 2) + 1))
                            last = nc.tensor.matmul(sums[:, bass.ds(sl * 512, F)], w_e[:, j, :], rows[:, s, j, 0:F],
                                                    start=(j == 0), stop=(j == J - 1))
                        last.then_inc(sums_ready, 1)
                        pe.reg_add(npair, npair, 1)
                        pe.reg_sub(slot, 1, slot)
                    pe.wait_ge(sums_ready, pe.snap(npair) + 1)
                    pe.sem_inc(rows_free, 1)

                spread(0, 0)
                with pe.Fori(0, NG // R - 1) as i:
                    for s in range(R):
                        groups(i, s, False)
                for s in range(R):
                    groups(NG // R - 1, s, s == R - 1)

    def product(self, name, terms, vectors, finish, finish_steps, prepare=None, prepare_steps=0, bufs=(),
                stores=(), columns=1, value=None):
        nc = self.nc
        nk = len(terms)
        SL, LEAD = 4, 3
        with ExitStack() as c:
            def sb(nm, shape, dt):
                return c.enter_context(nc.sbuf_tensor(f"{name}_{nm}", shape, dt))

            def sem(nm):
                return self.sem(c, f"{name}_{nm}")

            xin = sb("xin", [P, 2, nk, F], FP32)
            xT = sb("xT", [P, 2, 2 * nk, P], FP32)
            weights, vecs, loads = [], [], []
            for k, (_, w) in enumerate(terms):
                if w.shape[0] == F:
                    weights.append(sb(f"w{k}", [P, 2, F], FP32))
                    loads.append((weights[k][:, :, :], w.rearrange("(c k) n -> k c n", k=P)))
                else:
                    weights.append(w)
            for k, v in enumerate(vectors):
                vecs.append(sb(f"v{k}", [P, v.shape[0]], FP32))
                loads.append((vecs[k][:, :], row_on_all(v)))
            if value:
                bufs = list(bufs) + [("parts", [3, F], BF16)]
            buf = {nm: sb(nm, [P, SL] + shape, dt) for nm, shape, dt in bufs}
            at_slot = [{nm: b[:, s] for nm, b in buf.items()} for s in range(SL)]
            pT = c.enter_context(nc.psum_tensor(f"{name}_pT", [P, 2, 4, P], FP32))
            pY = c.enter_context(nc.psum_tensor(f"{name}_pY", [P, 2, 512], FP32))
            loaded, fetched, turned, xT_ready = sem("loaded"), sem("fetched"), sem("turned"), sem("xT_ready")
            y_ready, rounded, act_turns = sem("y_ready"), sem("rounded"), sem("act_turns")
            prepared, finished, parted = sem("prepared"), sem("finished"), sem("parted")
            stored = [sem(f"stored{s}") for s in range(SL)]
            block = c.enter_context(nc.Block())

            def over_tiles(eng, body):
                for t in range(2 * SL):
                    body(t, t % SL, t // SL or None)
                with eng.Fori(2, NT // SL - 1) as i:
                    for s in range(SL):
                        body(i * SL + s, s, i)
                for t in range((NT // SL - 1) * SL, NT):
                    body(t, t % SL, t // SL)

            @block.sync
            def _(sp):
                for dst, src in loads:
                    sp.dma_start(dst, src).then_inc(loaded, 16)

                def body(t, s, used):
                    if value:
                        sp.wait_ge(parted, t * 3 + 3)
                    else:
                        sp.wait_ge(finished, t * finish_steps + finish_steps)
                    for rows, part in stores:
                        sp.dma_start(rows.rearrange("(b p) (c f) -> b p c f", p=P, c=columns)[bass.ds(t, 1), :, :, :]
                                     .rearrange("b p c f -> (b p) c f"), part(buf, s)).then_inc(stored[s], 16)
                if stores:
                    over_tiles(sp, body)
                    for s in range(SL):
                        sp.wait_ge(stored[s], 16 * len(stores) * ((NT + SL - 1 - s) // SL))

            @block.vector
            def _(dve):
                def prep(t):
                    step = Chain(dve, prepared, t * prepare_steps)
                    prepare(dve, step, t)
                    assert step.n == prepare_steps

                def body(t, s, used):
                    if prepare and not is_int(t, NT - LEAD):
                        prep(t + LEAD)
                    dve.wait_ge(y_ready, t + 1)
                    if stores and not value and used is not None:
                        dve.wait_ge(stored[s], used * (16 * len(stores)))
                    step = Chain(dve, finished, t * finish_steps)
                    finish(dve, step, t, pY[:, s % 2, 0:F], at_slot[s], vecs)
                    assert step.n == finish_steps
                    if value and (not isinstance(t, int) or t > 0):
                        split_rest(t - 1, (s - 1) % SL)

                def split_rest(t, s):
                    v, (p0, p1, p2) = value(t, at_slot[s]), (at_slot[s]["parts"][:, k, :] for k in range(3))
                    dve.wait_ge(rounded, t + 1)
                    rest = self.rest[:, s % 2, :]
                    dve.tensor_tensor(rest, v, p0, ALU.subtract).then_inc(parted, 1)
                    dve.tensor_tensor(p1, v, p0, ALU.subtract).then_inc(parted, 1)
                    dve.wait_ge(parted, t * 3 + 2)
                    dve.tensor_tensor(p2, rest, p1, ALU.subtract).then_inc(parted, 1)

                dve.wait_ge(loaded, 16 * len(loads))
                if prepare:
                    for t in range(LEAD):
                        prep(t)
                over_tiles(dve, body)
                if value:
                    split_rest(NT - 1, (NT - 1) % SL)

            @block.scalar
            def _(act):
                def fetch(t, s):
                    if prepare:
                        act.wait_ge(prepared, t * prepare_steps + prepare_steps)
                    for k, (a, _) in enumerate(terms):
                        act.activation(xin[:, s % 2, k, :], tile(a, t)[:, 0:F], ACT.Copy).then_inc(fetched, 1)

                fetch(0, 0)
                fetch(1, 1)

                def body(t, s, used):
                    act.wait_ge(turned, t + 1)
                    act.activation(xT[:, s % 2, :, :], pT[:, s % 2, 0:2 * nk, :], ACT.Copy).then_inc(xT_ready, 1)
                    if not is_int(t, NT - 2):
                        fetch(t + 2, s)
                    if value and (not isinstance(t, int) or t > 0):
                        round_off(t - 1, (s - 1) % SL, used if used is None or s else used - 1)

                def round_off(t, s, used):
                    act.wait_ge(finished, t * finish_steps + finish_steps)
                    if stores and used is not None and (is_int(used, 1) or not isinstance(used, int)):
                        act.wait_ge(stored[s], used * (16 * len(stores)))
                    act.sem_inc(act_turns, 1)
                    act.activation(at_slot[s]["parts"][:, 0, :], value(t, at_slot[s]), ACT.Copy).then_inc(rounded, 1)

                over_tiles(act, body)
                if value:
                    round_off(NT - 1, (NT - 1) % SL, (NT - 1) // SL)

            @block.tensor
            def _(pe):
                def turn(t, s):
                    pe.wait_ge(fetched, (t + 1) * nk)
                    for k in range(nk):
                        for h in range(2):
                            last = nc.tensor.transpose(pT[:, s % 2, 2 * k + h, :], xin[:, s % 2, k, h * P:(h + 1) * P],
                                                       self.ident[:, :])
                    last.then_inc(turned, 1)

                def body(t, s, used):
                    if not is_int(t, NT - 1):
                        turn(t + 1, s + 1)
                    pe.wait_ge(xT_ready, t + 1)
                    if not isinstance(t, int) or t >= 2:
                        pe.wait_ge(finished, (t - 1) * finish_steps)
                    for k in range(nk):
                        for h in range(2):
                            last = nc.tensor.matmul(pY[:, s % 2, 0:F], xT[:, s % 2, 2 * k + h, :], weights[k][:, h, :],
                                                    start=(k == 0 and h == 0), stop=(k == nk - 1 and h == 1))
                    last.then_inc(y_ready, 1)

                if loads:
                    pe.wait_ge(loaded, 16 * len(loads))
                turn(0, 0)
                over_tiles(pe, body)

    def statistics(self, name, stages, setup=None, vectors=()):
        nc = self.nc
        with ExitStack() as c:
            def sem(nm):
                return self.sem(c, f"{name}_{nm}")

            vecs = [c.enter_context(nc.sbuf_tensor(f"{name}_v{k}", [P, v.shape[0]], FP32)) for k, v in enumerate(vectors)]
            ssteps, tsteps, loaded = sem("ssteps"), sem("tsteps"), sem("loaded")
            block = c.enter_context(nc.Block())

            @block.sync
            def _(sp):
                for dst, v in zip(vecs, vectors):
                    sp.dma_start(dst[:, :], row_on_all(v)).then_inc(loaded, 16)

            @block.vector
            def _(dve):
                if vectors:
                    dve.wait_ge(loaded, 16 * len(vectors))
                step = Chain(dve, ssteps)
                if setup:
                    setup(dve, step)
                U = 7
                assert NT % U == 0
                n_steps = U * sum(n for _, n in stages)
                with dve.Fori(0, NT // U) as i:
                    step = Chain(dve, tsteps, i * n_steps)
                    for stage, _ in stages:
                        for k in range(U):
                            stage(dve, step, i * U + k, vecs)
                        step.wait()
                    assert step.n == n_steps
                    dve.sem_inc(self.dve_turns, 1)
                    for k in range(U):
                        self.moments(dve, i * U + k)
        self.inverse_deviation(name)

    def moments(self, dve, t):
        dve.bn_stats(self.halves[:, bass.ds(t, 1), :].rearrange("p t c -> p (t c)"), tile(self.x, t)).then_inc(self.measured, 1)

    def inverse_deviation(self, name):
        nc = self.nc
        with ExitStack() as c:
            added, rooted, inverted = (self.sem(c, f"{name}_{nm}") for nm in ("added", "rooted", "inverted"))
            apart = c.enter_context(nc.sbuf_tensor(f"{name}_apart", [P, NT], FP32))
            block = c.enter_context(nc.Block())
            mean, var = self.moment[:, :, 0], self.moment[:, :, 1]
            mean_e, m2_e, mean_o, m2_o = (self.halves[:, :, k] for k in (1, 2, 4, 5))
            self.n_measured += NT

            @block.vector
            def _(dve):
                dve.wait_ge(self.measured, self.n_measured)
                step = Chain(dve, added)
                step(dve.tensor_tensor(mean, mean_e, mean_o, ALU.add))
                step(dve.tensor_scalar(mean, mean, 0.5, None, ALU.mult))
                step(dve.tensor_tensor(apart[:, :], mean_e, mean_o, ALU.subtract))
                step(dve.tensor_tensor(apart[:, :], apart[:, :], apart[:, :], ALU.mult))
                step(dve.tensor_scalar(apart[:, :], apart[:, :], 0.25, EPS, ALU.mult, ALU.add))
                step(dve.tensor_tensor(var, m2_e, m2_o, ALU.add))
                step(dve.scalar_tensor_tensor(var, var, 1.0 / F, apart[:, :], ALU.mult, ALU.add))
                dve.wait_ge(rooted, 1)
                dve.reciprocal(var, var).then_inc(inverted, 1)
                dve.wait_ge(inverted, 1)

            @block.scalar
            def _(act):
                act.wait_ge(added, 7)
                act.activation(var, var, ACT.Sqrt).then_inc(rooted, 1)

    def normalize(self, dve, step, t):
        x = tile(self.x, t)
        step.issue(dve.tensor_scalar(x, x, self.moment[:, bass.ds(t, 1), 0], self.moment[:, bass.ds(t, 1), 1],
                                     ALU.subtract, ALU.mult))

    def load_nodes(self):
        nc = self.nc
        x, w_z, w_f, w_b = (self.ins[n] for n in ("x", "L0_gnn_W", "L2_gnn_W_f", "L2_gnn_W_b"))
        with ExitStack() as c:
            wr = c.enter_context(nc.sbuf_tensor("ln_w", [P, 4, F], FP32))
            pw = c.enter_context(nc.psum_tensor("ln_pw", [P, 4, 2, P], FP32))
            cleared, nodes_in, w_in, turned, kept = (self.sem(c, f"ln_{n}")
                                                     for n in ("cleared", "nodes_in", "w_in", "turned", "kept"))
            block = c.enter_context(nc.Block())

            @block.sync
            def _(sp):
                sp.dma_start(wr[:, 0:2, :], w_z.rearrange("(c m) k -> m c k", m=P)).then_inc(w_in, 16)
                sp.dma_start(wr[:, 2, :], w_f).then_inc(w_in, 16)
                sp.dma_start(wr[:, 3, :], w_b).then_inc(w_in, 16)
                sp.wait_ge(cleared, 1)
                sp.dma_start(self.x[:, 0:NT - 1, :], x[0:(NT - 1) * P, :].rearrange("(b p) f -> p b f", p=P)).then_inc(nodes_in, 16)
                sp.dma_start(self.x[0:LAST, NT - 1, :], x[(NT - 1) * P:N_NODES, :]).then_inc(nodes_in, 16)
                sp.wait_ge(nodes_in, 32)

            @block.vector
            def _(dve):
                dve.memset(self.x[:, NT - 1, :], 0.0).then_inc(cleared, 1)
                dve.wait_ge(turned, 1)
                for m in range(4):
                    dst = (self.w_z, self.w_fb)[m // 2]
                    dve.tensor_copy(dst[:, :, (m % 2) * P:(m % 2 + 1) * P], pw[:, m, :, :]).then_inc(kept, 1)
                dve.wait_ge(kept, 4)

            @block.tensor
            def _(pe):
                pe.wait_ge(w_in, 48)
                for m in range(4):
                    for h in range(2):
                        last = nc.tensor.transpose(pw[:, m, h, :], wr[:, m, h * P:(h + 1) * P], self.ident[:, :])
                last.then_inc(turned, 1)

    def degree_factors(self):
        nc = self.nc
        with ExitStack() as c:
            steps, rooted = (self.sem(c, f"df_{n}") for n in ("steps", "rooted"))
            safe = c.enter_context(nc.sbuf_tensor("df_safe", [P, NT], FP32))
            some = c.enter_context(nc.sbuf_tensor("df_some", [P, NT], FP32))
            block = c.enter_context(nc.Block())

            @block.vector
            def _(dve):
                step = Chain(dve, steps)
                step(dve.tensor_scalar(self.r_in[:, :], self.deg_src[:, :], 1.0, None, ALU.add))
                step(dve.tensor_scalar(self.r_out[:, :], self.deg_dst[:, :], 1.0, None, ALU.add))
                step(dve.tensor_scalar(safe[:, :], self.deg_dst[:, :], 1.0, None, ALU.max))
                step(dve.tensor_scalar(some[:, :], self.deg_dst[:, :], 0.0, None, ALU.is_gt))
                dve.wait_ge(rooted, 3)
                step(dve.reciprocal(self.r_in[:, :], self.r_in[:, :]))
                step(dve.reciprocal(self.r_out[:, :], self.r_out[:, :]))
                step(dve.reciprocal(safe[:, :], safe[:, :]))
                step(dve.tensor_tensor(self.r_dst[:, :], safe[:, :], some[:, :], ALU.mult))
                step(dve.tensor_scalar(safe[:, :], self.deg_src[:, :], 1.0, None, ALU.max))
                step(dve.reciprocal(self.mean_src[:, :], safe[:, :]))

            @block.scalar
            def _(act):
                act.wait_ge(steps, 4)
                for a in (self.r_in, self.r_out, safe):
                    act.activation(a[:, :], a[:, :], ACT.Sqrt).then_inc(rooted, 1)

    def finish_nodes(self):
        nc = self.nc
        CH = 7
        with ExitStack() as c:
            steps, stored = (self.sem(c, f"fn_{n}") for n in ("steps", "stored"))
            block = c.enter_context(nc.Block())

            @block.vector
            def _(dve):
                with dve.Fori(0, NT // CH) as i:
                    for k in range(CH):
                        self.normalize(dve, Chain(dve, steps), i * CH + k)

            @block.sync
            def _(sp):
                for b in range(0, NT - CH, CH):
                    sp.wait_ge(steps, b + CH)
                    sp.dma_start(self.out[b * P:(b + CH) * P, :].rearrange("(b p) f -> p b f", p=P),
                                 self.x[:, b:b + CH, :]).then_inc(stored, 16)
                b = NT - CH
                sp.wait_ge(steps, NT)
                sp.dma_start(self.out[b * P:(NT - 1) * P, :].rearrange("(b p) f -> p b f", p=P),
                             self.x[:, b:NT - 1, :]).then_inc(stored, 16)
                sp.dma_start(self.out[(NT - 1) * P:N_NODES, :], self.x[0:LAST, NT - 1, :]).then_inc(stored, 16)
                sp.wait_ge(stored, 16 * (NT // CH + 1))


def tile(a, t):
    return a[:, bass.ds(t, 1), :].rearrange("p b f -> p (b f)")


def build(nc, ins, out):
    with ExitStack() as ctx:
        k = Kernel(nc, ctx, ins, out)
        sb = k.sb
        k.x = sb("x", [P, NT, F], FP32)
        k.acc = acc = sb("acc", [P, NT, F + 1], FP32)
        k.moment = sb("moment", [P, NT, 2], FP32)
        k.halves = sb("halves", [P, NT, 6], FP32)
        k.measured = ctx.enter_context(nc.semaphore("measured"))
        k.n_measured = 0
        k.dve_turns = ctx.enter_context(nc.semaphore("dve_turns"))
        k.rest = sb("rest", [P, 2, F], FP32)
        k.tmp = sb("tmp", [P, F], FP32)
        k.dot = sb("dot", [P, 1], FP32)
        k.w_z = sb("w_z", [P, 2, F], FP32)
        k.w_fb = sb("w_fb", [P, 2, F], FP32)
        k.deg_src = sb("deg_src", [P, NT], FP32)
        k.deg_dst = sb("deg_dst", [P, NT], FP32)
        k.r_in = sb("r_in", [P, NT], FP32)
        k.r_out = sb("r_out", [P, NT], FP32)
        k.r_dst = sb("r_dst", [P, NT], FP32)
        k.mean_src = sb("mean_src", [P, NT], FP32)
        k.constants()
        k.load_nodes()

        with ExitStack() as c:
            def scoped(name, shape, dt):
                return c.enter_context(nc.sbuf_tensor(name, shape, dt))

            k.rec = scoped("rec_all", [P, NG, J, 2], I32)
            k.place = scoped("place", [P, S], I32)
            k.logit_e = scoped("logit_e", [P, NG, J], FP32)
            a_dst = scoped("a_dst", [P, NT], FP32)
            k.edges()
            k.ranges(0)

            def finish_z(dve, step, t, y, buf, vec):
                z = buf["row"][:, 0:F]
                step.issue(dve.memset(buf["row"][:, F:W0], 1.0))
                step(dve.tensor_copy(z, y))
                for a, dot in ((0, buf["row"][:, C_SRC:C_SRC + 1]), (1, k.dot[:, :])):
                    dve.sem_inc(k.dve_turns, 1)
                    step(dve.tensor_tensor_reduce(out=k.tmp[:, :], in0=z, in1=vec[a][:, :], scale=1.0, scalar=0.0,
                                                  op0=ALU.mult, op1=ALU.add, accum_out=dot))
                step(copy(dve, a_dst[:, bass.ds(t, 1)], k.dot[:, :]))

            k.product("z", [(k.x, k.w_z)], [ins["L0_gnn_A"][0, 0:F], ins["L0_gnn_A"][0, F:2 * F]], finish_z, 5,
                      bufs=[("row", [W0], FP32)], stores=[(k.tab_z, lambda b, s: b["row"][:, s:s + 1, :])])
            k.attention(acc, a_dst, k.deg_dst)
        k.ranges(1)

        def softmax_setup(dve, step):
            step(dve.tensor_scalar(acc[:, :, F], acc[:, :, F], 2.0 ** -100, None, ALU.max))
            step(dve.reciprocal(acc[:, :, F], acc[:, :, F]))

        def add_attention(dve, step, t, vec):
            x = tile(k.x, t)
            step.issue(dve.scalar_tensor_tensor(x, tile(acc, t)[:, 0:F], acc[:, bass.ds(t, 1), F], x, ALU.mult, ALU.add))

        k.statistics("s0", [(add_attention, 1)], softmax_setup)

        with ExitStack() as c:
            h = c.enter_context(nc.sbuf_tensor("h", [P, NG // 2, F], FP32))

            def row_of(b, s):
                return b["parts"][:, s, :, :]

            def value_h(t, buf):
                return tile(h, t)

            def finish_in(dve, step, t, y, buf, vec):
                step.issue(dve.tensor_tensor(tile(h, t), y, vec[0][:, :], ALU.add))

            k.product("in", [(k.x, ins["L1_gnn_W_in"])], [ins["L1_gnn_b_in"]], finish_in, 1,
                      prepare=k.normalize, prepare_steps=1, value=value_h, columns=3, stores=[(k.tab_h[0], row_of)])

            def finish_layer(dve, step, t, y, buf, vec):
                step(dve.scalar_tensor_tensor(k.tmp[:, :], y, k.mean_src[:, bass.ds(t, 1)], tile(h, t), ALU.mult, ALU.add))
                step(dve.tensor_scalar(tile(h, t), k.tmp[:, :], 0.0, None, ALU.max))

            for layer in range(3):
                k.aggregate(f"h{layer}", 1, k.tab_h[layer], F, acc, 0, True, count=k.deg_src if layer == 0 else None,
                            own=(h, ins["L1_gnn_W_self"][layer], ins["L1_gnn_b_hid"][layer]))
                if layer == 0:
                    k.degree_factors()
                more = layer < 2
                k.product(f"l{layer}", [(acc, ins["L1_gnn_W_agg"][layer])], [], finish_layer, 2,
                          value=value_h if more else None, columns=3,
                          stores=[(k.tab_h[layer + 1], row_of)] if more else [])

            def finish_out(dve, step, t, y, buf, vec):
                x = tile(k.x, t)
                step(dve.tensor_tensor(k.tmp[:, :], y, vec[0][:, :], ALU.add))
                step(dve.tensor_tensor(x, x, k.tmp[:, :], ALU.add))
                dve.sem_inc(k.dve_turns, 1)
                k.moments(dve, t)

            k.product("out", [(h, ins["L1_gnn_W_out"])], [ins["L1_gnn_b_out"]], finish_out, 2)
        k.inverse_deviation("out")

        def finish_fb(dve, step, t, y, buf, vec):
            for w, r in enumerate((k.r_out, k.r_in)):
                step.issue(dve.tensor_scalar(tile(acc, t)[:, w * H:(w + 1) * H], y[:, w * H:(w + 1) * H],
                                             r[:, bass.ds(t, 1)], None, ALU.mult))

        k.product("fb", [(k.x, k.w_fb)], [], finish_fb, 2, prepare=k.normalize, prepare_steps=1,
                  value=lambda t, buf: tile(acc, t)[:, 0:F], columns=3,
                  stores=[(k.tab_fb[w], lambda b, s, w=w: b["parts"][:, s, :, w * H:(w + 1) * H]) for w in range(2)])
        k.aggregate("f", 1, k.tab_fb[0], H, acc, 0, False)
        k.aggregate("b", 0, k.tab_fb[1], H, acc, H, False)

        def add_bias(dve, step, t, vec):
            step.issue(dve.tensor_tensor(tile(k.x, t), tile(k.x, t), vec[0][:, :], ALU.add))

        def add_fb(dve, step, t, vec):
            for w, r in enumerate((k.r_in, k.r_out)):
                cols = slice(w * H, (w + 1) * H)
                x = tile(k.x, t)[:, cols]
                step.issue(dve.scalar_tensor_tensor(x, tile(acc, t)[:, cols], r[:, bass.ds(t, 1)], x, ALU.mult, ALU.add))

        k.statistics("s2", [(add_bias, 1), (add_fb, 2)], vectors=[ins["L2_gnn_bias_param"]])

        def finish_g(dve, step, t, y, buf, vec):
            step.issue(dve.tensor_scalar(buf["scaled"], y, k.r_dst[:, bass.ds(t, 1)], None, ALU.mult))

        k.product("g", [(k.x, ins["L3_gnn_W"])], [], finish_g, 1, prepare=k.normalize, prepare_steps=1,
                  bufs=[("scaled", [F], FP32)], value=lambda t, buf: buf["scaled"], columns=3,
                  stores=[(k.tab_g, lambda b, s: b["parts"][:, s, :, :])])
        k.aggregate("gg", 0, k.tab_g, F, acc, 0, True)

        def add_g(dve, step, t, vec):
            x = tile(k.x, t)
            step.issue(dve.scalar_tensor_tensor(x, tile(acc, t)[:, 0:F], k.r_dst[:, bass.ds(t, 1)], x, ALU.mult, ALU.add))

        k.statistics("s3", [(add_g, 1)])
        k.finish_nodes()


_INS = ['x', 'src', 'dst', 'edge_attr_64', 'L0_gnn_W', 'L0_gnn_A', 'L1_gnn_W_in', 'L1_gnn_b_in', 'L1_gnn_W_agg',
        'L1_gnn_W_self', 'L1_gnn_b_hid', 'L1_gnn_W_out', 'L1_gnn_b_out', 'L2_gnn_W_f', 'L2_gnn_W_b',
        'L2_gnn_bias_param', 'L3_gnn_W']


def kernel(**inputs):
    import numpy as _np
    import concourse.bacc as _bacc
    from concourse import mybir as _mybir
    from concourse.bass_utils import run_bass_kernel_spmd as _run

    nc = _bacc.Bacc("TRN2", target_bir_lowering=False, num_devices=1)
    arrays, args = {}, {}
    for name in _INS:
        a = _np.ascontiguousarray(inputs[name])
        arrays[f"in_{name}_dram"] = a
        args[name] = nc.dram_tensor(f"in_{name}_dram", a.shape, _mybir.dt.from_np(a.dtype), kind="ExternalInput").ap()
    out = nc.dram_tensor("out_0_dram", (6250, 256), _mybir.dt.float32, kind="ExternalOutput").ap()
    build(nc, args, out)
    r = _run(nc, [arrays], core_ids=[0])
    return r.results[0]["out_0_dram"]
```
